# Optimizing a Trainium2 kernel written in Bass

```python
import numpy as np
import jax
import jax.numpy as jnp

def _softmax(x, axis=-1):
    return jax.nn.softmax(x, axis=axis)

def _gelu(x):
    return jax.nn.gelu(x, approximate=True)

def _silu(x):
    return jax.nn.silu(x)

def _sigmoid(x):
    return jax.nn.sigmoid(x)

def _layernorm(x, axis=-1, eps=1e-05):
    m = jnp.mean(x, axis=axis, keepdims=True)
    v = jnp.var(x, axis=axis, keepdims=True)
    return (x - m) / jnp.sqrt(v + eps)

def _scatter_add(tgt, idx, src, axis=0):
    return tgt.at[idx].add(src)

def _segment_sum(src, seg, n):
    return jax.ops.segment_sum(src, seg, n)
kernel_name = 'mk_seq_preln_d4_jaxref_r8_d91d40'

def setup_inputs(seed: int=0):
    np.random.seed(seed)
    _w = jnp.asarray

    def _L0_attn_setup():
        import jax, jax.numpy as jnp
        import numpy as np
        N_HEADS = 1
        LATENT_DIM = 128
        SCALE = 1.0 / float(np.sqrt(LATENT_DIM * N_HEADS))
        key = jax.random.key(seed)
        kx, kq, ko = jax.random.split(key, 3)
        B, S, D = (4, 512, 128)
        x = jax.random.normal(kx, (B, S, D), dtype=jnp.float32)
        w_qkv = jax.random.normal(kq, (3 * N_HEADS * (LATENT_DIM // N_HEADS), D), dtype=jnp.float32) * 0.02
        w_o = jax.random.normal(ko, (LATENT_DIM, N_HEADS * (LATENT_DIM // N_HEADS)), dtype=jnp.float32) * 0.02
        return {'x': x, 'w_qkv': w_qkv, 'w_o': w_o}
    _L0_attn_in = _L0_attn_setup()

    def _L0_ffn_setup():
        import jax, jax.numpy as jnp
        import numpy as np
        LATENT = 128
        LEAF_W = 64
        DEPTH = 4
        N_LEAVES = 2 ** DEPTH
        N_NODES = 2 ** DEPTH - 1
        B, S = (4, 256)

        def _fff_params(key, prefix):
            ks = jax.random.split(key, 4)
            d, h, l, n = (LATENT, LEAF_W, N_LEAVES, N_NODES)
            s_in = 1.0 / np.sqrt(d).astype(np.float32)
            s_h = 1.0 / np.sqrt(h).astype(np.float32)
            return {f'{prefix}_node_w': jax.random.normal(ks[0], (n, d), jnp.float32) * s_in, f'{prefix}_node_b': jax.random.normal(ks[1], (n,), jnp.float32) * s_in, f'{prefix}_w1': jax.random.normal(ks[2], (l, d, h), jnp.float32) * s_in, f'{prefix}_b1': jnp.zeros((l, h), jnp.float32), f'{prefix}_w2': jax.random.normal(ks[3], (l, h, d), jnp.float32) * s_h, f'{prefix}_b2': jnp.zeros((l, d), jnp.float32)}

        def _fff(x, node_w, node_b, w1, b1, w2, b2):
            Bx, Sx, D = x.shape
            xf = x.reshape(-1, D)
            N = xf.shape[0]
            cur = jnp.zeros((N,), jnp.int32)
            for _ in range(DEPTH):
                pw = node_w[cur]
                score = jnp.einsum('nd,nd->n', xf, pw) + node_b[cur]
                cur = 2 * cur + 1 + (score >= 0).astype(jnp.int32)
            leaf = cur - N_NODES
            sel = jax.nn.one_hot(leaf, N_LEAVES, dtype=xf.dtype)
            hidden_all = jax.nn.relu(jnp.einsum('nd,ldh->lnh', xf, w1) + b1[:, None, :])
            hidden = hidden_all * sel.T[:, :, None]
            out = jnp.einsum('lnh,lho->no', hidden, w2) + sel @ b2
            return out.reshape(Bx, Sx, D)
        key = jax.random.key(seed)
        kx, kq, kk, kv = jax.random.split(key, 4)
        inp = {'x': jax.random.normal(kx, (B, S, LATENT), jnp.float32)}
        inp.update(_fff_params(kq, 'q'))
        inp.update(_fff_params(kk, 'k'))
        inp.update(_fff_params(kv, 'v'))
        return inp
    _L0_ffn_in = _L0_ffn_setup()

    def _L1_attn_setup():
        import jax, jax.numpy as jnp
        import numpy as np
        HEADS = 16
        key = jax.random.key(seed)
        ks = jax.random.split(key, 6)
        b, n, c = (4, 256, 128)
        h = 128
        s = 0.02
        return {'x': jax.random.normal(ks[0], (b, n, c), jnp.float32), 'Wq': jax.random.normal(ks[1], (h, c), jnp.float32) * s, 'Wk': jax.random.normal(ks[2], (h, c), jnp.float32) * s, 'Wv': jax.random.normal(ks[3], (h, c), jnp.float32) * s, 'Wout': jax.random.normal(ks[4], (c, h), jnp.float32) * s, 'bout': jnp.zeros((c,), jnp.float32)}
    _L1_attn_in = _L1_attn_setup()

    def _L1_ffn_setup():
        import jax, jax.numpy as jnp
        import numpy as np
        B, S, D = (1, 256, 128)
        F = 176
        E = 16
        K = 2
        CAP_FACTOR = 1.25

        def _mlp(h, wg, wu, wd):
            return jax.nn.silu(h @ wg) * (h @ wu) @ wd
        key = jax.random.key(seed)
        ks = jax.random.split(key, 10)
        sd = 0.02
        return {'x': jax.random.normal(ks[0], (B, S, D), jnp.float32), 'router_w': jax.random.normal(ks[1], (D, E), jnp.float32) * sd, 'router_b': jnp.zeros((E,), jnp.float32), 'w_gate': jax.random.normal(ks[2], (E, D, F), jnp.float32) * sd, 'w_up': jax.random.normal(ks[3], (E, D, F), jnp.float32) * sd, 'w_down': jax.random.normal(ks[4], (E, F, D), jnp.float32) * sd, 'sw_gate': jax.random.normal(ks[5], (D, F), jnp.float32) * sd, 'sw_up': jax.random.normal(ks[6], (D, F), jnp.float32) * sd, 'sw_down': jax.random.normal(ks[7], (F, D), jnp.float32) * sd}
    _L1_ffn_in = _L1_ffn_setup()

    def _L2_attn_setup():
        import jax, jax.numpy as jnp
        import numpy as np
        D_MODEL, D_STATE, D_CONV = (128, 16, 4)
        B, T = (2, 256)

        def _ssm_forward(x, in_proj_w, conv_w, conv_b, x_proj_w, dt_proj_w, dt_proj_b, A_log, out_proj_w):
            Bb, Tt, Dd = x.shape
            N = A_log.shape[1]
            xz = jnp.einsum('btd,ed->bte', x, in_proj_w)
            x_in, z = (xz[..., :Dd], xz[..., Dd:])
            x_c = jnp.swapaxes(x_in, 1, 2)
            x_c = jax.lax.conv_general_dilated(x_c, conv_w, window_strides=(1,), padding=[(D_CONV - 1, 0)], feature_group_count=Dd, dimension_numbers=('NCH', 'OIH', 'NCH'))
            x_c = x_c + conv_b[None, :, None]
            x_conv = jax.nn.silu(jnp.swapaxes(x_c, 1, 2))
            ssm_params = jnp.einsum('btd,ed->bte', x_conv, x_proj_w)
            B_ssm = ssm_params[..., :N]
            C_ssm = ssm_params[..., N:2 * N]
            dt = jax.nn.softplus(ssm_params[..., -1:] * dt_proj_w[None, None, :, 0] + dt_proj_b)
            A = -jnp.exp(A_log)
            dA = jnp.exp(dt[..., None] * A[None, None])
            dBx = dt[..., None] * B_ssm[:, :, None, :] * x_conv[..., None]

            def step(h, inp):
                dA_t, dBx_t, C_t = inp
                h = dA_t * h + dBx_t
                y_t = jnp.einsum('bdn,bn->bd', h, C_t)
                return (h, y_t)
            h0 = jnp.zeros((Bb, Dd, N), dtype=x.dtype)
            _, ys = jax.lax.scan(step, h0, (jnp.swapaxes(dA, 0, 1), jnp.swapaxes(dBx, 0, 1), jnp.swapaxes(C_ssm, 0, 1)))
            y = jnp.swapaxes(ys, 0, 1)
            y = y * jax.nn.silu(z)
            return jnp.einsum('btd,ed->bte', y, out_proj_w)
        key = jax.random.key(seed)
        ks = jax.random.split(key, 8)
        x = jax.random.normal(ks[0], (B, T, D_MODEL), dtype=jnp.float32)
        in_proj_w = jax.random.normal(ks[1], (2 * D_MODEL, D_MODEL), dtype=jnp.float32) * 0.02
        conv_w = jax.random.normal(ks[2], (D_MODEL, 1, D_CONV), dtype=jnp.float32) * (1.0 / np.sqrt(D_CONV))
        conv_b = jnp.zeros((D_MODEL,), dtype=jnp.float32)
        x_proj_w = jax.random.normal(ks[3], (2 * D_STATE + 1, D_MODEL), dtype=jnp.float32) * (1.0 / np.sqrt(D_MODEL))
        dt_proj_w = jax.random.normal(ks[4], (D_MODEL, 1), dtype=jnp.float32)
        dt_proj_b = jax.random.normal(ks[5], (D_MODEL,), dtype=jnp.float32) * 0.1
        A_log = jnp.broadcast_to(jnp.log(jnp.arange(1, D_STATE + 1, dtype=jnp.float32))[None, :], (D_MODEL, D_STATE)).copy()
        out_proj_w = jax.random.normal(ks[6], (D_MODEL, D_MODEL), dtype=jnp.float32) * 0.02
        return {'x': x, 'in_proj_w': in_proj_w, 'conv_w': conv_w, 'conv_b': conv_b, 'x_proj_w': x_proj_w, 'dt_proj_w': dt_proj_w, 'dt_proj_b': dt_proj_b, 'A_log': A_log, 'out_proj_w': out_proj_w}
    _L2_attn_in = _L2_attn_setup()

    def _L2_ffn_setup():
        import jax, jax.numpy as jnp
        import numpy as np
        E = 8
        TOP_K = 2
        D = 128
        H = 2 * D
        key = jax.random.key(seed)
        k0, k1, k2, k3, k4 = jax.random.split(key, 5)
        scale = 0.02
        x = jax.random.normal(k0, (4, 256, D), dtype=jnp.float32)
        Wg = jax.random.normal(k1, (D, E), dtype=jnp.float32) * scale
        W1 = jax.random.normal(k2, (E, D, H), dtype=jnp.float32) * scale
        W2 = jax.random.normal(k3, (E, D, H), dtype=jnp.float32) * scale
        W3 = jax.random.normal(k4, (E, H, D), dtype=jnp.float32) * scale
        return {'x': x, 'Wg': Wg, 'W1': W1, 'W2': W2, 'W3': W3}
    _L2_ffn_in = _L2_ffn_setup()

    def _L3_attn_setup():
        import jax, jax.numpy as jnp
        import numpy as np
        B, S, D = (8, 1024, 128)
        MIN_RAD, MAX_RAD = (0.9, 0.999)

        def _a_param_init(key, d):
            unif = jax.random.uniform(key, (d,))
            a = 0.5 * jnp.log(unif * (MAX_RAD ** 2 - MIN_RAD ** 2) + MIN_RAD ** 2)
            return jnp.log(jnp.exp(-a) - 1.0)
        key = jax.random.key(seed)
        ks = jax.random.split(key, 6)
        s = 1.0 / np.sqrt(D)
        return {'x': jax.random.normal(ks[0], (B, S, D), jnp.float32), 'W_in': jax.random.normal(ks[1], (D, D), jnp.float32) * s, 'b_in': jnp.zeros((D,), jnp.float32), 'W_gx': jax.random.normal(ks[2], (D, D), jnp.float32) * s, 'b_gx': jnp.zeros((D,), jnp.float32), 'W_ga': jax.random.normal(ks[3], (D, D), jnp.float32) * s, 'b_ga': jnp.zeros((D,), jnp.float32), 'a_param': _a_param_init(ks[4], D), 'W_out': jax.random.normal(ks[5], (D, D), jnp.float32) * s, 'b_out': jnp.zeros((D,), jnp.float32)}
    _L3_attn_in = _L3_attn_setup()

    def _L3_ffn_setup():
        import jax, jax.numpy as jnp
        import numpy as np
        E = 8
        K = 2
        B, S, H = (4, 256, 128)
        key = jax.random.key(seed)
        k1, k2, k3 = jax.random.split(key, 3)
        hidden_states = jax.random.normal(k1, (B, S, H), dtype=jnp.float32)
        weight = jax.random.normal(k2, (E, H, H), dtype=jnp.float32) * 0.02
        bias = jnp.zeros((E, H), dtype=jnp.float32)
        router_weight = jax.random.normal(k3, (E, H), dtype=jnp.float32) * 0.01
        router_bias = jnp.zeros((E,), dtype=jnp.float32)
        return {'hidden_states': hidden_states, 'weight': weight, 'bias': bias, 'router_weight': router_weight, 'router_bias': router_bias}
    _L3_ffn_in = _L3_ffn_setup()
    _d = {'L0_attn_x': _L0_attn_in['x'], 'L0_attn_w_qkv': _L0_attn_in['w_qkv'], 'L0_attn_w_o': _L0_attn_in['w_o'], 'L0_ffn_q_node_w': _L0_ffn_in['q_node_w'], 'L0_ffn_q_node_b': _L0_ffn_in['q_node_b'], 'L0_ffn_q_w1': _L0_ffn_in['q_w1'], 'L0_ffn_q_b1': _L0_ffn_in['q_b1'], 'L0_ffn_q_w2': _L0_ffn_in['q_w2'], 'L0_ffn_q_b2': _L0_ffn_in['q_b2'], 'L0_ffn_k_node_w': _L0_ffn_in['k_node_w'], 'L0_ffn_k_node_b': _L0_ffn_in['k_node_b'], 'L0_ffn_k_w1': _L0_ffn_in['k_w1'], 'L0_ffn_k_b1': _L0_ffn_in['k_b1'], 'L0_ffn_k_w2': _L0_ffn_in['k_w2'], 'L0_ffn_k_b2': _L0_ffn_in['k_b2'], 'L0_ffn_v_node_w': _L0_ffn_in['v_node_w'], 'L0_ffn_v_node_b': _L0_ffn_in['v_node_b'], 'L0_ffn_v_w1': _L0_ffn_in['v_w1'], 'L0_ffn_v_b1': _L0_ffn_in['v_b1'], 'L0_ffn_v_w2': _L0_ffn_in['v_w2'], 'L0_ffn_v_b2': _L0_ffn_in['v_b2'], 'L1_attn_Wq': _L1_attn_in['Wq'], 'L1_attn_Wk': _L1_attn_in['Wk'], 'L1_attn_Wv': _L1_attn_in['Wv'], 'L1_attn_Wout': _L1_attn_in['Wout'], 'L1_attn_bout': _L1_attn_in['bout'], 'L1_ffn_router_w': _L1_ffn_in['router_w'], 'L1_ffn_router_b': _L1_ffn_in['router_b'], 'L1_ffn_w_gate': _L1_ffn_in['w_gate'], 'L1_ffn_w_up': _L1_ffn_in['w_up'], 'L1_ffn_w_down': _L1_ffn_in['w_down'], 'L1_ffn_sw_gate': _L1_ffn_in['sw_gate'], 'L1_ffn_sw_up': _L1_ffn_in['sw_up'], 'L1_ffn_sw_down': _L1_ffn_in['sw_down'], 'L2_attn_in_proj_w': _L2_attn_in['in_proj_w'], 'L2_attn_conv_w': _L2_attn_in['conv_w'], 'L2_attn_conv_b': _L2_attn_in['conv_b'], 'L2_attn_x_proj_w': _L2_attn_in['x_proj_w'], 'L2_attn_dt_proj_w': _L2_attn_in['dt_proj_w'], 'L2_attn_dt_proj_b': _L2_attn_in['dt_proj_b'], 'L2_attn_A_log': _L2_attn_in['A_log'], 'L2_attn_out_proj_w': _L2_attn_in['out_proj_w'], 'L2_ffn_Wg': _L2_ffn_in['Wg'], 'L2_ffn_W1': _L2_ffn_in['W1'], 'L2_ffn_W2': _L2_ffn_in['W2'], 'L2_ffn_W3': _L2_ffn_in['W3'], 'L3_attn_W_in': _L3_attn_in['W_in'], 'L3_attn_b_in': _L3_attn_in['b_in'], 'L3_attn_W_gx': _L3_attn_in['W_gx'], 'L3_attn_b_gx': _L3_attn_in['b_gx'], 'L3_attn_W_ga': _L3_attn_in['W_ga'], 'L3_attn_b_ga': _L3_attn_in['b_ga'], 'L3_attn_a_param': _L3_attn_in['a_param'], 'L3_attn_W_out': _L3_attn_in['W_out'], 'L3_attn_b_out': _L3_attn_in['b_out'], 'L3_ffn_weight': _L3_ffn_in['weight'], 'L3_ffn_bias': _L3_ffn_in['bias'], 'L3_ffn_router_weight': _L3_ffn_in['router_weight'], 'L3_ffn_router_bias': _L3_ffn_in['router_bias']}
    _x0 = _d['L0_attn_x']
    _d['L0_attn_x'] = jax.random.normal(jax.random.fold_in(jax.random.key(seed), 1), (4, 512, 128), dtype=_x0.dtype)
    del _x0
    return _d

def reference(L0_attn_x, L0_attn_w_qkv, L0_attn_w_o, L0_ffn_q_node_w, L0_ffn_q_node_b, L0_ffn_q_w1, L0_ffn_q_b1, L0_ffn_q_w2, L0_ffn_q_b2, L0_ffn_k_node_w, L0_ffn_k_node_b, L0_ffn_k_w1, L0_ffn_k_b1, L0_ffn_k_w2, L0_ffn_k_b2, L0_ffn_v_node_w, L0_ffn_v_node_b, L0_ffn_v_w1, L0_ffn_v_b1, L0_ffn_v_w2, L0_ffn_v_b2, L1_attn_Wq, L1_attn_Wk, L1_attn_Wv, L1_attn_Wout, L1_attn_bout, L1_ffn_router_w, L1_ffn_router_b, L1_ffn_w_gate, L1_ffn_w_up, L1_ffn_w_down, L1_ffn_sw_gate, L1_ffn_sw_up, L1_ffn_sw_down, L2_attn_in_proj_w, L2_attn_conv_w, L2_attn_conv_b, L2_attn_x_proj_w, L2_attn_dt_proj_w, L2_attn_dt_proj_b, L2_attn_A_log, L2_attn_out_proj_w, L2_ffn_Wg, L2_ffn_W1, L2_ffn_W2, L2_ffn_W3, L3_attn_W_in, L3_attn_b_in, L3_attn_W_gx, L3_attn_b_gx, L3_attn_W_ga, L3_attn_b_ga, L3_attn_a_param, L3_attn_W_out, L3_attn_b_out, L3_ffn_weight, L3_ffn_bias, L3_ffn_router_weight, L3_ffn_router_bias):

    def _L0_attn_ref(x, w_qkv, w_o):
        import jax, jax.numpy as jnp
        import numpy as np
        N_HEADS = 1
        LATENT_DIM = 128
        SCALE = 1.0 / float(np.sqrt(LATENT_DIM * N_HEADS))
        B, S, _ = x.shape
        qkv = jnp.einsum('bsd,fd->bsf', x, w_qkv)
        qkv = qkv.reshape(B, S, N_HEADS, 3 * LATENT_DIM).transpose(0, 2, 1, 3)
        q, k, v = jnp.split(qkv, 3, axis=-1)
        attn_logits = jnp.einsum('bhqd,bhkd->bhqk', q, k) * SCALE
        attention = jax.nn.softmax(attn_logits, axis=1)
        values = jnp.einsum('bhqk,bhkd->bhqd', attention, v)
        values = values.transpose(0, 2, 1, 3).reshape(B, S, N_HEADS * LATENT_DIM)
        return jnp.einsum('bsf,of->bso', values, w_o)

    def _L0_ffn_ref(x, q_node_w, q_node_b, q_w1, q_b1, q_w2, q_b2, k_node_w, k_node_b, k_w1, k_b1, k_w2, k_b2, v_node_w, v_node_b, v_w1, v_b1, v_w2, v_b2):
        import jax, jax.numpy as jnp
        import numpy as np
        LATENT = 128
        LEAF_W = 64
        DEPTH = 4
        N_LEAVES = 2 ** DEPTH
        N_NODES = 2 ** DEPTH - 1
        B, S = (4, 256)

        def _fff_params(key, prefix):
            ks = jax.random.split(key, 4)
            d, h, l, n = (LATENT, LEAF_W, N_LEAVES, N_NODES)
            s_in = 1.0 / np.sqrt(d).astype(np.float32)
            s_h = 1.0 / np.sqrt(h).astype(np.float32)
            return {f'{prefix}_node_w': jax.random.normal(ks[0], (n, d), jnp.float32) * s_in, f'{prefix}_node_b': jax.random.normal(ks[1], (n,), jnp.float32) * s_in, f'{prefix}_w1': jax.random.normal(ks[2], (l, d, h), jnp.float32) * s_in, f'{prefix}_b1': jnp.zeros((l, h), jnp.float32), f'{prefix}_w2': jax.random.normal(ks[3], (l, h, d), jnp.float32) * s_h, f'{prefix}_b2': jnp.zeros((l, d), jnp.float32)}

        def _fff(x, node_w, node_b, w1, b1, w2, b2):
            Bx, Sx, D = x.shape
            xf = x.reshape(-1, D)
            N = xf.shape[0]
            cur = jnp.zeros((N,), jnp.int32)
            for _ in range(DEPTH):
                pw = node_w[cur]
                score = jnp.einsum('nd,nd->n', xf, pw) + node_b[cur]
                cur = 2 * cur + 1 + (score >= 0).astype(jnp.int32)
            leaf = cur - N_NODES
            sel = jax.nn.one_hot(leaf, N_LEAVES, dtype=xf.dtype)
            hidden_all = jax.nn.relu(jnp.einsum('nd,ldh->lnh', xf, w1) + b1[:, None, :])
            hidden = hidden_all * sel.T[:, :, None]
            out = jnp.einsum('lnh,lho->no', hidden, w2) + sel @ b2
            return out.reshape(Bx, Sx, D)
        q = _fff(x, q_node_w, q_node_b, q_w1, q_b1, q_w2, q_b2)
        k = _fff(x, k_node_w, k_node_b, k_w1, k_b1, k_w2, k_b2)
        v = _fff(x, v_node_w, v_node_b, v_w1, v_b1, v_w2, v_b2)
        scale = 1.0 / np.sqrt(LATENT).astype(np.float32)
        attn = jax.nn.softmax(jnp.einsum('bqd,bkd->bqk', q, k) * scale, axis=-1)
        return jnp.einsum('bqk,bkd->bqd', attn, v)

    def _L1_attn_ref(x, Wq, Wk, Wv, Wout, bout):
        import jax, jax.numpy as jnp
        import numpy as np
        HEADS = 16
        b, n, c = x.shape
        m = HEADS
        d = Wq.shape[0] // m
        q = jnp.einsum('bnc,hc->bnh', x, Wq).reshape(b, n, m, d)
        k = jnp.einsum('bnc,hc->bnh', x, Wk).reshape(b, n, m, d)
        v = jnp.einsum('bnc,hc->bnh', x, Wv).reshape(b, n, m, d)
        scale = d ** (-0.25)
        weight = jnp.einsum('bimd,bjmd->bmij', q * scale, k * scale)
        weight = jax.nn.softmax(weight, axis=-1)
        a = jnp.einsum('bmij,bjmd->bimd', weight, v).reshape(b, n, m * d)
        return jnp.einsum('bnh,ch->bnc', a, Wout) + bout

    def _L1_ffn_ref(x, router_w, router_b, w_gate, w_up, w_down, sw_gate, sw_up, sw_down):
        import jax, jax.numpy as jnp
        import numpy as np
        B, S, D = (1, 256, 128)
        F = 176
        E = 16
        K = 2
        CAP_FACTOR = 1.25

        def _mlp(h, wg, wu, wd):
            return jax.nn.silu(h @ wg) * (h @ wu) @ wd
        b, s, d = x.shape
        N = b * s
        NK = N * K
        C = int(np.ceil(CAP_FACTOR * NK / E))
        x_tokens = x.reshape(N, d)
        logits = x_tokens @ router_w + router_b
        probs = jax.nn.softmax(logits, axis=-1)
        vals, idx = jax.lax.top_k(probs, K)
        vals = vals / (jnp.sum(vals, axis=-1, keepdims=True) + 1e-09)
        idx_flat = idx.reshape(NK)
        vals_flat = vals.reshape(NK)
        oh_e = jax.nn.one_hot(idx_flat, E, dtype=x.dtype)
        pos = (jnp.cumsum(oh_e, axis=0) * oh_e).sum(axis=1) - 1
        within = (pos < C).astype(x.dtype)
        pos_c = jnp.clip(pos, 0, C - 1).astype(jnp.int32)
        token_ids = jnp.arange(NK) // K
        x_pair = x_tokens[token_ids] * within[:, None]
        expert_inputs = jnp.zeros((E, C, d), x.dtype).at[idx_flat, pos_c].add(x_pair)
        expert_outputs = jax.vmap(_mlp)(expert_inputs, w_gate, w_up, w_down)
        gathered = expert_outputs[idx_flat, pos_c] * (vals_flat * within)[:, None]
        output_tokens = gathered.reshape(N, K, d).sum(axis=1)
        return x + _mlp(x, sw_gate, sw_up, sw_down) + output_tokens.reshape(b, s, d)

    def _L2_attn_ref(x, in_proj_w, conv_w, conv_b, x_proj_w, dt_proj_w, dt_proj_b, A_log, out_proj_w):
        import jax, jax.numpy as jnp
        import numpy as np
        D_MODEL, D_STATE, D_CONV = (128, 16, 4)
        B, T = (2, 256)

        def _ssm_forward(x, in_proj_w, conv_w, conv_b, x_proj_w, dt_proj_w, dt_proj_b, A_log, out_proj_w):
            Bb, Tt, Dd = x.shape
            N = A_log.shape[1]
            xz = jnp.einsum('btd,ed->bte', x, in_proj_w)
            x_in, z = (xz[..., :Dd], xz[..., Dd:])
            x_c = jnp.swapaxes(x_in, 1, 2)
            x_c = jax.lax.conv_general_dilated(x_c, conv_w, window_strides=(1,), padding=[(D_CONV - 1, 0)], feature_group_count=Dd, dimension_numbers=('NCH', 'OIH', 'NCH'))
            x_c = x_c + conv_b[None, :, None]
            x_conv = jax.nn.silu(jnp.swapaxes(x_c, 1, 2))
            ssm_params = jnp.einsum('btd,ed->bte', x_conv, x_proj_w)
            B_ssm = ssm_params[..., :N]
            C_ssm = ssm_params[..., N:2 * N]
            dt = jax.nn.softplus(ssm_params[..., -1:] * dt_proj_w[None, None, :, 0] + dt_proj_b)
            A = -jnp.exp(A_log)
            dA = jnp.exp(dt[..., None] * A[None, None])
            dBx = dt[..., None] * B_ssm[:, :, None, :] * x_conv[..., None]

            def step(h, inp):
                dA_t, dBx_t, C_t = inp
                h = dA_t * h + dBx_t
                y_t = jnp.einsum('bdn,bn->bd', h, C_t)
                return (h, y_t)
            h0 = jnp.zeros((Bb, Dd, N), dtype=x.dtype)
            _, ys = jax.lax.scan(step, h0, (jnp.swapaxes(dA, 0, 1), jnp.swapaxes(dBx, 0, 1), jnp.swapaxes(C_ssm, 0, 1)))
            y = jnp.swapaxes(ys, 0, 1)
            y = y * jax.nn.silu(z)
            return jnp.einsum('btd,ed->bte', y, out_proj_w)
        return _ssm_forward(x, in_proj_w, conv_w, conv_b, x_proj_w, dt_proj_w, dt_proj_b, A_log, out_proj_w)

    def _L2_ffn_ref(x, Wg, W1, W2, W3):
        import jax, jax.numpy as jnp
        import numpy as np
        E = 8
        TOP_K = 2
        D = 128
        H = 2 * D
        logits = jnp.einsum('bsd,de->bse', x, Wg)
        top_vals, top_idx = jax.lax.top_k(logits, TOP_K)
        probs = jax.nn.softmax(top_vals, axis=-1)
        onehot = jax.nn.one_hot(top_idx, E, dtype=x.dtype)
        weights = jnp.einsum('bsk,bske->bse', probs, onehot)
        out = jnp.zeros_like(x)
        for e in range(E):
            u = jnp.einsum('bsd,dh->bsh', x, W1[e])
            v = jnp.einsum('bsd,dh->bsh', x, W2[e])
            h = u * jax.nn.sigmoid(u) * v
            y = jnp.einsum('bsh,hd->bsd', h, W3[e])
            out = out + y * weights[..., e][..., None]
        return out

    def _L3_attn_ref(x, W_in, b_in, W_gx, b_gx, W_ga, b_ga, a_param, W_out, b_out):
        import jax, jax.numpy as jnp
        import numpy as np
        B, S, D = (8, 1024, 128)
        MIN_RAD, MAX_RAD = (0.9, 0.999)

        def _a_param_init(key, d):
            unif = jax.random.uniform(key, (d,))
            a = 0.5 * jnp.log(unif * (MAX_RAD ** 2 - MIN_RAD ** 2) + MIN_RAD ** 2)
            return jnp.log(jnp.exp(-a) - 1.0)
        x = x @ W_in + b_in
        gate_x = jax.nn.sigmoid(x @ W_gx + b_gx)
        gate_a = jax.nn.sigmoid(x @ W_ga + b_ga)
        log_a = -8.0 * gate_a * jax.nn.softplus(a_param)
        a = jnp.exp(log_a)
        scale = jnp.sqrt(1.0 - jnp.exp(2.0 * log_a))
        xg = gate_x * x

        def step(h, inp):
            xt, at, st = inp
            h = at * h + st * xt
            return (h, h)
        init = jnp.zeros((x.shape[0], x.shape[2]), x.dtype)
        xs = (jnp.swapaxes(xg, 0, 1), jnp.swapaxes(a, 0, 1), jnp.swapaxes(scale, 0, 1))
        _, h = jax.lax.scan(step, init, xs, reverse=False)
        h = jnp.swapaxes(h, 0, 1)
        return h @ W_out + b_out

    def _L3_ffn_ref(hidden_states, weight, bias, router_weight, router_bias):
        import jax, jax.numpy as jnp
        import numpy as np
        E = 8
        K = 2
        B, S, H = (4, 256, 128)
        b, s, h = hidden_states.shape
        flat = hidden_states.reshape(b * s, h)
        logits = flat @ router_weight.T + router_bias
        scores = jax.nn.softmax(logits, axis=-1)
        _, topk_idx = jax.lax.top_k(scores, K)
        y = jnp.einsum('th,ehk->tek', flat, weight) + bias[None]
        sel = jnp.take_along_axis(y, topk_idx[:, :, None], axis=1)
        out = sel.sum(axis=1).reshape(b, s, h)
        return out
    x = L0_attn_x
    x = x + _L0_attn_ref(_layernorm(x, axis=-1), L0_attn_w_qkv, L0_attn_w_o)
    x = x + _L0_ffn_ref(_layernorm(x, axis=-1), L0_ffn_q_node_w, L0_ffn_q_node_b, L0_ffn_q_w1, L0_ffn_q_b1, L0_ffn_q_w2, L0_ffn_q_b2, L0_ffn_k_node_w, L0_ffn_k_node_b, L0_ffn_k_w1, L0_ffn_k_b1, L0_ffn_k_w2, L0_ffn_k_b2, L0_ffn_v_node_w, L0_ffn_v_node_b, L0_ffn_v_w1, L0_ffn_v_b1, L0_ffn_v_w2, L0_ffn_v_b2)
    x = x + _L1_attn_ref(_layernorm(x, axis=-1), L1_attn_Wq, L1_attn_Wk, L1_attn_Wv, L1_attn_Wout, L1_attn_bout)
    x = x + _L1_ffn_ref(_layernorm(x, axis=-1), L1_ffn_router_w, L1_ffn_router_b, L1_ffn_w_gate, L1_ffn_w_up, L1_ffn_w_down, L1_ffn_sw_gate, L1_ffn_sw_up, L1_ffn_sw_down)
    x = x + _L2_attn_ref(_layernorm(x, axis=-1), L2_attn_in_proj_w, L2_attn_conv_w, L2_attn_conv_b, L2_attn_x_proj_w, L2_attn_dt_proj_w, L2_attn_dt_proj_b, L2_attn_A_log, L2_attn_out_proj_w)
    x = x + _L2_ffn_ref(_layernorm(x, axis=-1), L2_ffn_Wg, L2_ffn_W1, L2_ffn_W2, L2_ffn_W3)
    x = x + _L3_attn_ref(_layernorm(x, axis=-1), L3_attn_W_in, L3_attn_b_in, L3_attn_W_gx, L3_attn_b_gx, L3_attn_W_ga, L3_attn_b_ga, L3_attn_a_param, L3_attn_W_out, L3_attn_b_out)
    x = x + _L3_ffn_ref(_layernorm(x, axis=-1), L3_ffn_weight, L3_ffn_bias, L3_ffn_router_weight, L3_ffn_router_bias)
    return x

_drawn_inputs = setup_inputs


def setup_inputs(seed=0):
    import zlib

    import numpy as np

    out = dict(_drawn_inputs(seed))
    spreads = {'L0_ffn_q_b1': (0.0, 0.1),
     'L0_ffn_q_b2': (0.0, 0.1),
     'L0_ffn_k_b1': (0.0, 0.1),
     'L0_ffn_k_b2': (0.0, 0.1),
     'L0_ffn_v_b1': (0.0, 0.1),
     'L0_ffn_v_b2': (0.0, 0.1),
     'L1_attn_bout': (0.0, 0.1),
     'L1_ffn_router_b': (0.0, 0.1),
     'L2_attn_conv_b': (0.0, 0.1),
     'L3_attn_b_in': (0.0, 0.1),
     'L3_attn_b_gx': (0.0, 0.1),
     'L3_attn_b_ga': (0.0, 0.1),
     'L3_attn_b_out': (0.0, 0.1),
     'L3_ffn_bias': (0.0, 0.1),
     'L3_ffn_router_bias': (0.0, 0.1)}
    factors = {}
    for name, (base, spread) in spreads.items():
        noise = np.random.default_rng([zlib.crc32(name.encode()), seed]).standard_normal(out[name].shape)
        drawn = base * np.exp(spread * noise) if base else spread * noise
        out[name] = jnp.asarray(drawn.astype(out[name].dtype))
    for name, factor in factors.items():
        out[name] = (out[name] * factor).astype(out[name].dtype)
    return out
```

```python
from contextlib import ExitStack

import numpy as np
import concourse.bass as bass
from concourse import mybir

F32 = mybir.dt.float32
BF16 = mybir.dt.bfloat16
U32 = mybir.dt.uint32
ALU = mybir.AluOpType
ACT = mybir.ActivationFunctionType
AX = mybir.AxisListType

P = 128
D = 128
NB, S = 4, 512
TT = S // P
NTOK = NB * S
EPS = 1e-5

DEPTH, LEAF_W = 4, 64
LEAVES, NODES = 2 ** DEPTH, 2 ** DEPTH - 1
HCH = LEAVES * LEAF_W // P
OFF_PATH = 2.0 ** 60
SCALE0 = float(np.float32(1.0) / np.sqrt(D).astype(np.float32))
HEADS, DH = 16, 8
SCALE1 = float(DH ** (-0.25))
GROUPS = HEADS // 4
PARTS = 3
MROW = PARTS * PARTS * DH
KSTACK = 96
E1, F1, K1 = 16, 176, 2
F1R = F1 - P
CAP = int(np.ceil(1.25 * NTOK * K1 / E1))
NSTATE, DCONV = 16, 4
E2, H2 = 8, 256
E3 = 8

TREES = ("q", "k", "v")


def shape_constants():
    bf = mybir.dt.np(BF16)
    eye = np.eye(P, dtype=np.float32)
    center = (eye - np.float32(1.0 / D)).astype(np.float32)
    mean = np.full((P, P), 1.0 / D, np.float32)
    ones = np.ones((P, P), np.float32)
    path = np.zeros((P, 3, LEAVES), np.float32)
    for leaf in range(LEAVES):
        node = 0
        for step in range(DEPTH):
            bit = leaf >> (DEPTH - 1 - step) & 1
            for f in range(3):
                path[32 * f + node, f, leaf] = 1.0 if bit else -1.0
                if not bit:
                    path[32 * f + NODES, f, leaf] += 1.0
            node = 2 * node + 1 + bit
        path[[32 * f + NODES for f in range(3)], range(3), leaf] -= DEPTH
    leafpath = np.zeros((P, P), np.float32)
    for f in range(3):
        leafpath[:, 32 * f:32 * f + LEAVES] = path[:, f]
    offpath = np.zeros((P, 3, HCH, P), np.float32)
    for c in range(HCH):
        for row in range(P):
            offpath[:, :, c, row] = path[:, :, 2 * c + row // LEAF_W] * OFF_PATH
    pick = np.zeros((KSTACK, 32, P), np.float32)
    for n in range(32):
        pick[[n, 32 + n, 64 + n], n] = 1.0
    rowsum = np.zeros((P, P), np.float32)
    for j in range(4):
        rowsum[32 * j + DH, 32 * j:32 * j + 32] = 1.0
    before = np.triu(np.ones((P, P), np.float32), 1)
    iota = np.broadcast_to(np.arange(16, dtype=np.float32), (P, 16)).copy()
    return {
        "c_eye": eye, "c_center": center, "c_mean": mean, "c_ones": ones, "c_leafpath": leafpath.astype(bf),
        "c_offpath": offpath.astype(bf), "c_pick": pick.astype(bf), "c_rowsum": rowsum,
        "c_before": before, "c_iota": iota,
    }


def build(nc, a, out):
    with ExitStack() as ctx:
        held = {}
        ctx.enter_context(nc.allow_non_contiguous_dma(reason="a bias goes one element to a partition"))

        def sb(name, shape, dt=F32):
            return ctx.enter_context(nc.sbuf_tensor("sb_" + name, shape, dt))

        def sem(name):
            if name not in held:
                held[name] = ctx.enter_context(nc.semaphore(name))
            return held[name]

        psum = ctx.enter_context(nc.psum_tensor("psum", [P, 8, S], F32))
        x = sb("x", [P, NB, S])
        h = sb("h", [P, NB, S])
        eye, center, mean, ones = (sb(n, [P, P]) for n in ("eye", "center", "mean", "ones"))
        rowsum, before, iota = sb("rowsum", [P, P]), sb("before", [P, P]), sb("iota", [P, 16])
        leafpath = sb("leafpath", [P, P], BF16)
        offpath = sb("offpath", [P, 3, HCH, P], BF16)
        pick = sb("pick", [KSTACK, 32, P], BF16)
        eps = sb("eps", [P, 1])
        one = sb("one", [P, 1])

        WV0, WO0, WQ1, WK1, WV1, WO1, WX2, WZ2, WOUT2, WSSM, WROUT3, WNODE = range(12)
        wT = sb("wT", [P, 12, D])
        nodeT = wT[:, WNODE, :]

        WIDE = sb("wide", [P, 6 * LEAVES * LEAF_W])
        w1 = [WIDE[:, f * 1024:(f + 1) * 1024] for f in range(3)]
        w2 = [WIDE[:, (3 + f) * 1024:(4 + f) * 1024].rearrange("p (c o) -> p c o", c=HCH) for f in range(3)]
        w1_2 = WIDE[:, 0:2048].rearrange("p (e n) -> p e n", e=E2)
        w2_2 = WIDE[:, 2048:4096].rearrange("p (e n) -> p e n", e=E2)
        w3_2 = WIDE[:, 4096:6144].rearrange("p (e k n) -> p e k n", e=E2, k=2)
        b1 = sb("b1", [P, 3, HCH])
        b2 = sb("b2", [P, 3, D])
        node_b = sb("node_b", [P, 1])

        woT = sb("woT", [P, GROUPS, D])
        bout1 = sb("bout1", [P, 1])
        router1, router1_b = sb("router1", [P, E1]), sb("router1_b", [P, 1])
        NE1 = E1 + 1
        gate0, up0 = sb("gate0", [P, NE1, P]), sb("up0", [P, NE1, P])
        rest = sb("rest", [P, NE1, P])
        down0 = sb("down0", [P, NE1, D])
        down1 = sb("down1", [P, (NE1 + 1) // 2, D])
        v32 = sb("v32", [P, TT, HEADS, 32])
        qstack = sb("qstack", [P, HEADS, S], BF16)
        kstack = sb("kstack", [P, HEADS, S], BF16)

        conv_w, conv_b = sb("conv_w", [P, DCONV]), sb("conv_b", [P, 1])
        dt_w, dt_b = sb("dt_w", [P, 1]), sb("dt_b", [P, 1])
        a_neg = sb("a_neg", [P, NSTATE])
        dt_rep = sb("dt_rep", [P, P])
        wg2 = sb("wg2", [P, E2])

        W_IN, W_GX, W_GA, W_OUT = range(4)
        w_3 = sb("w_3", [P, 4, D])
        b_3 = sb("b_3", [P, 4])
        a_par = sb("a_par", [P, 4])
        w_e3 = sb("w_e3", [P, E3, D])
        bias3 = sb("bias3", [P, D])
        router3_b = sb("router3_b", [P, 1])

        prob = sb("prob", [P, TT, 16])
        top = sb("top", [P, TT, 8])
        top_at = sb("top_at", [P, TT, 8], U32)
        top_f = sb("top_f", [P, TT, 8])
        chosen = sb("chosen", [P, TT, 16])
        weight = sb("weight", [P, TT, 16])
        earlier = sb("earlier", [P, TT + 1, 16])
        small = sb("small", [P, 8, TT])
        wparts = sb("wparts", [KSTACK, S], BF16)

        SCR = 12800
        scr = sb("scr", [P, SCR])

        def view(at, n, dt=F32):
            return scr[:, at:at + n] if dt is F32 else scr[:, at:at + n].bitcast(dt)

        squares = view(0, NB * S).rearrange("p (b s) -> p b s", b=NB)
        std = view(NB * S, NB * S).rearrange("p (b s) -> p b s", b=NB)
        wraw = view(4096, 12 * D).rearrange("p (n d) -> p n d", n=12)

        rows = view(8192, NB * TT * D).rearrange("p (t d) -> p t d", d=D)
        part_r, lt = view(10244, S)[0:32], view(10756, S)
        part_b = view(11268, S // 2, BF16)[0:32]
        hidden = view(0, HCH * S).rearrange("p (c s) -> p c s", c=HCH)
        qT0, kT0, v0 = view(4096, S), view(4608, S), view(5120, S)
        probs0 = view(5632, 2 * S).rearrange("p (r s) -> p r s", r=2)
        probsT0 = view(6656, TT * S).rearrange("p (k s) -> p k s", k=TT)
        gates = view(8704, S // 2, BF16)
        leaf = view(8960, S)
        token_sum, value_sum, attn0 = view(0, NB), view(4, NB), view(8, NB)

        expT = view(0, 8192).rearrange("p (r j k s) -> p r j k s", r=2, j=4, k=2)
        qrem, krem = view(8192, S), view(8704, S)
        qparts = view(9216, 768, BF16).rearrange("p (i s) -> p i s", i=PARTS)
        kparts = view(9984, 768, BF16).rearrange("p (i s) -> p i s", i=PARTS)
        vT1 = view(10752, S)
        mrem = view(10752, S)
        headmax = view(11264, TT * HEADS).rearrange("p (t h) -> p t h", t=TT)
        mparts = view(11328, 768, BF16).rearrange("p (i s) -> p i s", i=PARTS)
        head_raw, head_inv = qrem, krem
        head_out = vT1

        gact0 = view(0, 2 * S).rearrange("p (r s) -> p r s", r=2)
        gact1 = view(1024, 2 * S).rearrange("p (r s) -> p r s", r=2)
        prod0 = view(2048, 2 * S).rearrange("p (r s) -> p r s", r=2)
        prod1 = view(3072, 2 * S).rearrange("p (r s) -> p r s", r=2)
        hid0 = view(4096, 2 * S).rearrange("p (r s) -> p r s", r=2)
        hid1 = view(5120, 2 * S).rearrange("p (r s) -> p r s", r=2)

        xpad = view(0, S + DCONV)
        conv = view(516, S)
        xconv = view(1028, S)
        zgate = view(1540, S)
        dtv, dtl, dt = view(2052, S), view(2564, S), view(3076, S)
        dtx = view(3588, S)
        bcast_b = view(4612, 2 * S).rearrange("p (r s) -> p r s", r=2)
        decay = view(5636, 2 * S).rearrange("p (r s) -> p r s", r=2)
        drive = view(6660, 2 * S).rearrange("p (r s) -> p r s", r=2)
        state = view(7684, 2 * S).rearrange("p (r s) -> p r s", r=2)
        read = view(8708, 2 * S).rearrange("p (r s) -> p r s", r=2)
        ygate = view(9732, S)

        xw, gx, ga, dec, drv, st3 = (view(n * S, S) for n in range(6))
        sel3 = view(0, S)
        picked = view(512, 2 * S).rearrange("p (r s) -> p r s", r=2)

        q_bounce = nc.dram_tensor("q_bounce", [PARTS, P, S], BF16, kind="Internal").ap()
        k_bounce = nc.dram_tensor("k_bounce", [PARTS, P, S], BF16, kind="Internal").ap()

        x_ready, ln_done = sem("x_ready"), sem("ln_done")
        ATTN0, FFN0, ATTN1, FFN1, ATTN2, FFN2, ATTN3, FFN3 = range(8)

        def x_before(stage):
            return NB * (stage + 1)

        def turn(k, b):
            return b + NB * (k - 1)

        block = ctx.enter_context(nc.Block())

        @block.sync
        def _(sp):
            sp.dma_start(eye[:], a["c_eye"]).then_inc(sem("eye_loaded"), 16)
            xr = a["L0_attn_x"].rearrange("b (t p) d -> p (b t) d", p=P)
            sp.dma_start(rows, xr).then_inc(sem("rows_loaded"), 16)
            for t, n in ((center, "c_center"), (mean, "c_mean"), (ones, "c_ones")):
                sp.dma_start(t[:], a[n]).then_inc(sem("ln_consts"), 16)
            sp.wait_ge(sem("cleared"), 3)
            square = {WV0: a["L0_attn_w_qkv"][2 * D:3 * D, :], WO0: a["L0_attn_w_o"], WQ1: a["L1_attn_Wq"], WK1: a["L1_attn_Wk"],
                      WV1: a["L1_attn_Wv"], WO1: a["L1_attn_Wout"], WX2: a["L2_attn_in_proj_w"][0:D, :],
                      WZ2: a["L2_attn_in_proj_w"][D:2 * D, :], WOUT2: a["L2_attn_out_proj_w"], WSSM: a["L2_attn_x_proj_w"],
                      WROUT3: a["L3_ffn_router_weight"]}
            for n, src in square.items():
                sp.dma_start(wraw[0:src.shape[0], n, :], src).then_inc(sem("wraw_loaded"), 16)
            for f, name in enumerate(TREES):
                sp.dma_start(wraw[32 * f:32 * f + NODES, WNODE, :], a[f"L0_ffn_{name}_node_w"]).then_inc(sem("wraw_loaded"), 16)

            def column(name):
                return a[name].rearrange("(n o) -> n o", o=1)

            def load(group, dst, src):
                sp.dma_start(dst, src).then_inc(sem(group), 16)

            load("trees_loaded", leafpath[:], a["c_leafpath"])
            load("trees_loaded", offpath[:], a["c_offpath"])
            for f, name in enumerate(TREES):
                load("trees_loaded", node_b[32 * f:32 * f + NODES, :], column(f"L0_ffn_{name}_node_b"))
                load("trees_loaded", b2[32 * f:32 * f + LEAVES, f, :], a[f"L0_ffn_{name}_b2"])
                load("trees_loaded", b1[:, f, :], a[f"L0_ffn_{name}_b1"].rearrange("(c t) h -> (t h) c", t=2))
                load("trees_loaded", w1[f].rearrange("p (l h) -> p l h", h=LEAF_W), a[f"L0_ffn_{name}_w1"].rearrange("l d h -> d l h"))
                load("trees_loaded", w2[f], a[f"L0_ffn_{name}_w2"].rearrange("(c t) h o -> (t h) c o", t=2))
            load("attn1_loaded", rowsum[:], a["c_rowsum"])
            sp.wait_ge(sem("cleared"), N_CLEARED)
            load("attn1_loaded", bout1[:], column("L1_attn_bout"))
            load("ffn1_loaded", before[:], a["c_before"])
            load("ffn1_loaded", iota[:], a["c_iota"])
            load("ffn1_loaded", pick[:], a["c_pick"])
            load("ffn1_loaded", router1[:], a["L1_ffn_router_w"])
            load("ffn1_loaded", router1_b[0:E1, :], column("L1_ffn_router_b"))
            for dst, n, at in ((gate0, "gate", 0), (up0, "up", 0)):
                load("ffn1_loaded", dst[:, 0:E1, :], a[f"L1_ffn_w_{n}"].rearrange("e d f -> d e f")[:, :, 0:P])
                load("ffn1_loaded", dst[:, E1, :], a[f"L1_ffn_sw_{n}"][:, 0:P])
            for n, at in (("gate", 0), ("up", 64)):
                w = a[f"L1_ffn_w_{n}"].rearrange("(e t) d f -> d e t f", t=2)[:, :, :, P:F1]
                r = rest[:, 0:E1, :].rearrange("p (e t) f -> p e t f", t=2)
                load("ffn1_loaded", r[:, :, 0, at:at + F1R], w[:, :, 0, :])
                load("ffn1_loaded", r[:, :, 1, 64 - at:64 - at + F1R], w[:, :, 1, :])
                load("ffn1_loaded", rest[:, E1, at:at + F1R], a[f"L1_ffn_sw_{n}"][:, P:F1])
            load("ffn1_loaded", down0[:, 0:E1, :], a["L1_ffn_w_down"].rearrange("e f d -> f e d")[0:P])
            load("ffn1_loaded", down0[:, E1, :], a["L1_ffn_sw_down"][0:P])
            for t in range(2):
                load("ffn1_loaded", down1[64 * t:64 * t + F1R, 0:E1 // 2, :],
                     a["L1_ffn_w_down"].rearrange("(e t) f d -> t f e d", t=2)[t, P:F1])
            load("ffn1_loaded", down1[0:F1R, E1 // 2, :], a["L1_ffn_sw_down"][P:F1])
            load("attn2_loaded", conv_w[:], a["L2_attn_conv_w"].rearrange("d o k -> d (o k)"))
            load("attn2_loaded", conv_b[:], column("L2_attn_conv_b"))
            load("attn2_loaded", dt_w[:], a["L2_attn_dt_proj_w"])
            load("attn2_loaded", dt_b[:], column("L2_attn_dt_proj_b"))
            load("attn2_loaded", a_neg[:], a["L2_attn_A_log"])
            for n, name in enumerate(("in", "gx", "ga", "out")):
                load("attn3_loaded", w_3[:, n, :], a[f"L3_attn_W_{name}"])
                load("attn3_loaded", b_3[:, n:n + 1], column(f"L3_attn_b_{name}"))
            load("attn3_loaded", a_par[:, 0:1], column("L3_attn_a_param"))
            load("ffn3_loaded", w_e3[:], a["L3_ffn_weight"].rearrange("e d n -> d e n"))
            load("ffn3_loaded", bias3[0:E3, :], a["L3_ffn_bias"])
            load("ffn3_loaded", router3_b[0:E3, :], column("L3_ffn_router_bias"))
            sp.wait_ge(sem("wT_ready"), 3)
            for g in range(GROUPS):
                for j in range(4):
                    head = 4 * g + j
                    load("woT_ready", woT[32 * j:32 * j + DH, g, :], wT[head * DH:(head + 1) * DH, WO1, :])

            with sp.Fori(0, NB) as b:
                sp.wait_ge(sem("qparts_ready"), b + 1)
                sp.wait_ge(sem("kparts_ready"), b + 1)
                sp.dma_start(q_bounce.rearrange("i p s -> p i s"), qparts).then_inc(sem("bounced"), 16)
                sp.dma_start(k_bounce.rearrange("i p s -> p i s"), kparts).then_inc(sem("bounced"), 16)
                sp.wait_ge(sem("bounced"), b * 32 + 32)
                for i in range(PARTS):
                    for j in range(PARTS):
                        r = DH * (PARTS * i + j)
                        sp.dma_start(qstack[r:r + DH, :, :], q_bounce[i].rearrange("(h d) s -> d h s", d=DH)).then_inc(sem("stacked"), 16)
                        sp.dma_start(kstack[r:r + DH, :, :], k_bounce[j].rearrange("(h d) s -> d h s", d=DH)).then_inc(sem("stacked"), 16)
                sp.wait_ge(sem("mparts_ready"), b + 1)
                for i in range(PARTS):
                    sp.dma_start(qstack[96 + i:97 + i, :, :], mparts[0:HEADS, i, :]).then_inc(sem("max_stacked"), 16)

            sp.wait_ge(x_ready, x_before(ATTN1))
            load("ffn2_loaded", w1_2, a["L2_ffn_W1"].rearrange("e d n -> d e n"))
            load("ffn2_loaded", w2_2, a["L2_ffn_W2"].rearrange("e d n -> d e n"))
            load("ffn2_loaded", w3_2, a["L2_ffn_W3"].rearrange("e (k p) n -> p e k n", p=P))
            load("ffn2_loaded", wg2[:], a["L2_ffn_Wg"])

            orr = out.rearrange("(t p) d -> p t d", p=P)
            for b in range(NB):
                sp.wait_ge(sem("out_rows"), b + 1)
                sp.dma_start(orr[:, b * TT:(b + 1) * TT, :], rows[:, b * TT:(b + 1) * TT, :]).then_inc(sem("stored"), 16)
            sp.wait_ge(sem("stored"), 16 * NB)

        @block.gpsimd
        def _(pool):
            clears = [(wraw, 0.0), (b2[:], 0.0), (node_b[:], 0.0), (eps[:], EPS), (one[:], 1.0), (woT[:], 0.0),
                      (rest[:], 0.0), (down1[:], 0.0), (v32[:], 0.0), (qstack[64:P, :, :], 0.0), (kstack[64:96, :, :], 0.0),
                      (kstack[96:P, :, :], 1.0), (wparts[:], 0.0), (earlier[:, 0, :], 0.0), (bias3[:], 0.0), (router1_b[:], 0.0),
                      (router3_b[:], 0.0)]
            assert len(clears) == N_CLEARED - 1
            for n, (t, value) in enumerate(clears):
                if n >= 1:
                    pool.wait_ge(sem("cleared"), n)
                pool.memset(t, value).then_inc(sem("cleared"), 1)
            pool.wait_ge(sem("cleared"), N_CLEARED - 1)
            pool.memset(v32[:, :, :, DH], 1.0).then_inc(sem("cleared"), 1)

            with pool.Fori(0, NB) as b:
                for n in range(NSTATE):
                    r = n % 2
                    pool.wait_ge(sem("b_spread"), b * NSTATE + n + 1)
                    if n == 0:
                        pool.wait_ge(sem("dtx_ready"), b + 1)
                    if n >= 2:
                        pool.wait_ge(sem("scanned"), b * NSTATE + n - 1)
                    nc.gpsimd.tensor_tensor(drive[:, r, :], dtx, bcast_b[:, r, :], ALU.mult).then_inc(sem("drive_ready"), 1)

        @block.tensor
        def _(pe):
            def bank(n, m=S):
                return psum[:, n, 0:m]

            def mm(out_, w, r, start=True, stop=True, **kw):
                return nc.tensor.matmul(out_, w, r, start=start, stop=stop, **kw)

            def layer_norm(s):
                for half in range(2):
                    pe.wait_ge(x_ready, x_before(s))
                    if s == 0 and half == 0:
                        pe.wait_ge(sem("ln_consts"), 48)
                        pe.wait_ge(sem("wT_ready"), 3)
                    for k in range(2):
                        m = mm(bank(4 * half + k), center[:], x[:, 2 * half + k, :])
                    m.then_inc(sem("ln_centered"), 1)
                for half in range(2):
                    pe.wait_ge(sem("ln_squared"), 2 * s + half + 1)
                    for k in range(2):
                        m = mm(bank(4 * half + 2 + k), mean[:], squares[:, 2 * half + k, :])
                    m.then_inc(sem("ln_var"), 1)

            def stage_norm(s):
                layer_norm(s)
                pe.wait_ge(ln_done, 2 * s + 2)

            pe.wait_ge(sem("eye_loaded"), 16)
            pe.wait_ge(sem("rows_loaded"), 16)
            for b in range(NB):
                for t in range(TT):
                    m = nc.tensor.transpose(psum[:, b, t * P:(t + 1) * P], rows[:, b * TT + t, :], eye[:])
                m.then_inc(sem("x_turned"), 1)
            pe.wait_ge(sem("wraw_loaded"), 16 * (11 + 3))
            for k in range(3):
                for t in range(4):
                    m = nc.tensor.transpose(psum[:, 4 + k, t * P:(t + 1) * P], wraw[:, 4 * k + t, :], eye[:])
                m.then_inc(sem("w_turned"), 1)

            stage_norm(ATTN0)
            pe.wait_ge(sem("wT_ready"), 3)
            pe.wait_ge(sem("token_sums"), 1)
            mm(psum[:, 0, 0:NB], wT[:, WV0, :], token_sum).then_inc(sem("attn0_mm"), 1)
            pe.wait_ge(sem("attn0_out"), 1)
            mm(psum[:, 1, 0:NB], wT[:, WO0, :], value_sum).then_inc(sem("attn0_mm"), 1)

            stage_norm(FFN0)
            pe.wait_ge(sem("trees_loaded"), 16 * (2 + 15))
            n_hid = 3 * HCH
            with pe.Fori(0, NB) as b:
                pe.wait_ge(x_ready, b + x_before(FFN0))
                mm(bank(6), nodeT, h[:, b, :]).then_inc(sem("scored0"), 1)
                pe.wait_ge(sem("gates_ready"), b + 1)
                mm(bank(7), leafpath[:], gates).then_inc(sem("counted0"), 1)

                def out_of(i):
                    f, c = divmod(i, HCH)
                    pe.wait_ge(sem("hid_act" if i % 2 == 0 else "hid_dve"), b * (n_hid // 2) + i // 2 + 1)
                    if f < 2:
                        m = mm(bank(3 + f), w2[f][:, c, :], hidden[:, c, :], c == 0, False)
                    else:
                        for t in range(TT):
                            m = mm(psum[:, 5, t * D:(t + 1) * D], hidden[:, c, t * P:(t + 1) * P], w2[f][:, c, :],
                                   c == 0 and t == 0, False, skip_group_check=True)
                    if c < HCH - 1:
                        return
                    if i == HCH - 1:
                        pe.wait_ge(sem("leaf_ready"), b + 1)
                    if f < 2:
                        m = mm(bank(3 + f), b2[:, f, :], leaf, False, True)
                    else:
                        for t in range(TT):
                            m = mm(psum[:, 5, t * D:(t + 1) * D], leaf[:, t * P:(t + 1) * P], b2[:, f, :],
                                   False, t == TT - 1, skip_group_check=True)
                    m.then_inc(sem("tree_out"), 1)

                for i in range(n_hid):
                    f, c = divmod(i, HCH)
                    if i >= 3:
                        pe.wait_ge(sem("hid_act" if (i - 3) % 2 == 0 else "hid_dve"), b * (n_hid // 2) + (i - 3) // 2 + 1)
                    mm(bank(i % 3), w1[f][:, c * P:(c + 1) * P], h[:, b, :], True, False)
                    mm(bank(i % 3), offpath[:, f, c, :], gates, False, True).then_inc(sem("hidden0"), 1)
                    if i >= 2:
                        out_of(i - 2)
                out_of(n_hid - 2)
                out_of(n_hid - 1)
                pe.wait_ge(sem("qkv0_ready"), b * 3 + 2)
                for t in range(TT):
                    if t >= 2:
                        pe.wait_ge(sem("exp0"), b * TT + t - 1)
                    mm(bank(t % 2), qT0[:, t * P:(t + 1) * P], kT0).then_inc(sem("scores0"), 1)

                    def attend(t):
                        pe.wait_ge(sem("probs0"), b * TT + t + 1)
                        if t >= 2:
                            pe.wait_ge(sem("probsT0"), b * TT + t - 1)
                        for k in range(TT):
                            m = nc.tensor.transpose(psum[:, (2, 6)[t % 2], k * P:(k + 1) * P], probs0[:, t % 2, k * P:(k + 1) * P], eye[:])
                        m.then_inc(sem("probs_turned0"), 1)

                    if t >= 1:
                        attend(t - 1)
                attend(TT - 1)
                pe.wait_ge(sem("probsT0"), b * TT + TT)
                pe.wait_ge(sem("qkv0_ready"), b * 3 + 3)
                for k in range(TT):
                    m = mm(bank(7), v0[:, k * D:(k + 1) * D], probsT0[:, k, :], k == 0, k == TT - 1)
                m.then_inc(sem("attn_out0"), 1)

            stage_norm(ATTN1)
            pe.wait_ge(sem("attn1_loaded"), 32)
            pe.wait_ge(sem("woT_ready"), 256)
            with pe.Fori(0, NB) as b:
                pe.wait_ge(x_ready, b + x_before(ATTN1))
                for n, w in enumerate((WQ1, WK1, WV1)):
                    mm(bank(n), wT[:, w, :], h[:, b, :]).then_inc(sem("qkv1_mm"), 1)
                pe.wait_ge(sem("vT_ready"), b + 1)
                for t in range(TT):
                    m = nc.tensor.transpose(psum[:, 3, t * P:(t + 1) * P], vT1[:, t * P:(t + 1) * P], eye[:])
                m.then_inc(sem("v_turned"), 1)
                pe.wait_ge(sem("stacked"), b * (18 * 16) + 18 * 16)
                pe.wait_ge(sem("v_ready"), b + 1)
                for hd in range(HEADS):
                    if hd >= 2:
                        pe.wait_ge(sem("maxed"), b * HEADS + hd - 1)
                    for t in range(TT):
                        m = mm(bank(4 * (hd % 2) + t), qstack[0:96, hd, t * P:(t + 1) * P], kstack[0:96, hd, :])
                    m.then_inc(sem("scores1"), 1)
                pe.wait_ge(sem("maxed"), b * HEADS + HEADS)
                for t in range(TT):
                    m = nc.tensor.transpose(psum[0:HEADS, 0, t * P:(t + 1) * P], headmax[:, t, :], eye[:])
                m.then_inc(sem("max_turned"), 1)
                pe.wait_ge(sem("max_stacked"), b * 48 + 48)

                def score_pairs(u):
                    g, p = divmod(u, 2)
                    for j in range(4):
                        n = 4 * u + j
                        if n >= 2:
                            pe.wait_ge(sem("exp1"), b * 32 + n - 1)
                        for k in range(2):
                            kt = 2 * p + k
                            m = mm(bank(2 * (n % 2) + k), kstack[:, 4 * g + j, kt * P:(kt + 1) * P], qstack[:, 4 * g + j, :])
                        m.then_inc(sem("scoresT1"), 1)

                def values(u):
                    g, p = divmod(u, 2)
                    pe.wait_ge(sem("exp1"), b * 32 + 4 * u + 4)
                    if p == 0 and g >= 2:
                        pe.wait_ge(sem("head_raw_ready"), b * GROUPS + g - 1)
                    for k in range(2):
                        kt = 2 * p + k
                        for j in range(4):
                            m = mm(psum[32 * j:32 * j + 32, 4 + g % 2, :], v32[:, kt, 4 * g + j, :], expT[:, u % 2, j, k, :],
                                   kt == 0, kt == TT - 1, tile_position=(0, 32 * j))
                    m.then_inc(sem("keys_added"), 1)

                def spread(g):
                    pe.wait_ge(sem("head_raw_ready"), b * GROUPS + g + 1)
                    if g >= 1:
                        pe.wait_ge(sem("head_inv_ready"), b * GROUPS + g)
                    mm(bank(6), rowsum[:], head_raw).then_inc(sem("sum_spread"), 1)

                def project(g):
                    pe.wait_ge(sem("head_out_ready"), b * GROUPS + g + 1)
                    mm(bank(7), woT[:, g, :], head_out, g == 0, g == GROUPS - 1).then_inc(sem("attn_out1"), 1)

                for u in range(8):
                    score_pairs(u)
                    if u >= 1:
                        values(u - 1)
                    if u >= 3 and u % 2 == 1:
                        spread((u - 3) // 2)
                    if u >= 4 and u % 2 == 0:
                        project((u - 4) // 2)
                values(7)
                project(GROUPS - 2)
                spread(GROUPS - 1)
                project(GROUPS - 1)

            def turn_logits(k, b, n):
                pe.wait_ge(sem("route_logits"), turn(k, b) + 1)
                for t in range(TT):
                    m = nc.tensor.transpose(psum[:, 1, t * P:(t + 1) * P], lt[:, t * P:(t + 1) * P], eye[:])
                m.then_inc(sem("route_logits_turned"), 1)

            def turn_weights(k, b, n):
                pe.wait_ge(sem("route_weights"), turn(k, b) + 1)
                for t in range(TT):
                    m = nc.tensor.transpose(psum[0:n, 3, t * P:(t + 1) * P], weight[:, t, 0:n], eye[:])
                m.then_inc(sem("route_weights_turned"), 1)

            stage_norm(FFN1)
            pe.wait_ge(sem("ffn1_loaded"), 16 * N_FFN1)
            with pe.Fori(0, NB) as b:
                pe.wait_ge(x_ready, b + x_before(FFN1))
                mm(psum[0:E1, 0, :], router1[:], h[:, b, :]).then_inc(sem("route_scored"), 1)
                turn_logits(1, b, E1)
                pe.wait_ge(sem("r1_counted"), b + 1)
                for t in range(TT):
                    mm(psum[:, 2, t * E1:(t + 1) * E1], before[:], chosen[:, t, :], t == 0, False, skip_group_check=True)
                    m = mm(psum[:, 2, t * E1:(t + 1) * E1], ones[:], earlier[:, t, :], False, t == TT - 1, skip_group_check=True)
                m.then_inc(sem("r1_placed"), 1)
                turn_weights(1, b, E1)
                pe.wait_ge(sem("route_parts"), turn(1, b) + 1)

                def down(e):
                    pe.wait_ge(sem("hid1_ready"), b * NE1 + e + 1)
                    mm(bank(7), down0[:, e, :], hid0[:, e % 2, :], e == 0, False).then_inc(sem("down0_done"), 1)
                    if e % 2 == 1 or e == NE1 - 1:
                        m = mm(bank(7), down1[:, e // 2, :], hid1[:, (e // 2) % 2, :], False, False)
                    if e == NE1 - 1:
                        mm(bank(7), eye[:], h[:, b, :], False, True).then_inc(sem("ffn1_out"), 1)

                for e in range(NE1):
                    s0 = 3 * (e % 2)
                    if e >= 2:
                        pe.wait_ge(sem("act1_ready"), b * (2 * NE1) + 2 * (e - 1))
                        pe.wait_ge(sem("prod1_ready"), b * NE1 + e - 1)
                    mm(bank(s0), gate0[:, e, :], h[:, b, :])
                    mm(bank(s0 + 1), rest[:, e, :], h[:, b, :])
                    mm(bank(s0 + 2), up0[:, e, :], h[:, b, :]).then_inc(sem("up1_done"), 1)
                    if e < E1:
                        if e >= 1:
                            pe.wait_ge(sem("hid1_ready"), b * NE1 + e)
                        mm(bank(6), pick[:, e, :], wparts[:]).then_inc(sem("w1_spread"), 1)
                    if e >= 1:
                        down(e - 1)
                down(NE1 - 1)

            stage_norm(ATTN2)
            pe.wait_ge(sem("ffn1_loaded"), 16 * N_FFN1)
            pe.wait_ge(sem("dt_rep_ready"), 1)
            with pe.Fori(0, NB) as b:
                pe.wait_ge(x_ready, b + x_before(ATTN2))
                mm(bank(0), wT[:, WX2, :], h[:, b, :])
                mm(bank(1), wT[:, WZ2, :], h[:, b, :]).then_inc(sem("xz_done"), 1)
                pe.wait_ge(sem("xconv_ready"), b + 1)
                mm(bank(2), wT[:, WSSM, :], xconv)
                mm(bank(3), dt_rep[:], xconv).then_inc(sem("ssm_done"), 1)
                pe.wait_ge(sem("bc_parts"), b + 1)
                pe.wait_ge(sem("dtx_ready"), b + 1)

                def add_state(n):
                    pe.wait_ge(sem("read_ready"), b * NSTATE + n + 1)
                    mm(bank(6), eye[:], read[:, n % 2, :], n == 0, n == NSTATE - 1).then_inc(sem("y_added"), 1)

                for n in range(NSTATE):
                    r = n % 2
                    if n >= 2:
                        pe.wait_ge(sem("b_spread"), b * NSTATE + n - 1)
                        pe.wait_ge(sem("read_ready"), b * NSTATE + n - 1)
                    mm(bank(2 + r), pick[:, n, :], wparts[:]).then_inc(sem("b_done"), 1)
                    mm(bank(4 + r), pick[:, NSTATE + n, :], wparts[:]).then_inc(sem("c_done"), 1)
                    if n >= 1:
                        add_state(n - 1)
                add_state(NSTATE - 1)
                pe.wait_ge(sem("ygate_ready"), b + 1)
                mm(bank(7), wT[:, WOUT2, :], ygate).then_inc(sem("attn_out2"), 1)

            stage_norm(FFN2)
            pe.wait_ge(sem("ffn2_loaded"), 64)
            with pe.Fori(0, NB) as b:
                pe.wait_ge(x_ready, b + x_before(FFN2))
                mm(psum[0:E2, 0, :], wg2[:], h[:, b, :]).then_inc(sem("route_scored"), 1)
                turn_logits(2, b, E2)
                turn_weights(2, b, E2)
                pe.wait_ge(sem("route_parts"), turn(2, b) + 1)
                NC = 2 * E2

                def down2(i):
                    e, k = divmod(i, 2)
                    pe.wait_ge(sem("hid2_ready"), b * NC + i + 1)
                    m = mm(bank(7), w3_2[:, e, k, :], hid0[:, i % 2, :], i == 0, i == NC - 1)
                    m.then_inc(sem("down2_done"), 1)

                for i in range(NC):
                    e, k = divmod(i, 2)
                    s0 = 2 * (i % 2)
                    if i >= 2:
                        pe.wait_ge(sem("gact2_ready"), b * NC + i - 1)
                        pe.wait_ge(sem("prod2_ready"), b * NC + i - 1)
                    mm(bank(s0), w1_2[:, e, k * P:(k + 1) * P], h[:, b, :])
                    mm(bank(s0 + 1), w2_2[:, e, k * P:(k + 1) * P], h[:, b, :]).then_inc(sem("up2_done"), 1)
                    if k == 0:
                        if e >= 2:
                            pe.wait_ge(sem("hid2_ready"), b * NC + 2 * (e - 1))
                        mm(bank(4 + e % 2), pick[:, e, :], wparts[:]).then_inc(sem("w2_spread"), 1)
                    if i >= 1:
                        down2(i - 1)
                down2(NC - 1)

            stage_norm(ATTN3)
            pe.wait_ge(sem("attn3_loaded"), 16 * 9)
            with pe.Fori(0, NB) as b:
                pe.wait_ge(x_ready, b + x_before(ATTN3))
                mm(bank(0), w_3[:, W_IN, :], h[:, b, :]).then_inc(sem("xw_done"), 1)
                pe.wait_ge(sem("xw_ready"), b + 1)
                mm(bank(1), w_3[:, W_GX, :], xw)
                mm(bank(2), w_3[:, W_GA, :], xw).then_inc(sem("gates3_done"), 1)
                pe.wait_ge(sem("state3_ready"), b + 1)
                mm(bank(3), w_3[:, W_OUT, :], st3).then_inc(sem("attn_out3"), 1)

            stage_norm(FFN3)
            pe.wait_ge(sem("ffn3_loaded"), 48)
            with pe.Fori(0, NB) as b:
                pe.wait_ge(x_ready, b + x_before(FFN3))
                mm(psum[0:E3, 0, :], wT[:, WROUT3, 0:E3], h[:, b, :]).then_inc(sem("route_scored"), 1)
                turn_logits(3, b, E3)
                turn_weights(3, b, E3)
                pe.wait_ge(sem("route_parts"), turn(3, b) + 1)
                mm(bank(7), bias3[0:E3, :], sel3[0:E3, :], True, False)
                for e in range(E3):
                    r = e % 2
                    if e >= 2:
                        pe.wait_ge(sem("picked_ready"), b * E3 + e - 1)
                    mm(bank(4 + r), pick[:, e, :], wparts[:]).then_inc(sem("w3_spread"), 1)
                    if e >= 1:
                        pe.wait_ge(sem("picked_ready"), b * E3 + e)
                        mm(bank(7), w_e3[:, e - 1, :], picked[:, (e - 1) % 2, :], False, False).then_inc(sem("y3_added"), 1)
                pe.wait_ge(sem("picked_ready"), b * E3 + E3)
                mm(bank(7), w_e3[:, E3 - 1, :], picked[:, (E3 - 1) % 2, :], False, True).then_inc(sem("y3_added"), 1)

            pe.wait_ge(x_ready, x_before(FFN3 + 1))
            for b in range(NB):
                for t in range(TT):
                    m = nc.tensor.transpose(psum[:, b, t * D:(t + 1) * D], x[:, b, t * P:(t + 1) * P], eye[:])
                m.then_inc(sem("out_turned"), 1)

        @block.scalar
        def _(act):
            def bank(n, m=S):
                return psum[:, n, 0:m]

            def f(out_, in_, func, **kw):
                return nc.scalar.activation(out_, in_, func, **kw)

            def layer_norm(s):
                for half in range(2):
                    act.wait_ge(sem("ln_centered"), 2 * s + half + 1)
                    f(squares[:, 2 * half:2 * half + 2, :], psum[:, 4 * half:4 * half + 2, :], ACT.Square).then_inc(sem("ln_squared"), 1)
                for half in range(2):
                    act.wait_ge(sem("ln_var"), 2 * s + half + 1)
                    f(std[:, 2 * half:2 * half + 2, :], psum[:, 4 * half + 2:4 * half + 4, :], ACT.Sqrt, bias=eps[:]).then_inc(sem("ln_std"), 1)

            act.wait_ge(sem("cleared"), 5)
            for k in range(3):
                act.wait_ge(sem("w_turned"), k + 1)
                f(wT[:, 4 * k:4 * k + 4, :], bank(4 + k).rearrange("p (n d) -> p n d", n=4), ACT.Copy).then_inc(sem("wT_ready"), 1)

            layer_norm(ATTN0)
            act.wait_ge(sem("attn0_mm"), 1)
            f(value_sum, psum[:, 0, 0:NB], ACT.Copy).then_inc(sem("attn0_out"), 1)
            act.wait_ge(sem("attn0_mm"), 2)
            f(attn0, psum[:, 1, 0:NB], ACT.Copy).then_inc(sem("attn0_out"), 1)

            layer_norm(FFN0)
            act.wait_ge(sem("trees_loaded"), 16 * (2 + 15))
            n_hid = 3 * HCH
            with act.Fori(0, NB) as b:
                for i in range(0, n_hid, 2):
                    t, c = divmod(i, HCH)
                    act.wait_ge(sem("hidden0"), b * n_hid + i + 1)
                    if i >= HCH and c == 0:
                        act.wait_ge(sem("tree_out"), b * 3 + t)
                    f(hidden[:, c, :], bank(i % 3), ACT.Relu, bias=b1[:, t, c:c + 1]).then_inc(sem("hid_act"), 1)
                    if i in (HCH + 2, 2 * HCH + 2):
                        act.wait_ge(sem("tree_out"), b * 3 + t)
                        f((qT0, kT0)[t - 1], bank(2 + t), ACT.Copy).then_inc(sem("qkv0_ready"), 1)
                act.wait_ge(sem("tree_out"), b * 3 + 3)
                f(v0, bank(5), ACT.Copy).then_inc(sem("qkv0_ready"), 1)

                def copy_turned(t):
                    act.wait_ge(sem("probs_turned0"), b * TT + t + 1)
                    f(probsT0[:, :, t * P:(t + 1) * P], bank((2, 6)[t % 2]).rearrange("p (k q) -> p k q", k=TT),
                      ACT.Copy).then_inc(sem("probsT0"), 1)

                for t in range(TT):
                    act.wait_ge(sem("shift0"), b * TT + t + 1)
                    if t >= 2:
                        act.wait_ge(sem("probs_turned0"), b * TT + t - 1)
                    f(probs0[:, t % 2, :], bank(t % 2), ACT.Exp, bias=small[:, 1, t:t + 1], scale=SCALE0,
                      accum_out=small[:, 2, t:t + 1]).then_inc(sem("exp0"), 1)
                    if t >= 1:
                        copy_turned(t - 1)
                copy_turned(TT - 1)

            layer_norm(ATTN1)
            with act.Fori(0, NB) as b:
                act.wait_ge(sem("qkv1_mm"), b * 3 + 3)
                f(vT1, bank(2), ACT.Copy).then_inc(sem("vT_ready"), 1)
                for u in range(8):
                    g, p = divmod(u, 2)
                    for j in range(4):
                        n = 4 * u + j
                        act.wait_ge(sem("scoresT1"), b * 32 + n + 1)
                        if u >= 2 and j == 0:
                            act.wait_ge(sem("keys_added"), b * 8 + u - 1)
                        f(expT[:, u % 2, j, :, :], psum[:, 2 * (n % 2):2 * (n % 2) + 2, :], ACT.Exp).then_inc(sem("exp1"), 1)

            layer_norm(FFN1)
            act.wait_ge(sem("logits_cleared"), 1)
            with act.Fori(0, NB) as b:
                act.wait_ge(sem("route_scored"), turn(1, b) + 1)
                f(lt[0:E1, :], psum[0:E1, 0, :], ACT.Identity, bias=router1_b[0:E1, :]).then_inc(sem("route_logits"), 1)
                act.wait_ge(sem("r1_shift"), b + 1)
                for t in range(TT):
                    m = f(prob[:, t, :], psum[:, 1, t * P:t * P + E1], ACT.Exp, bias=small[:, 1, t:t + 1],
                          accum_out=small[:, 2, t:t + 1])
                m.then_inc(sem("r1_exp"), 1)
                for e in range(NE1):
                    s0 = 3 * (e % 2)
                    gr = slice(64 * (e % 2), 64 * (e % 2) + F1R)
                    act.wait_ge(sem("up1_done"), b * NE1 + e + 1)
                    if e >= 2:
                        act.wait_ge(sem("prod1_ready"), b * NE1 + e - 1)
                    f(gact0[:, e % 2, :], bank(s0), ACT.Silu).then_inc(sem("act1_ready"), 1)
                    f(gact1[gr, e % 2, :], psum[gr, s0 + 1, :], ACT.Silu).then_inc(sem("act1_ready"), 1)

            layer_norm(ATTN2)
            act.wait_ge(sem("attn2_loaded"), 80)
            f(a_neg[:], a_neg[:], ACT.Exp).then_inc(sem("a_exp"), 1)
            act.wait_ge(sem("a_neg_ready"), 1)
            with act.Fori(0, NB) as b:
                act.wait_ge(sem("xz_done"), b + 1)
                f(xpad[:, DCONV - 1:DCONV - 1 + S], bank(0), ACT.Copy).then_inc(sem("xin_ready"), 1)
                f(zgate, bank(1), ACT.Silu).then_inc(sem("zgate_ready"), 1)
                act.wait_ge(sem("conv_ready"), b + 1)
                f(xconv, conv, ACT.Silu).then_inc(sem("xconv_ready"), 1)
                act.wait_ge(sem("dtv_ready"), b + 1)
                f(dtl, dtv, ACT.Abs).then_inc(sem("dtl_step"), 1)
                act.wait_ge(sem("dtl_step"), b * 3 + 1)
                f(dtl, dtl, ACT.Exp, scale=-1.0).then_inc(sem("dtl_step"), 1)
                act.wait_ge(sem("dtl_step"), b * 3 + 2)
                f(dtl, dtl, ACT.Ln, bias=one[:]).then_inc(sem("dtl_step"), 1)
                act.wait_ge(sem("dtx_ready"), b + 1)
                for n in range(NSTATE):
                    r = n % 2
                    act.wait_ge(sem("b_done"), b * NSTATE + n + 1)
                    if n >= 2:
                        act.wait_ge(sem("drive_ready"), b * NSTATE + n - 1)
                        act.wait_ge(sem("scanned"), b * NSTATE + n - 1)
                    f(bcast_b[:, r, :], bank(2 + r), ACT.Copy).then_inc(sem("b_spread"), 1)
                    f(decay[:, r, :], dt, ACT.Exp, scale=a_neg[:, n:n + 1]).then_inc(sem("decay_ready"), 1)

            layer_norm(FFN2)
            act.wait_ge(sem("logits_cleared"), 2)
            NC = 2 * E2
            with act.Fori(0, NB) as b:
                act.wait_ge(sem("route_scored"), turn(2, b) + 1)
                f(lt[0:E2, :], psum[0:E2, 0, :], ACT.Copy).then_inc(sem("route_logits"), 1)
                act.wait_ge(sem("r2_gap"), b + 1)
                f(small[:, 1, :], small[:, 0, :], ACT.Exp).then_inc(sem("r2_exp"), 1)
                for i in range(NC):
                    act.wait_ge(sem("up2_done"), b * NC + i + 1)
                    if i >= 2:
                        act.wait_ge(sem("prod2_ready"), b * NC + i - 1)
                    f(gact0[:, i % 2, :], bank(2 * (i % 2)), ACT.Silu).then_inc(sem("gact2_ready"), 1)

            layer_norm(ATTN3)
            act.wait_ge(sem("attn3_loaded"), 16 * 9)
            f(a_par[:, 1:2], a_par[:, 0:1], ACT.Abs).then_inc(sem("apar_step"), 1)
            act.wait_ge(sem("apar_step"), 1)
            f(a_par[:, 1:2], a_par[:, 1:2], ACT.Exp, scale=-1.0).then_inc(sem("apar_step"), 1)
            act.wait_ge(sem("apar_step"), 2)
            f(a_par[:, 1:2], a_par[:, 1:2], ACT.Ln, bias=one[:]).then_inc(sem("apar_step"), 1)
            act.wait_ge(sem("apar_ready"), 3)
            with act.Fori(0, NB) as b:
                act.wait_ge(sem("xw_done"), b + 1)
                f(xw, bank(0), ACT.Identity, bias=b_3[:, W_IN:W_IN + 1]).then_inc(sem("xw_ready"), 1)
                act.wait_ge(sem("gates3_done"), b + 1)
                f(gx, bank(1), ACT.Sigmoid, bias=b_3[:, W_GX:W_GX + 1]).then_inc(sem("gx_ready"), 1)
                f(ga, bank(2), ACT.Sigmoid, bias=b_3[:, W_GA:W_GA + 1]).then_inc(sem("ga_ready"), 1)
                act.wait_ge(sem("ga_ready"), b + 1)
                f(dec, ga, ACT.Exp, scale=a_par[:, 2:3]).then_inc(sem("dec_ready"), 1)
                f(drv, ga, ACT.Exp, scale=a_par[:, 3:4]).then_inc(sem("drv_step"), 1)
                act.wait_ge(sem("drv_step"), b + 1)
                f(drv, drv, ACT.Sqrt, scale=-1.0, bias=one[:]).then_inc(sem("drv_ready"), 1)

            layer_norm(FFN3)
            act.wait_ge(sem("logits_cleared"), 3)
            with act.Fori(0, NB) as b:
                act.wait_ge(sem("route_scored"), turn(3, b) + 1)
                f(lt[0:E3, :], psum[0:E3, 0, :], ACT.Identity, bias=router3_b[0:E3, :]).then_inc(sem("route_logits"), 1)

            for b in range(NB):
                act.wait_ge(sem("out_turned"), b + 1)
                f(rows[:, b * TT:(b + 1) * TT, :], bank(b).rearrange("p (t d) -> p t d", t=TT), ACT.Copy).then_inc(sem("out_rows"), 1)

        @block.vector
        def _(dve):
            v = nc.vector

            def bank(n, m=S):
                return psum[:, n, 0:m]

            class Steps:

                def __init__(self, name, b=0, per=0):
                    self.sem, self.b, self.per, self.n = sem(name), b, per, 0

                def did(self, instruction):
                    instruction.then_inc(self.sem, 1)
                    self.n += 1

                def wait(self):
                    dve.wait_ge(self.sem, self.b * self.per + self.n)

                def then(self, instruction_of):
                    self.wait()
                    self.did(instruction_of())

                def end(self):
                    assert self.n == self.per, self.n

            def layer_norm(s):
                for half in range(2):
                    hv = slice(2 * half, 2 * half + 2)
                    dve.wait_ge(sem("ln_std"), 2 * s + half + 1)
                    v.reciprocal(std[:, hv, :], std[:, hv, :]).then_inc(sem("ln_rstd"), 1)
                    dve.wait_ge(sem("ln_rstd"), 2 * s + half + 1)
                    v.tensor_tensor(h[:, hv, :], psum[:, 4 * half:4 * half + 2, :], std[:, hv, :], ALU.mult).then_inc(ln_done, 1)

            def add_to_x(b, n):
                v.tensor_tensor(x[:, b, :], bank(n), x[:, b, :], ALU.add).then_inc(x_ready, 1)

            for b in range(NB):
                dve.wait_ge(sem("x_turned"), b + 1)
                v.tensor_copy(x[:, b, :], bank(b)).then_inc(x_ready, 1)

            layer_norm(ATTN0)
            dve.wait_ge(ln_done, 2)
            v.reduce_sum(token_sum, h[:], AX.X).then_inc(sem("token_sums"), 1)
            dve.wait_ge(sem("attn0_out"), 2)
            for b in range(NB):
                v.tensor_scalar(x[:, b, :], x[:, b, :], attn0[:, b:b + 1], None, ALU.add).then_inc(x_ready, 1)

            layer_norm(FFN0)
            dve.wait_ge(sem("trees_loaded"), 16 * (2 + 15))
            n_hid = 3 * HCH
            with dve.Fori(0, NB) as b:
                dve.wait_ge(sem("scored0"), b + 1)
                v.tensor_scalar(gates, bank(6), node_b[:], 0.0, ALU.add, ALU.is_ge).then_inc(sem("gates_ready"), 1)
                dve.wait_ge(sem("counted0"), b + 1)
                v.tensor_scalar(leaf, bank(7), 0.0, None, ALU.is_equal).then_inc(sem("leaf_ready"), 1)
                for i in range(1, n_hid, 2):
                    t, c = divmod(i, HCH)
                    dve.wait_ge(sem("hidden0"), b * n_hid + i + 1)
                    if t >= 1 and c == 1:
                        dve.wait_ge(sem("tree_out"), b * 3 + t)
                    v.tensor_scalar(hidden[:, c, :], bank(i % 3), b1[:, t, c:c + 1], 0.0, ALU.add, ALU.max).then_inc(sem("hid_dve"), 1)
                for t in range(TT):
                    dve.wait_ge(sem("scores0"), b * TT + t + 1)
                    v.reduce_max(small[:, 0, t:t + 1], bank(t % 2), AX.X).then_inc(sem("max0"), 1)
                    dve.wait_ge(sem("max0"), b * TT + t + 1)
                    v.tensor_scalar(small[:, 1, t:t + 1], small[:, 0, t:t + 1], -SCALE0, None, ALU.mult).then_inc(sem("shift0"), 1)
                    dve.wait_ge(sem("exp0"), b * TT + t + 1)
                    v.reciprocal(small[:, 3, t:t + 1], small[:, 2, t:t + 1]).then_inc(sem("inv0"), 1)
                    dve.wait_ge(sem("inv0"), b * TT + t + 1)
                    v.tensor_scalar(probs0[:, t % 2, :], probs0[:, t % 2, :], small[:, 3, t:t + 1], None, ALU.mult).then_inc(sem("probs0"), 1)
                dve.wait_ge(sem("attn_out0"), b + 1)
                add_to_x(b, 7)

            def cut(b, tag, n, scale, rows_, parts, rem, ready):
                src = psum[rows_, n, :]
                st = Steps(tag + "_cut", b, 3)
                st.did(v.tensor_scalar(parts[rows_, 0, :], src, scale, None, ALU.mult))
                st.then(lambda: v.scalar_tensor_tensor(rem[rows_], src, scale, parts[rows_, 0, :], ALU.mult, ALU.subtract))
                st.then(lambda: v.tensor_copy(parts[rows_, 1, :], rem[rows_]))
                st.wait()
                st.end()
                v.tensor_tensor(parts[rows_, 2, :], rem[rows_], parts[rows_, 1, :], ALU.subtract).then_inc(sem(ready), 1)

            layer_norm(ATTN1)
            dve.wait_ge(sem("cleared"), N_CLEARED)
            everything, heads = slice(0, P), slice(0, HEADS)
            with dve.Fori(0, NB) as b:
                dve.wait_ge(sem("qkv1_mm"), b * 3 + 2)
                cut(b, "q", 0, SCALE1, everything, qparts, qrem, "qparts_ready")
                cut(b, "k", 1, SCALE1, everything, kparts, krem, "kparts_ready")
                dve.wait_ge(sem("v_turned"), b + 1)
                v.tensor_copy(v32[:, :, :, 0:DH], bank(3).rearrange("p (t h d) -> p t h d", t=TT, h=HEADS)).then_inc(sem("v_ready"), 1)
                for hd in range(HEADS):
                    s0 = 4 * (hd % 2)
                    dve.wait_ge(sem("scores1"), b * HEADS + hd + 1)
                    v.reduce_max(headmax[:, :, hd], psum[:, s0:s0 + 4, :], AX.X).then_inc(sem("maxed"), 1)
                dve.wait_ge(sem("max_turned"), b + 1)
                cut(b, "m", 0, -1.0, heads, mparts, mrem, "mparts_ready")
                for g in range(GROUPS):
                    dve.wait_ge(sem("keys_added"), b * 8 + 2 * g + 2)
                    if g >= 1:
                        dve.wait_ge(sem("sum_spread"), b * GROUPS + g)
                        dve.wait_ge(sem("head_out_ready"), b * GROUPS + g)
                    v.tensor_copy(head_raw, bank(4 + g % 2)).then_inc(sem("head_raw_ready"), 1)
                    dve.wait_ge(sem("sum_spread"), b * GROUPS + g + 1)
                    v.reciprocal(head_inv, bank(6)).then_inc(sem("head_inv_ready"), 1)
                    if g >= 1:
                        dve.wait_ge(sem("attn_out1"), b * GROUPS + g)
                    dve.wait_ge(sem("head_raw_ready"), b * GROUPS + g + 1)
                    dve.wait_ge(sem("head_inv_ready"), b * GROUPS + g + 1)
                    v.tensor_tensor(head_out, head_raw, head_inv, ALU.mult).then_inc(sem("head_out_ready"), 1)
                dve.wait_ge(sem("attn_out1"), b * GROUPS + GROUPS)
                v.scalar_tensor_tensor(x[:, b, :], bank(7), bout1[:], x[:, b, :], ALU.add, ALU.add).then_inc(x_ready, 1)

            def weight_parts(k, b, src, n):
                st = Steps("route_cut", turn(k, b), 4)
                st.did(v.tensor_copy(wparts[0:n, :], src))
                st.then(lambda: v.tensor_tensor(part_r[0:n, :], src, wparts[0:n, :], ALU.subtract))
                st.then(lambda: v.tensor_copy(part_b[0:n, :], part_r[0:n, :]))
                st.then(lambda: v.tensor_copy(wparts[32:32 + n, :], part_b[0:n, :]))
                st.end()
                v.tensor_tensor(wparts[64:64 + n, :], part_r[0:n, :], part_b[0:n, :], ALU.subtract).then_inc(sem("route_parts"), 1)

            def two_best(st, n, of):
                st.did(v.memset(top_f[:, :, 0:4], 0.0))
                for t in range(TT):
                    st.did(v.max(top[:, t, :], of(t)))
                st.wait()
                st.did(v.memset(top_f[:, :, 4:8], 0.0))
                for t in range(TT):
                    st.did(v.max_index(top_at[:, t, :], top[:, t, :], of(t)))
                st.then(lambda: v.tensor_copy(top_f[:, :, 0:2], top_at[:, :, 0:2]))
                st.wait()

            def clear_logits(stage, k):
                dve.wait_ge(ln_done, 2 * stage + 2)
                v.memset(lt, 0.0).then_inc(sem("logits_cleared"), 1)

            def best(n, t, k):
                return iota[:, 0:n], top_f[:, t, k:k + 1]

            layer_norm(FFN1)
            dve.wait_ge(sem("ffn1_loaded"), 16 * N_FFN1)
            dve.wait_ge(ln_done, 2 * FFN1 + 2)
            v.memset(hid1, 0.0).then_inc(sem("hid1_cleared"), 1)
            dve.wait_ge(sem("hid1_cleared"), 1)
            clear_logits(FFN1, 1)
            with dve.Fori(0, NB) as b:
                dve.wait_ge(sem("route_logits_turned"), turn(1, b) + 1)
                l3 = bank(1).rearrange("p (t e) -> p t e", t=TT)[:, :, 0:E1]
                st = Steps("r1_step", b, 43)
                st.did(v.reduce_max(small[:, 0, :], l3, AX.X))
                st.wait()
                v.tensor_scalar(small[:, 1, :], small[:, 0, :], -1.0, None, ALU.mult).then_inc(sem("r1_shift"), 1)
                dve.wait_ge(sem("r1_exp"), b + 1)
                st.did(v.reciprocal(small[:, 3, :], small[:, 2, :]))
                st.wait()
                for t in range(TT):
                    st.did(v.tensor_scalar(prob[:, t, :], prob[:, t, :], small[:, 3, t:t + 1], None, ALU.mult))
                st.wait()
                two_best(st, E1, lambda t: prob[:, t, :])
                st.did(v.tensor_tensor(small[:, 4, :], top[:, :, 0], top[:, :, 1], ALU.add))
                st.then(lambda: v.tensor_scalar(small[:, 4, :], small[:, 4, :], 1e-9, None, ALU.add))
                st.then(lambda: v.reciprocal(small[:, 5, :], small[:, 4, :]))
                st.wait()
                for k in range(K1):
                    st.did(v.tensor_tensor(small[:, 6 + k, :], top[:, :, k], small[:, 5, :], ALU.mult))
                st.wait()
                for t in range(TT):
                    i, at = best(E1, t, 0)
                    st.did(v.tensor_scalar(chosen[:, t, :], i, at, None, ALU.is_equal))
                    st.did(v.tensor_scalar(weight[:, t, :], i, at, small[:, 6, t:t + 1], ALU.is_equal, ALU.mult))
                    i, at = best(E1, t, 1)
                    st.did(v.tensor_scalar(prob[:, t, :], i, at, small[:, 7, t:t + 1], ALU.is_equal, ALU.mult))
                st.wait()
                for t in range(TT):
                    i, at = best(E1, t, 1)
                    st.did(v.scalar_tensor_tensor(chosen[:, t, :], i, at, chosen[:, t, :], ALU.is_equal, ALU.add))
                st.did(v.tensor_tensor(weight[:], weight[:], prob[:], ALU.add))
                for t in range(TT):
                    st.wait()
                    m = v.tensor_tensor(earlier[:, t + 1, :], earlier[:, t, :], chosen[:, t, :], ALU.add)
                    if t < TT - 1:
                        st.did(m)
                m.then_inc(sem("r1_counted"), 1)
                dve.wait_ge(sem("r1_placed"), b + 1)
                dve.wait_ge(sem("r1_counted"), b + 1)
                st.did(v.tensor_copy(earlier[:, 0, :], earlier[:, TT, :]))
                p3 = psum[:, 2, 0:TT * E1].rearrange("p (t e) -> p t e", t=TT)
                st.wait()
                st.end()
                v.scalar_tensor_tensor(weight[:], p3, float(CAP), weight[:], ALU.is_lt, ALU.mult).then_inc(sem("route_weights"), 1)
                dve.wait_ge(sem("route_weights_turned"), turn(1, b) + 1)
                weight_parts(1, b, psum[0:E1, 3, :], E1)
                for e in range(NE1):
                    s0, r, q = 3 * (e % 2), e % 2, e // 2 % 2
                    gr = slice(64 * (e % 2), 64 * (e % 2) + F1R)
                    ur = slice(64 - 64 * (e % 2), 64 - 64 * (e % 2) + F1R)
                    dve.wait_ge(sem("act1_ready"), b * (2 * NE1) + 2 * e + 2)
                    if e >= 2:
                        dve.wait_ge(sem("down0_done"), b * NE1 + e - 1)
                    if e == E1:
                        v.tensor_tensor(hid0[:, r, :], bank(s0 + 2), gact0[:, r, :], ALU.mult).then_inc(sem("prod1_ready"), 1)
                        v.tensor_tensor(hid1[gr, q, :], psum[ur, s0 + 1, :], gact1[gr, r, :], ALU.mult).then_inc(sem("hid1_ready"), 1)
                        continue
                    v.tensor_tensor(prod0[:, r, :], bank(s0 + 2), gact0[:, r, :], ALU.mult)
                    v.tensor_tensor(prod1[gr, r, :], psum[ur, s0 + 1, :], gact1[gr, r, :], ALU.mult).then_inc(sem("prod1_ready"), 1)
                    dve.wait_ge(sem("w1_spread"), b * E1 + e + 1)
                    dve.wait_ge(sem("prod1_ready"), b * NE1 + e + 1)
                    v.tensor_tensor(hid0[:, r, :], bank(6), prod0[:, r, :], ALU.mult)
                    v.tensor_tensor(hid1[gr, q, :], psum[gr, 6, :], prod1[gr, r, :], ALU.mult).then_inc(sem("hid1_ready"), 1)
                dve.wait_ge(sem("ffn1_out"), b + 1)
                add_to_x(b, 7)

            layer_norm(ATTN2)
            dve.wait_ge(sem("wT_ready"), 3)
            v.tensor_scalar(dt_rep[:], ones[:], wT[:, WSSM, 2 * NSTATE:2 * NSTATE + 1], None, ALU.mult).then_inc(sem("dt_rep_ready"), 1)
            dve.wait_ge(sem("a_exp"), 1)
            v.tensor_scalar(a_neg[:], a_neg[:], -1.0, None, ALU.mult).then_inc(sem("a_neg_ready"), 1)
            dve.wait_ge(ln_done, 2 * ATTN2 + 2)
            v.memset(xpad[:, 0:DCONV - 1], 0.0).then_inc(sem("xpad_cleared"), 1)
            dve.wait_ge(sem("xpad_cleared"), 1)
            with dve.Fori(0, NB) as b:
                dve.wait_ge(sem("xin_ready"), b + 1)
                st = Steps("conv_step", b, DCONV - 1)
                st.did(v.tensor_scalar(conv, xpad[:, 0:S], conv_w[:, 0:1], conv_b[:], ALU.mult, ALU.add))
                for k in range(1, DCONV):
                    st.wait()
                    m = v.scalar_tensor_tensor(conv, xpad[:, k:k + S], conv_w[:, k:k + 1], conv, ALU.mult, ALU.add)
                    if k < DCONV - 1:
                        st.did(m)
                st.end()
                m.then_inc(sem("conv_ready"), 1)
                dve.wait_ge(sem("ssm_done"), b + 1)
                v.tensor_scalar(dtv, bank(3), dt_w[:], dt_b[:], ALU.mult, ALU.add).then_inc(sem("dtv_ready"), 1)
                st = Steps("bc_step", b, 4)
                bcp = psum[0:2 * NSTATE, 2, :]
                st.did(v.tensor_copy(wparts[0:32, :], bcp))
                st.then(lambda: v.tensor_tensor(part_r, bcp, wparts[0:32, :], ALU.subtract))
                st.then(lambda: v.tensor_copy(part_b, part_r))
                st.then(lambda: v.tensor_copy(wparts[32:64, :], part_b))
                st.end()
                v.tensor_tensor(wparts[64:96, :], part_r, part_b, ALU.subtract).then_inc(sem("bc_parts"), 1)
                dve.wait_ge(sem("dtl_step"), b * 3 + 3)
                dve.wait_ge(sem("dtv_ready"), b + 1)
                v.scalar_tensor_tensor(dt, dtv, 0.0, dtl, ALU.max, ALU.add).then_inc(sem("dt_ready"), 1)
                dve.wait_ge(sem("dt_ready"), b + 1)
                v.tensor_tensor(dtx, dt, xconv, ALU.mult).then_inc(sem("dtx_ready"), 1)
                for n in range(NSTATE):
                    r = n % 2
                    dve.wait_ge(sem("decay_ready"), b * NSTATE + n + 1)
                    dve.wait_ge(sem("drive_ready"), b * NSTATE + n + 1)
                    v.tensor_tensor_scan(state[:, r, :], decay[:, r, :], drive[:, r, :], 0.0, ALU.mult, ALU.add).then_inc(sem("scanned"), 1)
                    dve.wait_ge(sem("c_done"), b * NSTATE + n + 1)
                    if n >= 2:
                        dve.wait_ge(sem("y_added"), b * NSTATE + n - 1)
                    dve.wait_ge(sem("scanned"), b * NSTATE + n + 1)
                    v.tensor_tensor(read[:, r, :], bank(4 + r), state[:, r, :], ALU.mult).then_inc(sem("read_ready"), 1)
                dve.wait_ge(sem("y_added"), b * NSTATE + NSTATE)
                dve.wait_ge(sem("zgate_ready"), b + 1)
                v.tensor_tensor(ygate, bank(6), zgate, ALU.mult).then_inc(sem("ygate_ready"), 1)
                dve.wait_ge(sem("attn_out2"), b + 1)
                add_to_x(b, 7)

            layer_norm(FFN2)
            clear_logits(FFN2, 2)
            NC = 2 * E2
            with dve.Fori(0, NB) as b:
                dve.wait_ge(sem("route_logits_turned"), turn(2, b) + 1)
                st = Steps("r2_step", b, 25)
                two_best(st, E2, lambda t: psum[:, 1, t * P:t * P + E2])
                v.tensor_tensor(small[:, 0, :], top[:, :, 1], top[:, :, 0], ALU.subtract).then_inc(sem("r2_gap"), 1)
                dve.wait_ge(sem("r2_exp"), b + 1)
                st.did(v.tensor_scalar(small[:, 2, :], small[:, 1, :], 1.0, None, ALU.add))
                st.then(lambda: v.reciprocal(small[:, 3, :], small[:, 2, :]))
                st.then(lambda: v.tensor_tensor(small[:, 4, :], small[:, 1, :], small[:, 3, :], ALU.mult))
                st.wait()
                for t in range(TT):
                    for k, dst in ((0, weight), (1, prob)):
                        i, at = best(E2, t, k)
                        st.did(v.tensor_scalar(dst[:, t, 0:E2], i, at, small[:, 3 + k, t:t + 1], ALU.is_equal, ALU.mult))
                st.wait()
                for t in range(TT):
                    m = v.tensor_tensor(weight[:, t, 0:E2], weight[:, t, 0:E2], prob[:, t, 0:E2], ALU.add)
                    if t < TT - 1:
                        st.did(m)
                st.end()
                m.then_inc(sem("route_weights"), 1)
                dve.wait_ge(sem("route_weights_turned"), turn(2, b) + 1)
                weight_parts(2, b, psum[0:E2, 3, :], E2)
                for i in range(NC):
                    e, k = divmod(i, 2)
                    s0, r = 2 * (i % 2), i % 2
                    dve.wait_ge(sem("gact2_ready"), b * NC + i + 1)
                    v.tensor_tensor(prod0[:, r, :], bank(s0 + 1), gact0[:, r, :], ALU.mult).then_inc(sem("prod2_ready"), 1)
                    dve.wait_ge(sem("w2_spread"), b * E2 + e + 1)
                    if i >= 2:
                        dve.wait_ge(sem("down2_done"), b * NC + i - 1)
                    dve.wait_ge(sem("prod2_ready"), b * NC + i + 1)
                    v.tensor_tensor(hid0[:, r, :], bank(4 + e % 2), prod0[:, r, :], ALU.mult).then_inc(sem("hid2_ready"), 1)
                dve.wait_ge(sem("down2_done"), b * NC + NC)
                add_to_x(b, 7)

            layer_norm(ATTN3)
            dve.wait_ge(sem("apar_step"), 3)
            v.scalar_tensor_tensor(a_par[:, 1:2], a_par[:, 0:1], 0.0, a_par[:, 1:2], ALU.max, ALU.add).then_inc(sem("apar_ready"), 1)
            dve.wait_ge(sem("apar_ready"), 1)
            v.tensor_scalar(a_par[:, 2:3], a_par[:, 1:2], -8.0, None, ALU.mult).then_inc(sem("apar_ready"), 1)
            v.tensor_scalar(a_par[:, 3:4], a_par[:, 1:2], -16.0, None, ALU.mult).then_inc(sem("apar_ready"), 1)
            with dve.Fori(0, NB) as b:
                dve.wait_ge(sem("gx_ready"), b + 1)
                st = Steps("xg_step", b, 2)
                st.did(v.tensor_tensor(gx, gx, xw, ALU.mult))
                dve.wait_ge(sem("drv_ready"), b + 1)
                st.then(lambda: v.tensor_tensor(gx, gx, drv, ALU.mult))
                st.wait()
                st.end()
                v.tensor_tensor_scan(st3, dec, gx, 0.0, ALU.mult, ALU.add).then_inc(sem("state3_ready"), 1)
                dve.wait_ge(sem("attn_out3"), b + 1)
                v.scalar_tensor_tensor(x[:, b, :], bank(3), b_3[:, W_OUT:W_OUT + 1], x[:, b, :], ALU.add, ALU.add).then_inc(x_ready, 1)

            layer_norm(FFN3)
            clear_logits(FFN3, 3)
            v.memset(wparts[:], 0.0).then_inc(sem("wparts_cleared"), 1)
            dve.wait_ge(sem("wparts_cleared"), 1)
            with dve.Fori(0, NB) as b:
                dve.wait_ge(sem("route_logits_turned"), turn(3, b) + 1)
                st = Steps("r3_step", b, 15)
                two_best(st, E3, lambda t: psum[:, 1, t * P:t * P + E3])
                for t in range(TT):
                    i, at = best(E3, t, 0)
                    st.did(v.tensor_scalar(chosen[:, t, 0:E3], i, at, None, ALU.is_equal))
                st.wait()
                st.end()
                for t in range(TT):
                    i, at = best(E3, t, 1)
                    m = v.scalar_tensor_tensor(weight[:, t, 0:E3], i, at, chosen[:, t, 0:E3], ALU.is_equal, ALU.add)
                m.then_inc(sem("route_weights"), 1)
                dve.wait_ge(sem("route_weights_turned"), turn(3, b) + 1)
                v.tensor_copy(sel3[0:E3, :], psum[0:E3, 3, :])
                v.tensor_copy(wparts[0:E3, :], psum[0:E3, 3, :]).then_inc(sem("route_parts"), 1)
                for e in range(E3):
                    r = e % 2
                    dve.wait_ge(sem("w3_spread"), b * E3 + e + 1)
                    if e >= 2:
                        dve.wait_ge(sem("y3_added"), b * E3 + e - 1)
                    v.tensor_tensor(picked[:, r, :], h[:, b, :], bank(4 + r), ALU.mult).then_inc(sem("picked_ready"), 1)
                dve.wait_ge(sem("y3_added"), b * E3 + E3)
                add_to_x(b, 7)


N_CLEARED = 18
N_FFN1 = 3 + 2 + 4 + 6 + 2 + 2 + 1


def kernel(**inputs):
    import concourse.bacc as bacc
    from concourse.bass_utils import run_bass_kernel_spmd

    nc = bacc.Bacc("TRN2", target_bir_lowering=False, num_devices=1)
    arrays = {name: np.ascontiguousarray(value) for name, value in {**inputs, **shape_constants()}.items()}
    args = {name: nc.dram_tensor(name, value.shape, mybir.dt.from_np(value.dtype), kind="ExternalInput").ap()
            for name, value in arrays.items()}
    out = nc.dram_tensor("out", (NTOK, D), F32, kind="ExternalOutput").ap()
    build(nc, args, out)
    result = run_bass_kernel_spmd(nc, [arrays], core_ids=[0])
    return result.results[0]["out"].reshape(NB, S, D)
```

```python
from contextlib import ExitStack

import numpy as np
import concourse.bass as bass
from concourse import mybir

F32 = mybir.dt.float32
BF16 = mybir.dt.bfloat16
U32 = mybir.dt.uint32
ALU = mybir.AluOpType
ACT = mybir.ActivationFunctionType
AX = mybir.AxisListType

P = 128
D = 128
NB, S = 4, 512
TT = S // P
NT = NB * TT
NTOK = NB * S
EPS = 1e-5

DEPTH, LEAF_W = 4, 64
LEAVES, NODES = 2 ** DEPTH, 2 ** DEPTH - 1
HCH = LEAVES * LEAF_W // P
OFF_PATH = 2.0 ** 60
SCALE0 = float(np.float32(1.0) / np.sqrt(D).astype(np.float32))
HEADS, DH = 16, 8
SCALE1 = float(DH ** (-0.25))
GROUPS = HEADS // 4
PARTS = 3
MROW = PARTS * PARTS * DH
KSTACK = 96
E1, F1, K1 = 16, 176, 2
F1R = F1 - P
CAP = int(np.ceil(1.25 * NTOK * K1 / E1))
NPAIR = E1 // 2
PT = 2 * CAP // P
SKIP = float(1 << 20)
NSTATE, DCONV = 16, 4
E2, H2 = 8, 256
E3 = 8

TREES = ("q", "k", "v")


def shape_constants():
    bf = mybir.dt.np(BF16)
    eye = np.eye(P, dtype=np.float32)
    center = (eye - np.float32(1.0 / D)).astype(np.float32)
    mean = np.full((P, P), 1.0 / D, np.float32)
    ones = np.ones((P, P), np.float32)
    path = np.zeros((P, 3, LEAVES), np.float32)
    for leaf in range(LEAVES):
        node = 0
        for step in range(DEPTH):
            bit = leaf >> (DEPTH - 1 - step) & 1
            for f in range(3):
                path[32 * f + node, f, leaf] = 1.0 if bit else -1.0
                if not bit:
                    path[32 * f + NODES, f, leaf] += 1.0
            node = 2 * node + 1 + bit
        path[[32 * f + NODES for f in range(3)], range(3), leaf] -= DEPTH
    leafpath = np.zeros((P, P), np.float32)
    for f in range(3):
        leafpath[:, 32 * f:32 * f + LEAVES] = path[:, f]
    offpath = np.zeros((P, 3, HCH, P), np.float32)
    for c in range(HCH):
        for row in range(P):
            offpath[:, :, c, row] = path[:, :, 2 * c + row // LEAF_W] * OFF_PATH
    pick = np.zeros((KSTACK, 32, P), np.float32)
    for n in range(32):
        pick[[n, 32 + n, 64 + n], n] = 1.0
    sumrow = np.zeros((P, 4), np.float32)
    sumrow[[32 * j + DH for j in range(4)], range(4)] = 1.0
    before = np.triu(np.ones((P, P), np.float32), 1)
    iota = np.broadcast_to(np.arange(16, dtype=np.float32), (P, 16)).copy()
    return {
        "c_eye": eye, "c_center": center, "c_mean": mean, "c_ones": ones, "c_leafpath": leafpath.astype(bf),
        "c_offpath": offpath.astype(bf), "c_pick": pick.astype(bf), "c_sumrow": sumrow,
        "c_before": before.astype(bf), "c_iota": iota,
    }


def build(nc, a, out):
    with ExitStack() as ctx:
        held = {}
        ctx.enter_context(nc.allow_non_contiguous_dma(reason="a bias goes one element to a partition"))

        def sb(name, shape, dt=F32):
            return ctx.enter_context(nc.sbuf_tensor("sb_" + name, shape, dt))

        def sem(name):
            if name not in held:
                held[name] = ctx.enter_context(nc.semaphore(name))
            return held[name]

        psum = ctx.enter_context(nc.psum_tensor("psum", [P, 8, S], F32))
        x = sb("x", [P, NB, S])
        h = sb("h", [P, NB, S])
        eye, center, mean, ones = (sb(n, [P, P]) for n in ("eye", "center", "mean", "ones"))
        sumrow, before, iota = sb("sumrow", [P, 4]), sb("before", [P, P], BF16), sb("iota", [P, 16])
        ones_b = sb("ones_b", [P, P], BF16)
        eye_b = sb("eye_b", [P, P], BF16)
        leafpath = sb("leafpath", [P, P], BF16)
        offpath = sb("offpath", [P, 3, HCH, P], BF16)
        pick = sb("pick", [KSTACK, 32, P], BF16)
        eps = sb("eps", [P, 1])
        one = sb("one", [P, 1])

        WV0, WO0, WQ1, WK1, WV1, WO1, WX2, WZ2, WOUT2, WSSM, WROUT3, WNODE = range(12)
        wT = sb("wT", [P, 12, D])
        nodeT = wT[:, WNODE, :]

        WIDE = sb("wide", [P, 6 * LEAVES * LEAF_W])
        w1 = [WIDE[:, f * 1024:(f + 1) * 1024] for f in range(3)]
        w2 = [WIDE[:, (3 + f) * 1024:(4 + f) * 1024].rearrange("p (c o) -> p c o", c=HCH) for f in range(3)]
        w1_2 = WIDE[:, 0:2048].rearrange("p (e n) -> p e n", e=E2)
        w2_2 = WIDE[:, 2048:4096].rearrange("p (e n) -> p e n", e=E2)
        w3_2 = WIDE[:, 4096:6144].rearrange("p (e k n) -> p e k n", e=E2, k=2)
        b1 = sb("b1", [P, 3, HCH])
        b2 = sb("b2", [P, 3, D])
        node_b = sb("node_b", [P, 1])

        woT = sb("woT", [P, GROUPS, D])
        bout1 = sb("bout1", [P, 1])
        router1, router1_row = sb("router1", [P, E1]), sb("router1_row", [P, E1])
        shared_gate_up = sb("shared_gate_up", [P, 2 * F1])
        shared_down = sb("shared_down", [P, 2, D])
        gate_up, down_ = sb("gate_up", [P, 2, 2, 2 * F1]), sb("down", [P, 2, 2, 2, D])
        v32 = sb("v32", [P, TT, HEADS, 32])
        qstack = sb("qstack", [P, HEADS, S], BF16)
        kstack = sb("kstack", [P, HEADS, S], BF16)

        conv_w, conv_b = sb("conv_w", [P, DCONV]), sb("conv_b", [P, 1])
        dt_w, dt_b = sb("dt_w", [P, 1]), sb("dt_b", [P, 1])
        a_neg = sb("a_neg", [P, NSTATE])
        dt_rep = sb("dt_rep", [P, P])
        wg2 = sb("wg2", [P, E2])

        W_IN, W_GX, W_GA, W_OUT = range(4)
        w_3 = sb("w_3", [P, 4, D])
        b_3 = sb("b_3", [P, 4])
        a_par = sb("a_par", [P, 4])
        w_e3 = sb("w_e3", [P, E3, D])
        bias3 = sb("bias3", [P, D])
        router3_b = sb("router3_b", [P, 1])

        prob = sb("prob", [P, TT, 16])
        top = sb("top", [P, TT, 8])
        top_at = sb("top_at", [P, TT, 8], U32)
        top_f = sb("top_f", [P, TT, 8])
        chosen = sb("chosen", [P, TT, 16])
        weight = sb("weight", [P, TT, 16])
        small = sb("small", [P, 8, TT])
        ln_std_t, ln_rstd_t = sb("ln_std_t", [P, NB, TT]), sb("ln_rstd_t", [P, NB, TT])
        wparts = sb("wparts", [KSTACK, S], BF16)

        SCR = 12800
        scr = sb("scr", [P, SCR])

        def view(at, n, dt=F32):
            return scr[:, at:at + n] if dt is F32 else scr[:, at:at + n].bitcast(dt)

        squares = view(0, 2 * S).rearrange("p (r s) -> p r s", r=2)
        centered = view(2 * S, NB * S).rearrange("p (b s) -> p b s", b=NB)
        diag = view(6 * S, 2 * S).rearrange("p (r s) -> p r s", r=2)
        wraw = view(4096, 12 * D).rearrange("p (n d) -> p n d", n=12)

        rows = view(8192, NB * TT * D).rearrange("p (t d) -> p t d", d=D)
        part_r, lt = view(10244, S)[0:32], view(10756, S)
        part_b = view(11268, S // 2, BF16)[0:32]
        hidden = view(0, HCH * S).rearrange("p (c s) -> p c s", c=HCH)
        qT0, kT0, v0 = view(4096, S), view(4608, S), view(5120, S)
        probs0 = view(5632, 2 * S).rearrange("p (r s) -> p r s", r=2)
        probsT0 = view(6656, TT * S).rearrange("p (k s) -> p k s", k=TT)
        gates = view(8704, S // 2, BF16)
        leaf = view(8960, S)
        token_sum, value_sum, attn0 = (sb(n, [P, NB]) for n in ("token_sum", "value_sum", "attn0"))

        expT = view(0, 4096).rearrange("p (r j s) -> p r j s", r=2, j=4)
        qparts = view(4096, 768, BF16).rearrange("p (i s) -> p i s", i=PARTS)
        kparts = view(4864, 768, BF16).rearrange("p (i s) -> p i s", i=PARTS)
        qrem, krem = view(5632, S), view(6144, S)
        vT1, vtok = view(6656, S), view(7168, S).rearrange("p (t h d) -> p t h d", t=TT, h=HEADS)
        headmax = view(7680, 2 * TT * 4).rearrange("p (r t j) -> p r t j", r=2, t=TT)
        maxrem = view(7712, 2 * TT * 4).rearrange("p (r t j) -> p r t j", r=2, t=TT)
        maxparts = view(7744, TT * PARTS * 4, BF16).rearrange("p (r t i j) -> p r t i j", r=2, t=TT, i=PARTS)
        sum_inv = view(7792, TT * 4).rearrange("p (t j) -> p t j", t=TT)
        max_rows = view(7808, S, BF16).rearrange("p (r s) -> p r s", r=2)
        head_raw, head_out = view(8320, S), view(8832, S)
        inv_rows = view(9344, S).rearrange("p (t j c) -> p t j c", t=TT, j=4)

        gact0 = view(0, 2 * S).rearrange("p (r s) -> p r s", r=2)
        prod0 = view(2048, 2 * S).rearrange("p (r s) -> p r s", r=2)
        hid0 = view(4096, 2 * S).rearrange("p (r s) -> p r s", r=2)

        def by_expert(at):
            return view(at, NT * E1).rearrange("p (t e) -> p t e", t=NT)

        def by_choice(n, dt=F32):
            return view(5632 + n * K1 * NT, K1 * NT, dt).rearrange("p (k t) -> p k t", k=K1)

        prob1, first1, second1, place_first, place_second = (by_expert(4096 + 256 * n) for n in range(5))
        top1 = view(5376, NT * 8).rearrange("p (t k) -> p t k", t=NT)
        top1_at = view(5504, NT * 8, U32).rearrange("p (t k) -> p t k", t=NT)
        expert_at, place, beyond, base, scatter_f, gather_f, pair_weight = (by_choice(n) for n in range(7))
        scatter_at, gather_at = by_choice(7, U32), by_choice(8, U32)
        peak1, sum1, sum1_inv = (view(5920 + NT * n, NT) for n in range(3))
        chosen1 = view(6016, NT * E1 // 2, BF16).rearrange("p (t e) -> p t e", t=NT)
        h_rows = view(6208, NT * D).rearrange("p (t d) -> p t d", t=NT)
        gathered = view(6208, 2 * NT * D).rearrange("p (t k d) -> p t k d", t=NT, k=K1)
        shared_act0, shared_act1, shared_hid0, shared_hid1 = (view(8256 + S * n, S) for n in range(4))
        x_in = view(10304, 2 * PT * D).rearrange("p (r t d) -> p r t d", r=2, t=PT)
        xT_in = view(11584, 2 * P).rearrange("p (r t) -> p r t", r=2)
        gate_act = view(11840, 2 * F1).rearrange("p (r f) -> p r f", r=2)
        hid_rows = view(12192, 4 * P).rearrange("p (r f) -> p r f", r=2)
        hidT = view(0, 4 * P).rearrange("p (r f t) -> p r f t", r=2, f=2)
        y_rows = view(512, 2 * PT * D).rearrange("p (r t d) -> p r t d", r=2, t=PT)
        zeros = view(10240, 2560)

        xpad = view(0, S + DCONV)
        conv = view(516, S)
        xconv = view(1028, S)
        zgate = view(1540, S)
        dtv, dtl, dt = view(2052, S), view(2564, S), view(3076, S)
        dtx = view(3588, S)
        bcast_b = view(4612, 2 * S).rearrange("p (r s) -> p r s", r=2)
        decay = view(5636, 2 * S).rearrange("p (r s) -> p r s", r=2)
        drive = view(6660, 2 * S).rearrange("p (r s) -> p r s", r=2)
        state = view(7684, 2 * S).rearrange("p (r s) -> p r s", r=2)
        read = view(8708, 2 * S).rearrange("p (r s) -> p r s", r=2)
        ygate = view(9732, S)

        xw, gx, ga, dec, drv, st3 = (view(n * S, S) for n in range(6))
        sel3 = view(0, S)
        picked = view(512, 2 * S).rearrange("p (r s) -> p r s", r=2)

        q_bounce = nc.dram_tensor("q_bounce", [HEADS, PARTS, DH, S], BF16, kind="Internal").ap()
        k_bounce = nc.dram_tensor("k_bounce", [HEADS, PARTS, DH, S], BF16, kind="Internal").ap()

        expert_in = nc.dram_tensor("expert_in", [E1 * CAP, D], F32, kind="Internal").ap()
        expert_out = nc.dram_tensor("expert_out", [E1 * CAP, D], F32, kind="Internal").ap()

        x_ready, ln_done = sem("x_ready"), sem("ln_done")
        GTILES = 4 * TT
        STACKS, BOUNCES = 16 * PARTS * (1 + PARTS), 16 * 2 * PARTS
        stacked, max_stacked = ([sem(f"{n}{g}") for g in range(GROUPS)] for n in ("stacked", "max_stacked"))
        PAIR_LOADS = 16 * 5
        gathered_sem, x_loaded, y_stored = ([sem(f"{n}{g}") for g in range(m)] for n, m in
                                            (("gathered", NB), ("x_loaded", 2), ("y_stored", 2)))
        ATTN0, FFN0, ATTN1, FFN1, ATTN2, FFN2, ATTN3, FFN3 = range(8)

        def x_before(stage):
            return NB * (stage + 1)

        def outs_before(stage):
            return NB * (FFN0, FFN1, ATTN2, ATTN3).index(stage)

        setup = sem("setup")
        SETUP = ("eye_b", "hid1", "logits1", "chosen1", "places1", "dt_rep", "a_neg", "xpad", "logits2", "apar", "apar_8", "apar_16", "logits3", "wparts")

        def turn(k, b):
            return b + NB * (k - 1)

        def run_tiles(engine, steps):
            per = 2 * PT

            def turn_of(u, begin):
                for c in range(per):
                    for k, step in enumerate(steps):
                        if step is None:
                            continue
                        if c >= k:
                            step(u, c - k, per * u + c - k, begin)
                        elif not begin:
                            step(u - 1, per + c - k, per * (u - 1) + per + c - k, False)

            turn_of(0, True)
            with engine.Fori(1, E1 // 4) as u:
                turn_of(u, False)
            last = E1 // 4 - 1
            for c in range(len(steps) - 1):
                for k, step in enumerate(steps):
                    if step is not None and k > c:
                        step(last, per + c - k, per * last + per + c - k, False)

        block = ctx.enter_context(nc.Block())

        @block.sync
        def _(sp):
            sp.dma_start(eye[:], a["c_eye"]).then_inc(sem("input_loaded"), 16)
            xr = a["L0_attn_x"].rearrange("b (t p) d -> p (b t) d", p=P)
            sp.dma_start(rows, xr).then_inc(sem("input_loaded"), 16)
            for t, n in ((center, "c_center"), (mean, "c_mean"), (ones, "c_ones")):
                sp.dma_start(t[:], a[n]).then_inc(sem("ln_consts"), 16)
            sp.wait_ge(sem("cleared"), 3)
            square = {WV0: a["L0_attn_w_qkv"][2 * D:3 * D, :], WO0: a["L0_attn_w_o"], WQ1: a["L1_attn_Wq"], WK1: a["L1_attn_Wk"],
                      WV1: a["L1_attn_Wv"], WO1: a["L1_attn_Wout"], WX2: a["L2_attn_in_proj_w"][0:D, :],
                      WZ2: a["L2_attn_in_proj_w"][D:2 * D, :], WOUT2: a["L2_attn_out_proj_w"], WSSM: a["L2_attn_x_proj_w"],
                      WROUT3: a["L3_ffn_router_weight"]}
            for n, src in square.items():
                sp.dma_start(wraw[0:src.shape[0], n, :], src).then_inc(sem("wraw_loaded"), 16)
            for f, name in enumerate(TREES):
                sp.dma_start(wraw[32 * f:32 * f + NODES, WNODE, :], a[f"L0_ffn_{name}_node_w"]).then_inc(sem("wraw_loaded"), 16)

            def column(name):
                return a[name].rearrange("(n o) -> n o", o=1)

            def load(group, dst, src):
                sp.dma_start(dst, src).then_inc(sem(group), 16)

            load("trees_loaded", leafpath[:], a["c_leafpath"])
            load("trees_loaded", offpath[:], a["c_offpath"])
            for f, name in enumerate(TREES):
                load("trees_loaded", node_b[32 * f:32 * f + NODES, :], column(f"L0_ffn_{name}_node_b"))
                load("trees_loaded", b2[32 * f:32 * f + LEAVES, f, :], a[f"L0_ffn_{name}_b2"])
                load("trees_loaded", b1[:, f, :], a[f"L0_ffn_{name}_b1"].rearrange("(c t) h -> (t h) c", t=2))
                load("trees_loaded", w1[f].rearrange("p (l h) -> p l h", h=LEAF_W), a[f"L0_ffn_{name}_w1"].rearrange("l d h -> d l h"))
                load("trees_loaded", w2[f], a[f"L0_ffn_{name}_w2"].rearrange("(c t) h o -> (t h) c o", t=2))
            load("attn1_loaded", sumrow[:], a["c_sumrow"])
            sp.wait_ge(sem("cleared"), N_CLEARED)
            load("attn1_loaded", bout1[:], column("L1_attn_bout"))
            load("ffn1_loaded", before[:], a["c_before"])
            load("ffn1_loaded", iota[:], a["c_iota"])
            load("ffn1_loaded", pick[:], a["c_pick"])
            load("ffn1_loaded", router1[:], a["L1_ffn_router_w"])
            load("ffn1_loaded", router1_row[0:1, :], a["L1_ffn_router_b"].rearrange("(o n) -> o n", o=1))
            for at, n in ((0, "gate"), (F1, "up")):
                load("ffn1_loaded", shared_gate_up[:, at:at + F1], a[f"L1_ffn_sw_{n}"])
            for k, (lo, hi) in enumerate(((0, P), (P, F1))):
                load("ffn1_loaded", shared_down[0:hi - lo, k, :], a["L1_ffn_sw_down"][lo:hi])
            table = expert_in.rearrange("(n p r) d -> n p (r d)", n=2, p=P)
            for n in range(2):
                sp.dma_start(table[n], zeros).then_inc(sem("table_cleared"), 16)
            load("attn2_loaded", conv_w[:], a["L2_attn_conv_w"].rearrange("d o k -> d (o k)"))
            load("attn2_loaded", conv_b[:], column("L2_attn_conv_b"))
            load("attn2_loaded", dt_w[:], a["L2_attn_dt_proj_w"])
            load("attn2_loaded", dt_b[:], column("L2_attn_dt_proj_b"))
            load("attn2_loaded", a_neg[:], a["L2_attn_A_log"])
            for n, name in enumerate(("in", "gx", "ga", "out")):
                load("attn3_loaded", w_3[:, n, :], a[f"L3_attn_W_{name}"])
                load("attn3_loaded", b_3[:, n:n + 1], column(f"L3_attn_b_{name}"))
            load("attn3_loaded", a_par[:, 0:1], column("L3_attn_a_param"))
            load("ffn3_loaded", w_e3[:], a["L3_ffn_weight"].rearrange("e d n -> d e n"))
            load("ffn3_loaded", bias3[0:E3, :], a["L3_ffn_bias"])
            load("ffn3_loaded", router3_b[0:E3, :], column("L3_ffn_router_bias"))
            sp.wait_ge(sem("wT_ready"), 3)
            for g in range(GROUPS):
                for j in range(4):
                    head = 4 * g + j
                    load("woT_ready", woT[32 * j:32 * j + DH, g, :], wT[head * DH:(head + 1) * DH, WO1, :])

            def bounce(b):
                sp.wait_ge(sem("kparts_ready"), b + 1)
                for i in range(PARTS):
                    sp.dma_start(q_bounce[:, i], qparts[:, i, :]).then_inc(sem("bounced"), 16)
                    sp.dma_start(k_bounce[:, i], kparts[:, i, :]).then_inc(sem("bounced"), 16)
                sp.wait_ge(sem("bounced"), (b + 1) * BOUNCES)

            def stack(b, g):
                hs = slice(4 * g, 4 * g + 4)
                for j in range(PARTS):
                    rows_j = slice(PARTS * DH * j, PARTS * DH * (j + 1))
                    sp.dma_start(qstack[rows_j, hs, :], q_bounce[hs].rearrange("h i d s -> (i d) h s")).then_inc(stacked[g], 16)
                    for i in range(PARTS):
                        r = DH * (PARTS * j + i)
                        sp.dma_start(kstack[r:r + DH, hs, :], k_bounce[hs, j].rearrange("h d s -> d h s")).then_inc(stacked[g], 16)

            def stack_maxima(b, g):
                n = GROUPS * b + g
                sp.wait_ge(sem("max_rows_ready"), n + 1)
                for i in range(PARTS):
                    sp.dma_start(qstack[96 + i:97 + i, 4 * g:4 * g + 4, :],
                                 max_rows[4 * i:4 * i + 4, g % 2, :]).then_inc(max_stacked[g], 16)

            def stack_batch(b, first, last):
                for g in range(GROUPS):
                    n = GROUPS * b + g
                    if g == 0 or not last:
                        if g >= 1 or not first:
                            sp.wait_ge(sem("scoresT1"), n * GTILES)
                        stack(b, 3) if g == 0 else stack(b + 1, g - 1)
                    if g < GROUPS - 1 or not last:
                        stack_maxima(*((b, g + 1) if g < GROUPS - 1 else (b + 1, 0)))
                    if g == 0 and not last:
                        bounce(b + 1)

            bounce(0)
            for g in range(GROUPS - 1):
                stack(0, g)
            stack_maxima(0, 0)
            stack_batch(0, True, False)
            with sp.Fori(1, NB - 1) as b:
                stack_batch(b, False, False)
            stack_batch(NB - 1, False, True)

            sp.wait_ge(x_ready, x_before(ATTN1))
            load("ffn2_loaded", w1_2, a["L2_ffn_W1"].rearrange("e d n -> d e n"))
            load("ffn2_loaded", w2_2, a["L2_ffn_W2"].rearrange("e d n -> d e n"))
            load("ffn2_loaded", w3_2, a["L2_ffn_W3"].rearrange("e (k p) n -> p e k n", p=P))
            load("ffn2_loaded", wg2[:], a["L2_ffn_Wg"])

            pair_in = expert_in.rearrange("(q t p) d -> q p t d", q=NPAIR, t=PT)
            pair_out = expert_out.rearrange("(q t p) d -> q p t d", q=NPAIR, t=PT)

            def load_experts(q):
                es, r = slice(2 * q, 2 * q + 2), q % 2
                for at, n in ((0, "gate"), (F1, "up")):
                    sp.dma_start(gate_up[:, r, :, at:at + F1], a[f"L1_ffn_w_{n}"][es].rearrange("e d f -> d e f")).then_inc(x_loaded[r], 16)
                for k, (lo, hi) in enumerate(((0, P), (P, F1))):
                    sp.dma_start(down_[0:hi - lo, r, :, k, :],
                                 a["L1_ffn_w_down"][es].rearrange("e f d -> f e d")[lo:hi]).then_inc(x_loaded[r], 16)

            for q in range(NPAIR + 2):
                if q >= 2:
                    sp.wait_ge(sem("y1_ready"), PT * (q - 1))
                    sp.dma_start(pair_out[q - 2], y_rows[:, q % 2]).then_inc(y_stored[q % 2], 16)
                if q < NPAIR:
                    load_experts(q)
                    if q == 0:
                        sp.wait_ge(sem("scattered"), 16 * K1 * NT)
                    sp.dma_start(x_in[:, q % 2], pair_in[q]).then_inc(x_loaded[q % 2], 16)

            orr = out.rearrange("(t p) d -> p t d", p=P)
            for b in range(NB):
                sp.wait_ge(sem("out_rows"), b + 1)
                sp.dma_start(orr[:, b * TT:(b + 1) * TT, :], rows[:, b * TT:(b + 1) * TT, :]).then_inc(sem("stored"), 16)
            sp.wait_ge(sem("stored"), 16 * NB)

        @block.gpsimd
        def _(pool):
            clears = [(wraw, 0.0), (b2[:], 0.0), (node_b[:], 0.0), (eps[:], EPS), (one[:], 1.0), (woT[:], 0.0),
                      (zeros, 0.0), (shared_down[:], 0.0), (down_[:], 0.0), (v32[:], 0.0), (qstack[64:P, :, :], 0.0), (kstack[64:96, :, :], 0.0),
                      (kstack[96:P, :, :], 1.0), (wparts[:], 0.0), (ones_b[:], 1.0), (bias3[:], 0.0), (router1_row[:], 0.0),
                      (router3_b[:], 0.0)]
            assert len(clears) == N_CLEARED - 1
            for n, (t, value) in enumerate(clears):
                if n >= 1:
                    pool.wait_ge(sem("cleared"), n)
                pool.memset(t, value).then_inc(sem("cleared"), 1)
            pool.wait_ge(sem("cleared"), N_CLEARED - 1)
            pool.memset(v32[:, :, :, DH], 1.0).then_inc(sem("cleared"), 1)

            pool.wait_ge(setup, SETUP.index("places1") + 1)
            pool.wait_ge(sem("h_rows_ready"), NB)
            pool.wait_ge(sem("table_cleared"), 32)
            for t in range(NT):
                for k in range(K1):
                    nc.gpsimd.indirect_dma_start(
                        out=expert_in, out_offset=bass.IndirectOffsetOnAxis(ap=scatter_at[:, k, t:t + 1], axis=0),
                        in_=h_rows[:, t, :], in_offset=None, bounds_check=E1 * CAP - 1, oob_is_err=False).then_inc(sem("scattered"), 16)
            for r in range(2):
                pool.wait_ge(y_stored[r], 16 * (NPAIR // 2))
            for t in range(NT):
                for k in range(K1):
                    nc.gpsimd.indirect_dma_start(
                        out=gathered[:, t, k, :], out_offset=None, in_=expert_out,
                        in_offset=bass.IndirectOffsetOnAxis(ap=gather_at[:, k, t:t + 1], axis=0)).then_inc(gathered_sem[t // TT], 16)

            with pool.Fori(0, NB) as b:
                for n in range(NSTATE):
                    r = n % 2
                    pool.wait_ge(sem("b_spread"), b * NSTATE + n + 1)
                    if n == 0:
                        pool.wait_ge(sem("dtx_ready"), b + 1)
                    if n >= 2:
                        pool.wait_ge(sem("scanned"), b * NSTATE + n - 1)
                    nc.gpsimd.tensor_tensor(drive[:, r, :], dtx, bcast_b[:, r, :], ALU.mult).then_inc(sem("drive_ready"), 1)

        @block.tensor
        def _(pe):
            def bank(n, m=S):
                return psum[:, n, 0:m]

            def mm(out_, w, r, start=True, stop=True, **kw):
                return nc.tensor.matmul(out_, w, r, start=start, stop=stop, **kw)

            def layer_norm(s):
                n = NB * s

                def subtract_mean(b):
                    pe.wait_ge(x_ready, n + b + 1)
                    if b >= 2:
                        pe.wait_ge(sem("ln_squared"), n + b - 1)
                    mm(bank(b % 2), center[:], x[:, b, :]).then_inc(sem("ln_centered"), 1)

                def variance(b):
                    pe.wait_ge(sem("ln_squared"), n + b + 1)
                    if b >= 2:
                        pe.wait_ge(sem("ln_std"), n + b - 1)
                    for t in range(TT):
                        m = mm(psum[:, 2 + b % 2, t:t + 1], squares[:, b % 2, t * P:(t + 1) * P], mean[:, 0:1],
                               skip_group_check=True)
                    m.then_inc(sem("ln_var"), 1)

                def spread_rstd(b):
                    pe.wait_ge(sem("ln_diag"), n + b + 1)
                    if b >= 2:
                        pe.wait_ge(ln_done, n + b - 1)
                    mm(bank(4 + b % 2), ones[:], diag[:, b % 2, :]).then_inc(sem("ln_spread"), 1)

                if s == 0:
                    pe.wait_ge(sem("ln_consts"), 48)
                    pe.wait_ge(x_ready, NB)
                    pe.wait_ge(sem("wT_ready"), 3)
                for b in range(NB + 2):
                    if b < NB:
                        subtract_mean(b)
                    if 1 <= b <= NB:
                        variance(b - 1)
                    if b >= 2:
                        spread_rstd(b - 2)

            def stage_norm(s):
                layer_norm(s)
                pe.wait_ge(ln_done, NB * s + NB)

            pe.wait_ge(sem("input_loaded"), 32)
            for b in range(NB):
                for t in range(TT):
                    m = nc.tensor.transpose(psum[:, b, t * P:(t + 1) * P], rows[:, b * TT + t, :], eye[:])
                m.then_inc(sem("x_turned"), 1)
            pe.wait_ge(sem("wraw_loaded"), 16 * (11 + 3))
            for k in range(3):
                for t in range(4):
                    m = nc.tensor.transpose(psum[:, 4 + k, t * P:(t + 1) * P], wraw[:, 4 * k + t, :], eye[:])
                m.then_inc(sem("w_turned"), 1)

            stage_norm(ATTN0)
            pe.wait_ge(sem("wT_ready"), 3)
            pe.wait_ge(sem("token_sums"), 1)
            mm(psum[:, 0, 0:NB], wT[:, WV0, :], token_sum[:]).then_inc(sem("attn0_mm"), 1)
            pe.wait_ge(sem("attn0_out"), 1)
            mm(psum[:, 1, 0:NB], wT[:, WO0, :], value_sum[:]).then_inc(sem("attn0_mm"), 1)

            stage_norm(FFN0)
            pe.wait_ge(sem("trees_loaded"), 16 * (2 + 15))
            n_hid = 3 * HCH
            with pe.Fori(0, NB) as b:
                pe.wait_ge(x_ready, b + x_before(FFN0))
                mm(bank(6), nodeT, h[:, b, :]).then_inc(sem("nodes0"), 1)
                pe.wait_ge(sem("path_ready"), 2 * b + 1)
                mm(bank(7), leafpath[:], gates).then_inc(sem("nodes0"), 1)

                def out_of(i):
                    f, c = divmod(i, HCH)
                    pe.wait_ge(sem("hid_act" if i % 2 == 0 else "hid_dve"), b * (n_hid // 2) + i // 2 + 1)
                    if f < 2:
                        m = mm(bank(3 + f), w2[f][:, c, :], hidden[:, c, :], c == 0, False)
                    else:
                        for t in range(TT):
                            m = mm(psum[:, 5, t * D:(t + 1) * D], hidden[:, c, t * P:(t + 1) * P], w2[f][:, c, :],
                                   c == 0 and t == 0, False, skip_group_check=True)
                    if c < HCH - 1:
                        return
                    if i == HCH - 1:
                        pe.wait_ge(sem("path_ready"), 2 * b + 2)
                    if f < 2:
                        m = mm(bank(3 + f), b2[:, f, :], leaf, False, True)
                    else:
                        for t in range(TT):
                            m = mm(psum[:, 5, t * D:(t + 1) * D], leaf[:, t * P:(t + 1) * P], b2[:, f, :],
                                   False, t == TT - 1, skip_group_check=True)
                    m.then_inc(sem("tree_out"), 1)

                for i in range(n_hid):
                    f, c = divmod(i, HCH)
                    if i >= 3:
                        pe.wait_ge(sem("hid_act" if (i - 3) % 2 == 0 else "hid_dve"), b * (n_hid // 2) + (i - 3) // 2 + 1)
                    mm(bank(i % 3), w1[f][:, c * P:(c + 1) * P], h[:, b, :], True, False)
                    mm(bank(i % 3), offpath[:, f, c, :], gates, False, True).then_inc(sem("hidden0"), 1)
                    if i >= 2:
                        out_of(i - 2)
                out_of(n_hid - 2)
                out_of(n_hid - 1)
                pe.wait_ge(sem("qkv0_ready"), b * 3 + 2)
                for t in range(TT):
                    if t >= 2:
                        pe.wait_ge(sem("exp0"), b * TT + t - 1)
                    mm(bank(t % 2), qT0[:, t * P:(t + 1) * P], kT0).then_inc(sem("scores0"), 1)

                    def attend(t):
                        pe.wait_ge(sem("probs0"), b * TT + t + 1)
                        if t >= 2:
                            pe.wait_ge(sem("probsT0"), b * TT + t - 1)
                        for k in range(TT):
                            m = nc.tensor.transpose(psum[:, (2, 6)[t % 2], k * P:(k + 1) * P], probs0[:, t % 2, k * P:(k + 1) * P], eye[:])
                        m.then_inc(sem("probs_turned0"), 1)

                    if t >= 1:
                        attend(t - 1)
                attend(TT - 1)
                pe.wait_ge(sem("probsT0"), b * TT + TT)
                pe.wait_ge(sem("qkv0_ready"), b * 3 + 3)
                for k in range(TT):
                    m = mm(bank(7), v0[:, k * D:(k + 1) * D], probsT0[:, k, :], k == 0, k == TT - 1)
                m.then_inc(sem("batch_out"), 1)

            def project_q(b):
                mm(bank(6), wT[:, WQ1, :], h[:, b, :]).then_inc(sem("qkv1_done"), 1)

            def project_k(b):
                pe.wait_ge(sem("qparts_ready"), b + 1)
                mm(bank(6), wT[:, WK1, :], h[:, b, :]).then_inc(sem("qkv1_done"), 1)

            def project_v(b):
                pe.wait_ge(sem("kparts_ready"), b + 1)
                mm(bank(6), wT[:, WV1, :], h[:, b, :]).then_inc(sem("qkv1_done"), 1)

            def turn_v(b):
                pe.wait_ge(sem("vT_ready"), b + 1)
                for t in range(TT):
                    m = nc.tensor.transpose(psum[:, 6, t * P:(t + 1) * P], vT1[:, t * P:(t + 1) * P], eye[:])
                m.then_inc(sem("v_turned"), 1)

            def score_for_max(b, g, i, first):
                j, t = divmod(i, TT)
                n = GROUPS * b + g
                if i == 0:
                    pe.wait_ge(stacked[g], (b + 1) * STACKS)
                if i >= 2 or not first:
                    pe.wait_ge(sem("maxed"), n * GTILES + i - 1)
                mm(bank(i % 2), qstack[0:96, 4 * g + j, t * P:(t + 1) * P], kstack[0:96, 4 * g + j, :]).then_inc(sem("scores1"), 1)

            def turn_maxima(b, g):
                n = GROUPS * b + g
                pe.wait_ge(sem("maxparts_ready"), n + 1)
                for t in range(TT):
                    m = mm(psum[0:4 * PARTS, 6, t * P:(t + 1) * P], maxparts[:, g % 2, t].rearrange("p i j -> p (i j)"), eye_b[:],
                           skip_group_check=True)
                m.then_inc(sem("max_turned"), 1)

            def score(b, g, i, first):
                kt, j = divmod(i, 4)
                n = GROUPS * b + g
                if i == 0:
                    pe.wait_ge(max_stacked[g], (b + 1) * 16 * PARTS)
                if i >= 2 or not first:
                    pe.wait_ge(sem("exp1"), n * GTILES + i - 1)
                mm(bank(2 + i % 2), kstack[:, 4 * g + j, kt * P:(kt + 1) * P], qstack[:, 4 * g + j, :]).then_inc(sem("scoresT1"), 1)

            def values(b, g, kt, first):
                n = GROUPS * b + g
                pe.wait_ge(sem("exp1"), n * GTILES + 4 * kt + 4)
                if kt == 0:
                    pe.wait_ge(sem("v_ready"), n + 1)
                    if not first:
                        pe.wait_ge(sem("head_raw_ready"), n)
                for j in range(4):
                    m = mm(psum[32 * j:32 * j + 32, 4, :], v32[:, kt, 4 * g + j, :], expT[:, kt % 2, j, :],
                           kt == 0, kt == TT - 1, tile_position=(0, 32 * j))
                m.then_inc(sem("keys_added"), 1)

            def sum_by_token(b, g):
                n = GROUPS * b + g
                pe.wait_ge(sem("head_raw_ready"), n + 1)
                if not (isinstance(b, int) and n == 0):
                    pe.wait_ge(sem("head_out_ready"), n)
                for t in range(TT):
                    m = mm(psum[:, 5, 4 * t:4 * t + 4], head_raw[:, t * P:(t + 1) * P], sumrow[:], skip_group_check=True)
                m.then_inc(sem("sums_by_token"), 1)

            def spread_inverse(b, g):
                n = GROUPS * b + g
                pe.wait_ge(sem("inv_rows_ready"), n + 1)
                for t in range(TT):
                    m = mm(psum[:, 5, t * P:(t + 1) * P], inv_rows[:, t].rearrange("p j c -> p (j c)"), eye[:], skip_group_check=True)
                m.then_inc(sem("inverse_spread"), 1)

            def project(b, g):
                n = GROUPS * b + g
                pe.wait_ge(sem("head_out_ready"), n + 1)
                if g == 0:
                    pe.wait_ge(x_ready, b + x_before(ATTN1))
                mm(bank(7), woT[:, g, :], head_out, g == 0, g == GROUPS - 1).then_inc(sem("attn_out1"), 1)

            def attend_batch(b, first, last):
                for g in range(GROUPS):
                    begin = first and g == 0
                    prev = (b, g - 1) if g >= 1 else (b - 1, GROUPS - 1)
                    ahead = (b, g + 2) if g < 2 else (b + 1, g - 2)
                    for kt in range(TT):
                        for j in range(4):
                            i = 4 * kt + j
                            score(b, g, i, begin)
                            if g < 2 or not last:
                                score_for_max(*ahead, i, False)
                            if j == 1 and kt >= 1:
                                values(b, g, kt - 1, begin)
                            elif j == 1 and not begin:
                                values(*prev, TT - 1, False)
                        if kt == 0 and (g < GROUPS - 1 or not last):
                            if g == 2 and not last:
                                pe.wait_ge(sem("vtok_ready"), b + 2)
                            if g == 1 and not last:
                                pe.wait_ge(sem("kparts_ready"), b + 2)
                            turn_maxima(*((b, g + 1) if g < GROUPS - 1 else (b + 1, 0)))
                        if kt == 1 and not begin:
                            sum_by_token(*prev)
                        if kt == 2 and not begin:
                            spread_inverse(*prev)
                        if kt == 3 and not begin:
                            project(*prev)
                        if not last:
                            if g == 0 and kt == 1:
                                pe.wait_ge(sem("max_rows_ready"), GROUPS * b + 2)
                                project_q(b + 1)
                            if g == 0 and kt == 2:
                                project_k(b + 1)
                            if g == 1 and kt == 1:
                                pe.wait_ge(sem("max_rows_ready"), GROUPS * b + 3)
                                project_v(b + 1)
                            if g == 1 and kt == 3:
                                turn_v(b + 1)

            stage_norm(ATTN1)
            pe.wait_ge(sem("attn1_loaded"), 32)
            pe.wait_ge(sem("woT_ready"), 256)
            pe.wait_ge(setup, SETUP.index("eye_b") + 1)
            project_q(0)
            project_k(0)
            project_v(0)
            turn_v(0)
            for g in range(2):
                for i in range(GTILES):
                    score_for_max(0, g, i, g == 0)
                if g == 0:
                    pe.wait_ge(sem("vtok_ready"), 1)
                    turn_maxima(0, 0)
            attend_batch(0, True, False)
            with pe.Fori(1, NB - 1) as b:
                attend_batch(b, False, False)
            attend_batch(NB - 1, False, True)
            end = (NB - 1, GROUPS - 1)
            values(*end, TT - 1, False)
            sum_by_token(*end)
            spread_inverse(*end)
            project(*end)

            def turn_logits(k, b, n):
                pe.wait_ge(sem("route_logits"), turn(k, b) + 1)
                for t in range(TT):
                    m = nc.tensor.transpose(psum[:, 1, t * P:(t + 1) * P], lt[:, t * P:(t + 1) * P], eye[:])
                m.then_inc(sem("route_logits_turned"), 1)

            def turn_weights(k, b, n):
                pe.wait_ge(sem("route_weights"), turn(k, b) + 1)
                for t in range(TT):
                    m = nc.tensor.transpose(psum[0:n, 3, t * P:(t + 1) * P], weight[:, t, 0:n], eye[:])
                m.then_inc(sem("route_weights_turned"), 1)

            stage_norm(FFN1)
            pe.wait_ge(sem("ffn1_loaded"), 16 * N_FFN1)
            mm(psum[:, 0, 0:NT * E1].rearrange("p (t e) -> p t e", t=NT), ones[:],
               router1_row[:].unsqueeze(1).broadcast_to([P, NT, E1]), True, False, skip_group_check=True)
            for t in range(NT):
                m = mm(psum[:, 0, t * E1:(t + 1) * E1], h[:, t // TT, t % TT * P:(t % TT + 1) * P], router1[:], False, t == NT - 1,
                       skip_group_check=True)
            m.then_inc(sem("counted1"), 1)
            for b in range(NB):
                if b >= 2:
                    pe.wait_ge(sem("h_rows_ready"), b - 1)
                for t in range(TT):
                    m = nc.tensor.transpose(psum[:, 1 + b % 2, t * P:(t + 1) * P], h[:, b, t * P:(t + 1) * P], eye[:])
                m.then_inc(sem("h_turned"), 1)

            def shared(b):
                if b >= 1:
                    pe.wait_ge(sem("shared_hid"), b)
                for n, (lo, hi) in enumerate(((0, P), (P, F1), (F1, F1 + P), (F1 + P, 2 * F1))):
                    m = mm(psum[0:hi - lo, 3 + n, :], shared_gate_up[:, lo:hi], h[:, b, :])
                    if n % 2 == 1:
                        m.then_inc(sem("shared_up"), 1)
                if b >= 1:
                    pe.wait_ge(sem("shared_added"), b)
                mm(bank(7), eye[:], h[:, b, :], True, False)
                pe.wait_ge(sem("shared_hid"), b + 1)
                mm(bank(7), shared_down[:, 0, :], shared_hid0, False, False)
                mm(bank(7), shared_down[:, 1, :], shared_hid1, False, True).then_inc(sem("shared_out"), 1)

            shared(0)
            pe.wait_ge(setup, SETUP.index("chosen1") + 1)
            mm(psum[:, 0, 0:NT * E1], before[:], chosen1.rearrange("p t e -> p (t e)"), True, False, skip_group_check=True)
            for t in range(NT - 1):
                later = NT - 1 - t
                m = mm(psum[:, 0, (t + 1) * E1:NT * E1].rearrange("p (t e) -> p t e", t=later), ones_b[:],
                       chosen1[:, t, :].unsqueeze(1).broadcast_to([P, later, E1]), False, t == NT - 2, skip_group_check=True)
            m.then_inc(sem("counted1"), 1)
            for b in range(1, NB):
                shared(b)

            def tile(c):
                p, j = divmod(c, PT)
                if j == PT // 2:
                    return ((slice(0, P // 2), p, 0), (slice(P // 2, P), p, 1))
                return ((slice(0, P), p, j // (PT // 2 + 1)),)

            def turn_in(u, c, n, begin):
                r = c // PT
                if c % PT == 0:
                    pe.wait_ge(x_loaded[r], PAIR_LOADS * (u + 1))
                if c >= 2 or not begin:
                    pe.wait_ge(sem("xT1_ready"), n - 1)
                nc.tensor.transpose(psum[:, c % 2, 0:P], x_in[:, r, c % PT, :], eye[:]).then_inc(sem("x1_turned"), 1)

            def gate_and_up(u, c, n, begin):
                pe.wait_ge(sem("xT1_ready"), n + 1)
                if c >= 2 or not begin:
                    pe.wait_ge(sem("hid1_ready"), n - 1)
                for rows_, p, e in tile(c):
                    m = mm(psum[rows_, 2 + c % 2, 0:2 * F1], xT_in[:, c % 2, rows_], gate_up[:, p, e, :],
                           tile_position=(0, rows_.start))
                m.then_inc(sem("up1_done"), 1)

            def turn_hidden(u, c, n, begin):
                pe.wait_ge(sem("hid1_ready"), n + 1)
                if c >= 2 or not begin:
                    pe.wait_ge(sem("hidT1_ready"), n - 1)
                for k in range(2):
                    m = nc.tensor.transpose(psum[:, 4 + c % 2, k * P:(k + 1) * P], hid_rows[:, c % 2, k * P:(k + 1) * P], eye[:])
                m.then_inc(sem("hid1_turned"), 1)

            def down(u, c, n, begin):
                pe.wait_ge(sem("hidT1_ready"), n + 1)
                if c >= 2 or not begin:
                    pe.wait_ge(sem("y1_ready"), n - 1)
                for rows_, p, e in tile(c):
                    for k in range(2):
                        m = mm(psum[rows_, 6 + c % 2, 0:D], hidT[:, c % 2, k, rows_], down_[:, p, e, k, :], k == 0, k == 1,
                               tile_position=(0, rows_.start))
                m.then_inc(sem("y1_done"), 1)

            pe.wait_ge(sem("shared_added"), NB)
            run_tiles(pe, (turn_in, gate_and_up, turn_hidden, down))

            for b in range(NB):
                pe.wait_ge(sem("combined"), b + 1)
                if b >= 2:
                    pe.wait_ge(x_ready, x_before(FFN1) + b - 1)
                for t in range(TT):
                    m = nc.tensor.transpose(psum[:, 6 + b % 2, t * P:(t + 1) * P], gathered[:, b * TT + t, 0, :], eye[:])
                m.then_inc(sem("batch_out"), 1)

            stage_norm(ATTN2)
            pe.wait_ge(sem("ffn1_loaded"), 16 * N_FFN1)
            pe.wait_ge(setup, SETUP.index("dt_rep") + 1)
            with pe.Fori(0, NB) as b:
                pe.wait_ge(x_ready, b + x_before(ATTN2))
                mm(bank(0), wT[:, WX2, :], h[:, b, :])
                mm(bank(1), wT[:, WZ2, :], h[:, b, :]).then_inc(sem("proj2_done"), 1)
                pe.wait_ge(sem("xconv_ready"), b + 1)
                mm(bank(2), wT[:, WSSM, :], xconv)
                mm(bank(3), dt_rep[:], xconv).then_inc(sem("proj2_done"), 1)
                pe.wait_ge(sem("bc_parts"), b + 1)
                pe.wait_ge(sem("dtx_ready"), b + 1)

                def add_state(n):
                    pe.wait_ge(sem("read_ready"), b * NSTATE + n + 1)
                    mm(bank(6), eye[:], read[:, n % 2, :], n == 0, n == NSTATE - 1).then_inc(sem("y_added"), 1)

                for n in range(NSTATE):
                    r = n % 2
                    if n >= 2:
                        pe.wait_ge(sem("b_spread"), b * NSTATE + n - 1)
                        pe.wait_ge(sem("read_ready"), b * NSTATE + n - 1)
                    mm(bank(2 + r), pick[:, n, :], wparts[:]).then_inc(sem("b_done"), 1)
                    mm(bank(4 + r), pick[:, NSTATE + n, :], wparts[:]).then_inc(sem("c_done"), 1)
                    if n >= 1:
                        add_state(n - 1)
                add_state(NSTATE - 1)
                pe.wait_ge(sem("ygate_ready"), b + 1)
                mm(bank(7), wT[:, WOUT2, :], ygate).then_inc(sem("batch_out"), 1)

            stage_norm(FFN2)
            pe.wait_ge(sem("ffn2_loaded"), 64)
            with pe.Fori(0, NB) as b:
                pe.wait_ge(x_ready, b + x_before(FFN2))
                mm(psum[0:E2, 0, :], wg2[:], h[:, b, :]).then_inc(sem("route_scored"), 1)
                turn_logits(1, b, E2)
                turn_weights(1, b, E2)
                pe.wait_ge(sem("route_parts"), turn(1, b) + 1)
                NC = 2 * E2

                def down2(i):
                    e, k = divmod(i, 2)
                    pe.wait_ge(sem("hid2_ready"), b * NC + i + 1)
                    m = mm(bank(7), w3_2[:, e, k, :], hid0[:, i % 2, :], i == 0, i == NC - 1)
                    m.then_inc(sem("down2_done"), 1)

                for i in range(NC):
                    e, k = divmod(i, 2)
                    s0 = 2 * (i % 2)
                    if i >= 2:
                        pe.wait_ge(sem("gact2_ready"), b * NC + i - 1)
                        pe.wait_ge(sem("prod2_ready"), b * NC + i - 1)
                    mm(bank(s0), w1_2[:, e, k * P:(k + 1) * P], h[:, b, :])
                    mm(bank(s0 + 1), w2_2[:, e, k * P:(k + 1) * P], h[:, b, :]).then_inc(sem("up2_done"), 1)
                    if k == 0:
                        if e >= 2:
                            pe.wait_ge(sem("hid2_ready"), b * NC + 2 * (e - 1))
                        mm(bank(4 + e % 2), pick[:, e, :], wparts[:]).then_inc(sem("weights_spread"), 1)
                    if i >= 1:
                        down2(i - 1)
                down2(NC - 1)

            stage_norm(ATTN3)
            pe.wait_ge(sem("attn3_loaded"), 16 * 9)
            with pe.Fori(0, NB) as b:
                pe.wait_ge(x_ready, b + x_before(ATTN3))
                mm(bank(0), w_3[:, W_IN, :], h[:, b, :]).then_inc(sem("proj3_done"), 1)
                pe.wait_ge(sem("xw_ready"), b + 1)
                mm(bank(1), w_3[:, W_GX, :], xw)
                mm(bank(2), w_3[:, W_GA, :], xw).then_inc(sem("proj3_done"), 1)
                pe.wait_ge(sem("state3_ready"), b + 1)
                mm(bank(7), w_3[:, W_OUT, :], st3).then_inc(sem("batch_out"), 1)

            stage_norm(FFN3)
            pe.wait_ge(sem("ffn3_loaded"), 48)
            with pe.Fori(0, NB) as b:
                pe.wait_ge(x_ready, b + x_before(FFN3))
                mm(psum[0:E3, 0, :], wT[:, WROUT3, 0:E3], h[:, b, :]).then_inc(sem("route_scored"), 1)
                turn_logits(2, b, E3)
                turn_weights(2, b, E3)
                pe.wait_ge(sem("route_parts"), turn(2, b) + 1)
                mm(bank(7), bias3[0:E3, :], sel3[0:E3, :], True, False)
                for e in range(E3):
                    r = e % 2
                    if e >= 2:
                        pe.wait_ge(sem("picked_ready"), b * E3 + e - 1)
                    mm(bank(4 + r), pick[:, e, :], wparts[:]).then_inc(sem("weights_spread"), 1)
                    if e >= 1:
                        pe.wait_ge(sem("picked_ready"), b * E3 + e)
                        mm(bank(7), w_e3[:, e - 1, :], picked[:, (e - 1) % 2, :], False, False).then_inc(sem("y3_added"), 1)
                pe.wait_ge(sem("picked_ready"), b * E3 + E3)
                mm(bank(7), w_e3[:, E3 - 1, :], picked[:, (E3 - 1) % 2, :], False, True).then_inc(sem("y3_added"), 1)

            pe.wait_ge(x_ready, x_before(FFN3 + 1))
            for b in range(NB):
                for t in range(TT):
                    m = nc.tensor.transpose(psum[:, b, t * D:(t + 1) * D], x[:, b, t * P:(t + 1) * P], eye[:])
                m.then_inc(sem("x_turned"), 1)

        @block.scalar
        def _(act):
            def bank(n, m=S):
                return psum[:, n, 0:m]

            def f(out_, in_, func, **kw):
                return nc.scalar.activation(out_, in_, func, **kw)

            def layer_norm(s):
                n = NB * s
                for b in range(NB + 1):
                    if b < NB:
                        act.wait_ge(sem("ln_centered"), n + b + 1)
                        if b >= 2:
                            act.wait_ge(sem("ln_var"), n + b - 1)
                        f(centered[:, b, :], bank(b % 2), ACT.Copy)
                        f(squares[:, b % 2, :], bank(b % 2), ACT.Square).then_inc(sem("ln_squared"), 1)
                    if b >= 1:
                        act.wait_ge(sem("ln_var"), n + b)
                        f(ln_std_t[:, b - 1, :], psum[:, 2 + (b - 1) % 2, 0:TT], ACT.Sqrt, bias=eps[:]).then_inc(sem("ln_std"), 1)

            act.wait_ge(sem("cleared"), 5)
            for k in range(3):
                act.wait_ge(sem("w_turned"), k + 1)
                f(wT[:, 4 * k:4 * k + 4, :], bank(4 + k).rearrange("p (n d) -> p n d", n=4), ACT.Copy).then_inc(sem("wT_ready"), 1)

            layer_norm(ATTN0)
            act.wait_ge(sem("attn0_mm"), 1)
            f(value_sum[:], psum[:, 0, 0:NB], ACT.Copy).then_inc(sem("attn0_out"), 1)
            act.wait_ge(sem("attn0_mm"), 2)
            f(attn0[:], psum[:, 1, 0:NB], ACT.Copy).then_inc(sem("attn0_out"), 1)

            layer_norm(FFN0)
            act.wait_ge(sem("trees_loaded"), 16 * (2 + 15))
            n_hid = 3 * HCH
            with act.Fori(0, NB) as b:
                for i in range(0, n_hid, 2):
                    t, c = divmod(i, HCH)
                    act.wait_ge(sem("hidden0"), b * n_hid + i + 1)
                    if i >= HCH and c == 0:
                        act.wait_ge(sem("tree_out"), b * 3 + t)
                    f(hidden[:, c, :], bank(i % 3), ACT.Relu, bias=b1[:, t, c:c + 1]).then_inc(sem("hid_act"), 1)
                    if i in (HCH + 2, 2 * HCH + 2):
                        act.wait_ge(sem("tree_out"), b * 3 + t)
                        f((qT0, kT0)[t - 1], bank(2 + t), ACT.Copy).then_inc(sem("qkv0_ready"), 1)
                act.wait_ge(sem("tree_out"), b * 3 + 3)
                f(v0, bank(5), ACT.Copy).then_inc(sem("qkv0_ready"), 1)

                def copy_turned(t):
                    act.wait_ge(sem("probs_turned0"), b * TT + t + 1)
                    f(probsT0[:, :, t * P:(t + 1) * P], bank((2, 6)[t % 2]).rearrange("p (k q) -> p k q", k=TT),
                      ACT.Copy).then_inc(sem("probsT0"), 1)

                for t in range(TT):
                    act.wait_ge(sem("shift0"), b * TT + t + 1)
                    if t >= 2:
                        act.wait_ge(sem("probs_turned0"), b * TT + t - 1)
                    f(probs0[:, t % 2, :], bank(t % 2), ACT.Exp, bias=small[:, 1, t:t + 1], scale=SCALE0,
                      accum_out=small[:, 2, t:t + 1]).then_inc(sem("exp0"), 1)
                    if t >= 1:
                        copy_turned(t - 1)
                copy_turned(TT - 1)

            def copy_vT(b):
                act.wait_ge(sem("qkv1_done"), 3 * b + 3)
                f(vT1, bank(6), ACT.Copy).then_inc(sem("vT_ready"), 1)

            def copy_max_rows(b, g):
                n = GROUPS * b + g
                act.wait_ge(sem("max_turned"), n + 1)
                if not (isinstance(b, int) and n < 2):
                    act.wait_ge(max_stacked[(g + 2) % GROUPS], (b + g // 2) * 16 * PARTS)
                f(max_rows[0:4 * PARTS, g % 2, :], psum[0:4 * PARTS, 6, :], ACT.Copy).then_inc(sem("max_rows_ready"), 1)

            def copy_heads(b, g):
                n = GROUPS * b + g
                act.wait_ge(sem("keys_added"), (n + 1) * TT)
                if not (isinstance(b, int) and n == 0):
                    act.wait_ge(sem("head_out_ready"), n)
                f(head_raw, bank(4), ACT.Copy).then_inc(sem("head_raw_ready"), 1)

            def exp_batch(b, first, last):
                for g in range(GROUPS):
                    n = GROUPS * b + g
                    begin = first and g == 0
                    for kt in range(TT):
                        for j in range(4):
                            i = 4 * kt + j
                            act.wait_ge(sem("scoresT1"), n * GTILES + i + 1)
                            if j == 0 and (kt >= 2 or not begin):
                                act.wait_ge(sem("keys_added"), n * TT + kt - 1)
                            f(expT[:, kt % 2, j, :], bank(2 + i % 2), ACT.Exp).then_inc(sem("exp1"), 1)
                        if kt == 0 and not begin:
                            copy_heads(*((b, g - 1) if g >= 1 else (b - 1, GROUPS - 1)))
                        if kt == 0 and (g < GROUPS - 1 or not last):
                            copy_max_rows(*((b, g + 1) if g < GROUPS - 1 else (b + 1, 0)))
                        if kt == 2 and g == 1 and not last:
                            copy_vT(b + 1)

            layer_norm(ATTN1)
            copy_vT(0)
            copy_max_rows(0, 0)
            exp_batch(0, True, False)
            with act.Fori(1, NB - 1) as b:
                exp_batch(b, False, False)
            exp_batch(NB - 1, False, True)
            copy_heads(NB - 1, GROUPS - 1)

            layer_norm(FFN1)
            for b in range(NB):
                act.wait_ge(sem("h_turned"), b + 1)
                f(h_rows[:, b * TT:(b + 1) * TT, :], bank(1 + b % 2).rearrange("p (t d) -> p t d", t=TT),
                  ACT.Copy).then_inc(sem("h_rows_ready"), 1)
            act.wait_ge(setup, SETUP.index("logits1") + 1)
            f(prob1, prob1, ACT.Exp).then_inc(sem("act_setup"), 1)
            for b in range(NB):
                act.wait_ge(sem("shared_up"), 2 * b + 1)
                if b >= 1:
                    act.wait_ge(sem("shared_hid"), b)
                f(shared_act0, bank(3), ACT.Silu).then_inc(sem("shared_gate"), 1)
                f(shared_act1[0:F1R], psum[0:F1R, 4, :], ACT.Silu).then_inc(sem("shared_gate"), 1)

            def copy_in(u, c, n, begin):
                act.wait_ge(sem("x1_turned"), n + 1)
                if c >= 2 or not begin:
                    act.wait_ge(sem("up1_done"), n - 1)
                f(xT_in[:, c % 2, :], psum[:, c % 2, 0:P], ACT.Copy).then_inc(sem("xT1_ready"), 1)

            def gate(u, c, n, begin):
                act.wait_ge(sem("up1_done"), n + 1)
                if c >= 2 or not begin:
                    act.wait_ge(sem("hid1_ready"), n - 1)
                f(gate_act[:, c % 2, :], psum[:, 2 + c % 2, 0:F1], ACT.Silu).then_inc(sem("gate1_ready"), 1)

            def copy_out(u, c, n, begin):
                r = c // PT
                act.wait_ge(sem("y1_done"), n + 1)
                if c % PT == 0 and not begin:
                    act.wait_ge(y_stored[r], 16 * u)
                f(y_rows[:, r, c % PT, :], psum[:, 6 + c % 2, 0:D], ACT.Copy).then_inc(sem("y1_ready"), 1)

            run_tiles(act, (copy_in, gate, None, copy_out))

            layer_norm(ATTN2)
            act.wait_ge(sem("attn2_loaded"), 80)
            f(a_neg[:], a_neg[:], ACT.Exp).then_inc(sem("act_setup"), 1)
            act.wait_ge(setup, SETUP.index("a_neg") + 1)
            with act.Fori(0, NB) as b:
                act.wait_ge(sem("proj2_done"), 2 * b + 1)
                f(xpad[:, DCONV - 1:DCONV - 1 + S], bank(0), ACT.Copy).then_inc(sem("xin_ready"), 1)
                f(zgate, bank(1), ACT.Silu).then_inc(sem("zgate_ready"), 1)
                act.wait_ge(sem("conv_ready"), b + 1)
                f(xconv, conv, ACT.Silu).then_inc(sem("xconv_ready"), 1)
                act.wait_ge(sem("dtv_ready"), b + 1)
                f(dtl, dtv, ACT.Abs).then_inc(sem("dtl_step"), 1)
                act.wait_ge(sem("dtl_step"), b * 3 + 1)
                f(dtl, dtl, ACT.Exp, scale=-1.0).then_inc(sem("dtl_step"), 1)
                act.wait_ge(sem("dtl_step"), b * 3 + 2)
                f(dtl, dtl, ACT.Ln, bias=one[:]).then_inc(sem("dtl_step"), 1)
                act.wait_ge(sem("dtx_ready"), b + 1)
                for n in range(NSTATE):
                    r = n % 2
                    act.wait_ge(sem("b_done"), b * NSTATE + n + 1)
                    if n >= 2:
                        act.wait_ge(sem("drive_ready"), b * NSTATE + n - 1)
                        act.wait_ge(sem("scanned"), b * NSTATE + n - 1)
                    f(bcast_b[:, r, :], bank(2 + r), ACT.Copy).then_inc(sem("b_spread"), 1)
                    f(decay[:, r, :], dt, ACT.Exp, scale=a_neg[:, n:n + 1]).then_inc(sem("decay_ready"), 1)

            layer_norm(FFN2)
            act.wait_ge(setup, SETUP.index("logits2") + 1)
            NC = 2 * E2
            with act.Fori(0, NB) as b:
                act.wait_ge(sem("route_scored"), turn(1, b) + 1)
                f(lt[0:E2, :], psum[0:E2, 0, :], ACT.Copy).then_inc(sem("route_logits"), 1)
                act.wait_ge(sem("route_shift"), turn(1, b) + 1)
                f(small[:, 1, :], small[:, 0, :], ACT.Exp).then_inc(sem("route_exp"), 1)
                for i in range(NC):
                    act.wait_ge(sem("up2_done"), b * NC + i + 1)
                    if i >= 2:
                        act.wait_ge(sem("prod2_ready"), b * NC + i - 1)
                    f(gact0[:, i % 2, :], bank(2 * (i % 2)), ACT.Silu).then_inc(sem("gact2_ready"), 1)

            layer_norm(ATTN3)
            act.wait_ge(sem("attn3_loaded"), 16 * 9)
            f(a_par[:, 1:2], a_par[:, 0:1], ACT.Abs).then_inc(sem("act_setup"), 1)
            act.wait_ge(sem("act_setup"), 3)
            f(a_par[:, 1:2], a_par[:, 1:2], ACT.Exp, scale=-1.0).then_inc(sem("act_setup"), 1)
            act.wait_ge(sem("act_setup"), 4)
            f(a_par[:, 1:2], a_par[:, 1:2], ACT.Ln, bias=one[:]).then_inc(sem("act_setup"), 1)
            act.wait_ge(setup, SETUP.index("apar_16") + 1)
            with act.Fori(0, NB) as b:
                act.wait_ge(sem("proj3_done"), 2 * b + 1)
                f(xw, bank(0), ACT.Identity, bias=b_3[:, W_IN:W_IN + 1]).then_inc(sem("xw_ready"), 1)
                act.wait_ge(sem("proj3_done"), 2 * b + 2)
                f(gx, bank(1), ACT.Sigmoid, bias=b_3[:, W_GX:W_GX + 1]).then_inc(sem("gx_ready"), 1)
                f(ga, bank(2), ACT.Sigmoid, bias=b_3[:, W_GA:W_GA + 1]).then_inc(sem("ga_ready"), 1)
                act.wait_ge(sem("ga_ready"), b + 1)
                f(dec, ga, ACT.Exp, scale=a_par[:, 2:3])
                f(drv, ga, ACT.Exp, scale=a_par[:, 3:4]).then_inc(sem("drv_step"), 1)
                act.wait_ge(sem("drv_step"), b + 1)
                f(drv, drv, ACT.Sqrt, scale=-1.0, bias=one[:]).then_inc(sem("drv_ready"), 1)

            layer_norm(FFN3)
            act.wait_ge(setup, SETUP.index("logits3") + 1)
            with act.Fori(0, NB) as b:
                act.wait_ge(sem("route_scored"), turn(2, b) + 1)
                f(lt[0:E3, :], psum[0:E3, 0, :], ACT.Identity, bias=router3_b[0:E3, :]).then_inc(sem("route_logits"), 1)

            for b in range(NB):
                act.wait_ge(sem("x_turned"), NB + b + 1)
                f(rows[:, b * TT:(b + 1) * TT, :], bank(b).rearrange("p (t d) -> p t d", t=TT), ACT.Copy).then_inc(sem("out_rows"), 1)

        @block.vector
        def _(dve):
            v = nc.vector

            def bank(n, m=S):
                return psum[:, n, 0:m]

            class Steps:

                def __init__(self, name, b, per, before=0):
                    self.sem, self.b, self.per, self.n, self.before = sem(name), b, per, 0, before

                def did(self, instruction):
                    instruction.then_inc(self.sem, 1)
                    self.n += 1

                def wait(self):
                    dve.wait_ge(self.sem, self.b * self.per + (self.before + self.n))

                def then(self, instruction_of):
                    self.wait()
                    self.did(instruction_of())

                def end(self):
                    assert self.n == self.per, self.n

            Q_STEPS, R1_STEPS, CONV_STEPS, R2_STEPS = NB * PARTS, 55, NB * (DCONV - 1), 25

            def layer_norm(s):
                n = NB * s
                for b in range(NB + 1):
                    if b < NB:
                        dve.wait_ge(sem("ln_std"), n + b + 1)
                        v.reciprocal(ln_rstd_t[:, b, :], ln_std_t[:, b, :]).then_inc(sem("ln_rstd"), 1)
                        dve.wait_ge(sem("ln_rstd"), n + b + 1)
                        if b >= 2:
                            dve.wait_ge(sem("ln_spread"), n + b - 1)
                        for t in range(TT):
                            m = v.tensor_scalar(diag[:, b % 2, t * P:(t + 1) * P], eye[:], ln_rstd_t[:, b, t:t + 1], None, ALU.mult)
                        m.then_inc(sem("ln_diag"), 1)
                    if b >= 1:
                        dve.wait_ge(sem("ln_spread"), n + b)
                        v.tensor_tensor(h[:, b - 1, :], centered[:, b - 1, :], bank(4 + (b - 1) % 2), ALU.mult).then_inc(ln_done, 1)

            def add_to_x(b, n):
                v.tensor_tensor(x[:, b, :], bank(n), x[:, b, :], ALU.add).then_inc(x_ready, 1)

            for b in range(NB):
                dve.wait_ge(sem("x_turned"), b + 1)
                v.tensor_copy(x[:, b, :], bank(b)).then_inc(x_ready, 1)

            layer_norm(ATTN0)
            dve.wait_ge(ln_done, NB)
            v.reduce_sum(token_sum[:], h[:], AX.X).then_inc(sem("token_sums"), 1)
            dve.wait_ge(sem("attn0_out"), 2)
            for b in range(NB):
                v.tensor_scalar(x[:, b, :], x[:, b, :], attn0[:, b:b + 1], None, ALU.add).then_inc(x_ready, 1)

            layer_norm(FFN0)
            dve.wait_ge(sem("trees_loaded"), 16 * (2 + 15))
            n_hid = 3 * HCH
            with dve.Fori(0, NB) as b:
                dve.wait_ge(sem("nodes0"), 2 * b + 1)
                v.tensor_scalar(gates, bank(6), node_b[:], 0.0, ALU.add, ALU.is_ge).then_inc(sem("path_ready"), 1)
                dve.wait_ge(sem("nodes0"), 2 * b + 2)
                v.tensor_scalar(leaf, bank(7), 0.0, None, ALU.is_equal).then_inc(sem("path_ready"), 1)
                for i in range(1, n_hid, 2):
                    t, c = divmod(i, HCH)
                    dve.wait_ge(sem("hidden0"), b * n_hid + i + 1)
                    if t >= 1 and c == 1:
                        dve.wait_ge(sem("tree_out"), b * 3 + t)
                    v.tensor_scalar(hidden[:, c, :], bank(i % 3), b1[:, t, c:c + 1], 0.0, ALU.add, ALU.max).then_inc(sem("hid_dve"), 1)
                for t in range(TT):
                    dve.wait_ge(sem("scores0"), b * TT + t + 1)
                    v.reduce_max(small[:, 0, t:t + 1], bank(t % 2), AX.X).then_inc(sem("softmax0_step"), 1)
                    dve.wait_ge(sem("softmax0_step"), 2 * (b * TT + t) + 1)
                    v.tensor_scalar(small[:, 1, t:t + 1], small[:, 0, t:t + 1], -SCALE0, None, ALU.mult).then_inc(sem("shift0"), 1)
                    dve.wait_ge(sem("exp0"), b * TT + t + 1)
                    v.reciprocal(small[:, 3, t:t + 1], small[:, 2, t:t + 1]).then_inc(sem("softmax0_step"), 1)
                    dve.wait_ge(sem("softmax0_step"), 2 * (b * TT + t) + 2)
                    v.tensor_scalar(probs0[:, t % 2, :], probs0[:, t % 2, :], small[:, 3, t:t + 1], None, ALU.mult).then_inc(sem("probs0"), 1)
                dve.wait_ge(sem("batch_out"), b + outs_before(FFN0) + 1)
                add_to_x(b, 7)

            def cut(b, tag, src, scale, parts, rem):
                st = Steps(tag + "_step", b, PARTS)
                st.did(v.tensor_scalar(parts(0), src, scale, None, ALU.mult))
                st.then(lambda: v.scalar_tensor_tensor(rem, src, scale, parts(0), ALU.mult, ALU.subtract))
                st.then(lambda: v.tensor_copy(parts(1), rem))
                st.wait()
                st.end()
                v.tensor_tensor(parts(2), rem, parts(1), ALU.subtract).then_inc(sem(tag + "parts_ready"), 1)

            def cut_q(b):
                dve.wait_ge(sem("qkv1_done"), 3 * b + 1)
                if not (isinstance(b, int) and b == 0):
                    dve.wait_ge(sem("bounced"), b * BOUNCES)
                cut(b, "q", bank(6), SCALE1, lambda i: qparts[:, i, :], qrem)

            def cut_k(b):
                dve.wait_ge(sem("qkv1_done"), 3 * b + 2)
                if not (isinstance(b, int) and b == 0):
                    dve.wait_ge(sem("bounced"), b * BOUNCES)
                    dve.wait_ge(stacked[GROUPS - 1], b * STACKS)
                cut(b, "k", bank(6), SCALE1, lambda i: kparts[:, i, :], krem)

            def values_by_token(b):
                dve.wait_ge(sem("v_turned"), b + 1)
                v.tensor_copy(vtok, bank(6).rearrange("p (t h d) -> p t h d", t=TT, h=HEADS)).then_inc(sem("vtok_ready"), 1)

            def place_values(b, g):
                hs = slice(4 * g, 4 * g + 4)
                dve.wait_ge(sem("vtok_ready"), b + 1)
                if not (isinstance(b, int) and b == 0):
                    dve.wait_ge(sem("keys_added"), (GROUPS * (b - 1) + g + 1) * TT)
                v.tensor_copy(v32[:, :, hs, 0:DH], vtok[:, :, hs, :]).then_inc(sem("v_ready"), 1)

            def maximum(b, g, i):
                j, t = divmod(i, TT)
                dve.wait_ge(sem("scores1"), (GROUPS * b + g) * GTILES + i + 1)
                v.reduce_max(headmax[:, g % 2, t, j:j + 1], bank(i % 2), AX.X).then_inc(sem("maxed"), 1)

            def cut_maxima(b, g):
                n = GROUPS * b + g
                dve.wait_ge(sem("maxed"), (n + 1) * GTILES)
                if not (isinstance(b, int) and n < 2):
                    dve.wait_ge(sem("max_turned"), n - 1)
                cut(n, "max", headmax[:, g % 2], -1.0, lambda i: maxparts[:, g % 2, :, i, :], maxrem[:, g % 2])

            def invert_sums(b, g):
                n = GROUPS * b + g
                dve.wait_ge(sem("sums_by_token"), n + 1)
                v.reciprocal(sum_inv, psum[:, 5, 0:4 * TT].rearrange("p (t j) -> p t j", t=TT)).then_inc(sem("sum_inv_ready"), 1)
                dve.wait_ge(sem("sum_inv_ready"), n + 1)
                v.tensor_copy(inv_rows, sum_inv.unsqueeze(3).broadcast_to([P, TT, 4, 32])).then_inc(sem("inv_rows_ready"), 1)

            def divide_heads(b, g):
                n = GROUPS * b + g
                dve.wait_ge(sem("inverse_spread"), n + 1)
                if not (isinstance(b, int) and n == 0):
                    dve.wait_ge(sem("attn_out1"), n)
                v.tensor_tensor(head_out, head_raw, bank(5), ALU.mult).then_inc(sem("head_out_ready"), 1)

            def add_attention(b):
                dve.wait_ge(sem("attn_out1"), GROUPS * b + GROUPS)
                v.scalar_tensor_tensor(x[:, b, :], bank(7), bout1[:], x[:, b, :], ALU.add, ALU.add).then_inc(x_ready, 1)

            def maxima_batch(b, first, last):
                for g in range(GROUPS):
                    begin = first and g == 0
                    prev = (b, g - 1) if g >= 1 else (b - 1, GROUPS - 1)
                    ahead = (b, g + 2) if g < 2 else (b + 1, g - 2)
                    for kt in range(TT):
                        if g < 2 or not last:
                            for j in range(4):
                                maximum(*ahead, 4 * kt + j)
                        if kt == 0:
                            if g == 0:
                                place_values(b, GROUPS - 1)
                            if not last:
                                if g == 2:
                                    values_by_token(b + 1)
                                    place_values(b + 1, 0)
                                    place_values(b + 1, 1)
                                if g == 3:
                                    place_values(b + 1, 2)
                        if kt == 1:
                            if not begin:
                                invert_sums(*prev)
                            if g == 0 and not last:
                                cut_q(b + 1)
                        if kt == 2 and not begin:
                            divide_heads(*prev)
                        if kt == 3:
                            if g < 2 or not last:
                                cut_maxima(*ahead)
                            if g == 0 and not begin:
                                add_attention(b - 1)
                            if g == 0 and not last:
                                cut_k(b + 1)

            layer_norm(ATTN1)
            v.tensor_copy(eye_b[:], eye[:]).then_inc(setup, 1)
            dve.wait_ge(sem("cleared"), N_CLEARED)
            cut_q(0)
            cut_k(0)
            values_by_token(0)
            for g in range(GROUPS - 1):
                place_values(0, g)
            for g in range(2):
                for i in range(GTILES):
                    maximum(0, g, i)
                cut_maxima(0, g)
            maxima_batch(0, True, False)
            with dve.Fori(1, NB - 1) as b:
                maxima_batch(b, False, False)
            maxima_batch(NB - 1, False, True)
            invert_sums(NB - 1, GROUPS - 1)
            divide_heads(NB - 1, GROUPS - 1)
            add_attention(NB - 1)

            def weight_parts(k, b, src, n):
                st = Steps("k_step", turn(k, b), 4, NB * (PARTS + 4))
                st.did(v.tensor_copy(wparts[0:n, :], src))
                st.then(lambda: v.tensor_tensor(part_r[0:n, :], src, wparts[0:n, :], ALU.subtract))
                st.then(lambda: v.tensor_copy(part_b[0:n, :], part_r[0:n, :]))
                st.then(lambda: v.tensor_copy(wparts[32:32 + n, :], part_b[0:n, :]))
                st.end()
                v.tensor_tensor(wparts[64:64 + n, :], part_r[0:n, :], part_b[0:n, :], ALU.subtract).then_inc(sem("route_parts"), 1)

            def two_best(st, n, of):
                st.did(v.memset(top_f[:, :, 0:4], 0.0))
                for t in range(TT):
                    st.did(v.max(top[:, t, :], of(t)))
                st.wait()
                st.did(v.memset(top_f[:, :, 4:8], 0.0))
                for t in range(TT):
                    st.did(v.max_index(top_at[:, t, :], top[:, t, :], of(t)))
                st.then(lambda: v.tensor_copy(top_f[:, :, 0:2], top_at[:, :, 0:2]))
                st.wait()

            def clear_logits(stage, k):
                dve.wait_ge(ln_done, NB * stage + NB)
                v.memset(lt, 0.0).then_inc(setup, 1)

            def best(n, t, k):
                return iota[:, 0:n], top_f[:, t, k:k + 1]

            layer_norm(FFN1)
            dve.wait_ge(sem("ffn1_loaded"), 16 * N_FFN1)
            dve.wait_ge(ln_done, NB * FFN1 + NB)
            v.memset(shared_hid1, 0.0)
            v.memset(hid_rows, 0.0).then_inc(setup, 1)
            dve.wait_ge(sem("counted1"), 1)
            scores1 = psum[:, 0, 0:NT * E1].rearrange("p (t e) -> p t e", t=NT)

            def each(per_tile):
                return per_tile.unsqueeze(2).broadcast_to([P, NT, E1])

            st = Steps("q_step", 0, R1_STEPS, Q_STEPS)
            st.did(v.reduce_max(peak1, scores1, AX.X))
            st.wait()
            v.tensor_tensor(prob1, scores1, each(peak1), ALU.subtract).then_inc(setup, 1)
            dve.wait_ge(sem("act_setup"), 1)
            st.did(v.reduce_sum(sum1, prob1, AX.X))
            st.then(lambda: v.reciprocal(sum1_inv, sum1))
            st.then(lambda: v.tensor_tensor(prob1, prob1, each(sum1_inv), ALU.mult))
            st.wait()
            for t in range(NT):
                st.did(v.max(top1[:, t, :], prob1[:, t, :]))
            st.wait()
            for t in range(NT):
                st.did(v.max_index(top1_at[:, t, :], top1[:, t, :], prob1[:, t, :]))
            st.then(lambda: v.tensor_copy(expert_at, top1_at[:, :, 0:K1].rearrange("p t k -> p k t")))
            st.wait()
            experts = iota[:, 0:E1].unsqueeze(1).broadcast_to([P, NT, E1])
            for k, dst in enumerate((first1, second1)):
                st.did(v.tensor_tensor(dst, experts, each(expert_at[:, k, :]), ALU.is_equal))
            st.wait()
            v.tensor_tensor(chosen1, first1, second1, ALU.add).then_inc(setup, 1)
            st.did(v.tensor_tensor(sum1, top1[:, :, 0], top1[:, :, 1], ALU.add))
            st.then(lambda: v.tensor_scalar(sum1, sum1, 1e-9, None, ALU.add))
            st.then(lambda: v.reciprocal(sum1_inv, sum1))
            st.wait()
            for k in range(K1):
                st.did(v.tensor_tensor(pair_weight[:, k, :], top1[:, :, k], sum1_inv, ALU.mult))
            st.did(v.tensor_scalar(base, expert_at, float(CAP), None, ALU.mult))

            def shared_products(b):
                for n, (src, gates_, dst, rr) in enumerate(((5, shared_act0, shared_hid0, slice(0, P)),
                                                            (6, shared_act1, shared_hid1, slice(0, F1R)))):
                    dve.wait_ge(sem("shared_gate"), 2 * b + n + 1)
                    dve.wait_ge(sem("shared_up"), 2 * b + 2)
                    if b >= 1:
                        dve.wait_ge(sem("shared_out"), b)
                    m = v.tensor_tensor(dst[rr], psum[rr, src, :], gates_[rr], ALU.mult)
                m.then_inc(sem("shared_hid"), 1)

            def add_shared(b):
                dve.wait_ge(sem("shared_out"), b + 1)
                v.tensor_tensor(x[:, b, :], bank(7), x[:, b, :], ALU.add).then_inc(sem("shared_added"), 1)

            shared_products(0)
            dve.wait_ge(sem("counted1"), 2)
            for oh, dst in ((first1, place_first), (second1, place_second)):
                st.did(v.tensor_tensor(dst, scores1, oh, ALU.mult))
            st.wait()
            for k, src in enumerate((place_first, place_second)):
                st.did(v.reduce_sum(place[:, k, :], src, AX.X))
            st.then(lambda: v.tensor_scalar(beyond, place, float(CAP), None, ALU.is_ge))
            st.did(v.scalar_tensor_tensor(gather_f, place, float(CAP - 1), base, ALU.min, ALU.add))
            st.did(v.scalar_tensor_tensor(pair_weight, place, float(CAP), pair_weight, ALU.is_lt, ALU.mult))
            st.did(v.tensor_tensor(scatter_f, place, base, ALU.add))
            st.then(lambda: v.scalar_tensor_tensor(scatter_f, beyond, SKIP, scatter_f, ALU.mult, ALU.add))
            st.then(lambda: v.tensor_copy(gather_at, gather_f))
            st.end()
            v.tensor_copy(scatter_at, scatter_f).then_inc(setup, 1)
            for b in range(1, NB):
                add_shared(b - 1)
                shared_products(b)
            add_shared(NB - 1)

            def hidden_rows(u, c, n, begin):
                dve.wait_ge(sem("gate1_ready"), n + 1)
                if c >= 2 or not begin:
                    dve.wait_ge(sem("hid1_turned"), n - 1)
                v.tensor_tensor(hid_rows[:, c % 2, 0:F1], psum[:, 2 + c % 2, F1:2 * F1], gate_act[:, c % 2, :],
                                ALU.mult).then_inc(sem("hid1_ready"), 1)

            def copy_hidden(u, c, n, begin):
                dve.wait_ge(sem("hid1_turned"), n + 1)
                if c >= 2 or not begin:
                    dve.wait_ge(sem("y1_done"), n - 1)
                v.tensor_copy(hidT[:, c % 2], psum[:, 4 + c % 2, 0:2 * P].rearrange("p (f t) -> p f t", f=2)).then_inc(sem("hidT1_ready"), 1)

            run_tiles(dve, (None, hidden_rows, copy_hidden, None))

            def combine(b):
                dve.wait_ge(gathered_sem[b], 16 * K1 * TT)
                for t in range(b * TT, (b + 1) * TT):
                    m = v.tensor_scalar(gathered[:, t, 0, :], gathered[:, t, 0, :], pair_weight[:, 0, t:t + 1], None, ALU.mult)
                m.then_inc(sem("max_step"), 1)
                dve.wait_ge(sem("max_step"), NB * GROUPS * PARTS + b + 1)
                for t in range(b * TT, (b + 1) * TT):
                    m = v.scalar_tensor_tensor(gathered[:, t, 0, :], gathered[:, t, 1, :], pair_weight[:, 1, t:t + 1],
                                               gathered[:, t, 0, :], ALU.mult, ALU.add)
                m.then_inc(sem("combined"), 1)

            def add_routed(b):
                dve.wait_ge(sem("batch_out"), b + outs_before(FFN1) + 1)
                add_to_x(b, 6 + b % 2)

            for b in range(NB):
                combine(b)
                if b >= 1:
                    add_routed(b - 1)
            add_routed(NB - 1)

            layer_norm(ATTN2)
            dve.wait_ge(sem("wT_ready"), 3)
            v.tensor_scalar(dt_rep[:], ones[:], wT[:, WSSM, 2 * NSTATE:2 * NSTATE + 1], None, ALU.mult).then_inc(setup, 1)
            dve.wait_ge(sem("act_setup"), 2)
            v.tensor_scalar(a_neg[:], a_neg[:], -1.0, None, ALU.mult).then_inc(setup, 1)
            dve.wait_ge(ln_done, NB * ATTN2 + NB)
            v.memset(xpad[:, 0:DCONV - 1], 0.0).then_inc(setup, 1)
            dve.wait_ge(setup, SETUP.index("xpad") + 1)
            with dve.Fori(0, NB) as b:
                dve.wait_ge(sem("xin_ready"), b + 1)
                st = Steps("q_step", b, DCONV - 1, Q_STEPS + R1_STEPS)
                st.did(v.tensor_scalar(conv, xpad[:, 0:S], conv_w[:, 0:1], conv_b[:], ALU.mult, ALU.add))
                for k in range(1, DCONV):
                    st.wait()
                    m = v.scalar_tensor_tensor(conv, xpad[:, k:k + S], conv_w[:, k:k + 1], conv, ALU.mult, ALU.add)
                    if k < DCONV - 1:
                        st.did(m)
                st.end()
                m.then_inc(sem("conv_ready"), 1)
                dve.wait_ge(sem("proj2_done"), 2 * b + 2)
                v.tensor_scalar(dtv, bank(3), dt_w[:], dt_b[:], ALU.mult, ALU.add).then_inc(sem("dtv_ready"), 1)
                st = Steps("k_step", b, 4, NB * PARTS)
                bcp = psum[0:2 * NSTATE, 2, :]
                st.did(v.tensor_copy(wparts[0:32, :], bcp))
                st.then(lambda: v.tensor_tensor(part_r, bcp, wparts[0:32, :], ALU.subtract))
                st.then(lambda: v.tensor_copy(part_b, part_r))
                st.then(lambda: v.tensor_copy(wparts[32:64, :], part_b))
                st.end()
                v.tensor_tensor(wparts[64:96, :], part_r, part_b, ALU.subtract).then_inc(sem("bc_parts"), 1)
                dve.wait_ge(sem("dtl_step"), b * 3 + 3)
                dve.wait_ge(sem("dtv_ready"), b + 1)
                v.scalar_tensor_tensor(dt, dtv, 0.0, dtl, ALU.max, ALU.add).then_inc(sem("dt_ready"), 1)
                dve.wait_ge(sem("dt_ready"), b + 1)
                v.tensor_tensor(dtx, dt, xconv, ALU.mult).then_inc(sem("dtx_ready"), 1)
                for n in range(NSTATE):
                    r = n % 2
                    dve.wait_ge(sem("decay_ready"), b * NSTATE + n + 1)
                    dve.wait_ge(sem("drive_ready"), b * NSTATE + n + 1)
                    v.tensor_tensor_scan(state[:, r, :], decay[:, r, :], drive[:, r, :], 0.0, ALU.mult, ALU.add).then_inc(sem("scanned"), 1)
                    dve.wait_ge(sem("c_done"), b * NSTATE + n + 1)
                    if n >= 2:
                        dve.wait_ge(sem("y_added"), b * NSTATE + n - 1)
                    dve.wait_ge(sem("scanned"), b * NSTATE + n + 1)
                    v.tensor_tensor(read[:, r, :], bank(4 + r), state[:, r, :], ALU.mult).then_inc(sem("read_ready"), 1)
                dve.wait_ge(sem("y_added"), b * NSTATE + NSTATE)
                dve.wait_ge(sem("zgate_ready"), b + 1)
                v.tensor_tensor(ygate, bank(6), zgate, ALU.mult).then_inc(sem("ygate_ready"), 1)
                dve.wait_ge(sem("batch_out"), b + outs_before(ATTN2) + 1)
                add_to_x(b, 7)

            layer_norm(FFN2)
            clear_logits(FFN2, 2)
            NC = 2 * E2
            with dve.Fori(0, NB) as b:
                dve.wait_ge(sem("route_logits_turned"), turn(1, b) + 1)
                st = Steps("q_step", b, R2_STEPS, Q_STEPS + R1_STEPS + CONV_STEPS)
                two_best(st, E2, lambda t: psum[:, 1, t * P:t * P + E2])
                v.tensor_tensor(small[:, 0, :], top[:, :, 1], top[:, :, 0], ALU.subtract).then_inc(sem("route_shift"), 1)
                dve.wait_ge(sem("route_exp"), turn(1, b) + 1)
                st.did(v.tensor_scalar(small[:, 2, :], small[:, 1, :], 1.0, None, ALU.add))
                st.then(lambda: v.reciprocal(small[:, 3, :], small[:, 2, :]))
                st.then(lambda: v.tensor_tensor(small[:, 4, :], small[:, 1, :], small[:, 3, :], ALU.mult))
                st.wait()
                for t in range(TT):
                    for k, dst in ((0, weight), (1, prob)):
                        i, at = best(E2, t, k)
                        st.did(v.tensor_scalar(dst[:, t, 0:E2], i, at, small[:, 3 + k, t:t + 1], ALU.is_equal, ALU.mult))
                st.wait()
                for t in range(TT):
                    m = v.tensor_tensor(weight[:, t, 0:E2], weight[:, t, 0:E2], prob[:, t, 0:E2], ALU.add)
                    if t < TT - 1:
                        st.did(m)
                st.end()
                m.then_inc(sem("route_weights"), 1)
                dve.wait_ge(sem("route_weights_turned"), turn(1, b) + 1)
                weight_parts(1, b, psum[0:E2, 3, :], E2)
                for i in range(NC):
                    e, k = divmod(i, 2)
                    s0, r = 2 * (i % 2), i % 2
                    dve.wait_ge(sem("gact2_ready"), b * NC + i + 1)
                    v.tensor_tensor(prod0[:, r, :], bank(s0 + 1), gact0[:, r, :], ALU.mult).then_inc(sem("prod2_ready"), 1)
                    dve.wait_ge(sem("weights_spread"), b * E2 + e + 1)
                    if i >= 2:
                        dve.wait_ge(sem("down2_done"), b * NC + i - 1)
                    dve.wait_ge(sem("prod2_ready"), b * NC + i + 1)
                    v.tensor_tensor(hid0[:, r, :], bank(4 + e % 2), prod0[:, r, :], ALU.mult).then_inc(sem("hid2_ready"), 1)
                dve.wait_ge(sem("down2_done"), b * NC + NC)
                add_to_x(b, 7)

            layer_norm(ATTN3)
            dve.wait_ge(sem("act_setup"), 5)
            v.scalar_tensor_tensor(a_par[:, 1:2], a_par[:, 0:1], 0.0, a_par[:, 1:2], ALU.max, ALU.add).then_inc(setup, 1)
            dve.wait_ge(setup, SETUP.index("apar") + 1)
            v.tensor_scalar(a_par[:, 2:3], a_par[:, 1:2], -8.0, None, ALU.mult).then_inc(setup, 1)
            v.tensor_scalar(a_par[:, 3:4], a_par[:, 1:2], -16.0, None, ALU.mult).then_inc(setup, 1)
            with dve.Fori(0, NB) as b:
                dve.wait_ge(sem("gx_ready"), b + 1)
                st = Steps("max_step", b, 2, NB * GROUPS * PARTS + NB)
                st.did(v.tensor_tensor(gx, gx, xw, ALU.mult))
                dve.wait_ge(sem("drv_ready"), b + 1)
                st.then(lambda: v.tensor_tensor(gx, gx, drv, ALU.mult))
                st.wait()
                st.end()
                v.tensor_tensor_scan(st3, dec, gx, 0.0, ALU.mult, ALU.add).then_inc(sem("state3_ready"), 1)
                dve.wait_ge(sem("batch_out"), b + outs_before(ATTN3) + 1)
                v.scalar_tensor_tensor(x[:, b, :], bank(7), b_3[:, W_OUT:W_OUT + 1], x[:, b, :], ALU.add, ALU.add).then_inc(x_ready, 1)

            layer_norm(FFN3)
            clear_logits(FFN3, 3)
            v.memset(wparts[:], 0.0).then_inc(setup, 1)
            dve.wait_ge(setup, SETUP.index("wparts") + 1)
            with dve.Fori(0, NB) as b:
                dve.wait_ge(sem("route_logits_turned"), turn(2, b) + 1)
                st = Steps("q_step", b, 15, Q_STEPS + R1_STEPS + CONV_STEPS + NB * R2_STEPS)
                two_best(st, E3, lambda t: psum[:, 1, t * P:t * P + E3])
                for t in range(TT):
                    i, at = best(E3, t, 0)
                    st.did(v.tensor_scalar(chosen[:, t, 0:E3], i, at, None, ALU.is_equal))
                st.wait()
                st.end()
                for t in range(TT):
                    i, at = best(E3, t, 1)
                    m = v.scalar_tensor_tensor(weight[:, t, 0:E3], i, at, chosen[:, t, 0:E3], ALU.is_equal, ALU.add)
                m.then_inc(sem("route_weights"), 1)
                dve.wait_ge(sem("route_weights_turned"), turn(2, b) + 1)
                v.tensor_copy(sel3[0:E3, :], psum[0:E3, 3, :])
                v.tensor_copy(wparts[0:E3, :], psum[0:E3, 3, :]).then_inc(sem("route_parts"), 1)
                for e in range(E3):
                    r = e % 2
                    dve.wait_ge(sem("weights_spread"), NB * E2 + b * E3 + e + 1)
                    if e >= 2:
                        dve.wait_ge(sem("y3_added"), b * E3 + e - 1)
                    v.tensor_tensor(picked[:, r, :], h[:, b, :], bank(4 + r), ALU.mult).then_inc(sem("picked_ready"), 1)
                dve.wait_ge(sem("y3_added"), b * E3 + E3)
                add_to_x(b, 7)


N_CLEARED = 19
N_FFN1 = 3 + 2 + 2 + 2


def kernel(**inputs):
    import concourse.bacc as bacc
    from concourse.bass_utils import run_bass_kernel_spmd

    nc = bacc.Bacc("TRN2", target_bir_lowering=False, num_devices=1)
    arrays = {name: np.ascontiguousarray(value) for name, value in {**inputs, **shape_constants()}.items()}
    args = {name: nc.dram_tensor(name, value.shape, mybir.dt.from_np(value.dtype), kind="ExternalInput").ap()
            for name, value in arrays.items()}
    out = nc.dram_tensor("out", (NTOK, D), F32, kind="ExternalOutput").ap()
    build(nc, args, out)
    result = run_bass_kernel_spmd(nc, [arrays], core_ids=[0])
    return result.results[0]["out"].reshape(NB, S, D)
```

```python
from contextlib import ExitStack

import numpy as np
import concourse.bass as bass
from concourse import mybir

F32 = mybir.dt.float32
BF16 = mybir.dt.bfloat16
U32 = mybir.dt.uint32
ALU = mybir.AluOpType
ACT = mybir.ActivationFunctionType
AX = mybir.AxisListType

P = 128
D = 128
NB, S = 4, 512
TT = S // P
NT = NB * TT
NTOK = NB * S
EPS = 1e-5

DEPTH, LEAF_W = 4, 64
LEAVES, NODES = 2 ** DEPTH, 2 ** DEPTH - 1
HCH = LEAVES * LEAF_W // P
OFF_PATH = 2.0 ** 60
SCALE0 = float(np.float32(1.0) / np.sqrt(D).astype(np.float32))
HEADS, DH = 16, 8
SCALE1 = float(DH ** (-0.25))
GROUPS = HEADS // 4
PARTS = 3
MROW = PARTS * PARTS * DH
KSTACK = 96
E1, F1, K1 = 16, 176, 2
F1R = F1 - P
CAP = int(np.ceil(1.25 * NTOK * K1 / E1))
NPAIR = E1 // 2
PT = 2 * CAP // P
SKIP = float(1 << 20)
NSTATE, DCONV = 16, 4
E2, H2 = 8, 256
E3 = 8

TREES = ("q", "k", "v")


def shape_constants():
    bf = mybir.dt.np(BF16)
    eye = np.eye(P, dtype=np.float32)
    center = (eye - np.float32(1.0 / D)).astype(np.float32)
    mean = np.full((P, P), 1.0 / D, np.float32)
    ones = np.ones((P, P), np.float32)
    path = np.zeros((P, 3, LEAVES), np.float32)
    for leaf in range(LEAVES):
        node = 0
        for step in range(DEPTH):
            bit = leaf >> (DEPTH - 1 - step) & 1
            for f in range(3):
                path[32 * f + node, f, leaf] = 1.0 if bit else -1.0
                if not bit:
                    path[32 * f + NODES, f, leaf] += 1.0
            node = 2 * node + 1 + bit
        path[[32 * f + NODES for f in range(3)], range(3), leaf] -= DEPTH
    leafpath = np.zeros((P, P), np.float32)
    for f in range(3):
        leafpath[:, 32 * f:32 * f + LEAVES] = path[:, f]
    offpath = np.zeros((P, 3, HCH, P), np.float32)
    for c in range(HCH):
        for row in range(P):
            offpath[:, :, c, row] = path[:, :, 2 * c + row // LEAF_W] * OFF_PATH
    pick = np.zeros((KSTACK, 32, P), np.float32)
    for n in range(32):
        pick[[n, 32 + n, 64 + n], n] = 1.0
    sumrow = np.zeros((P, 4), np.float32)
    sumrow[[32 * j + DH for j in range(4)], range(4)] = 1.0
    before = np.triu(np.ones((P, P), np.float32), 1)
    iota = np.broadcast_to(np.arange(16, dtype=np.float32), (P, 16)).copy()
    return {
        "c_eye": eye, "c_center": center, "c_mean": mean, "c_ones": ones, "c_leafpath": leafpath.astype(bf),
        "c_offpath": offpath.astype(bf), "c_pick": pick.astype(bf), "c_sumrow": sumrow,
        "c_before": before.astype(bf), "c_iota": iota,
    }


def build(nc, a, out):
    with ExitStack() as ctx:
        held = {}
        ctx.enter_context(nc.allow_non_contiguous_dma(reason="a bias goes one element to a partition"))

        def sb(name, shape, dt=F32):
            return ctx.enter_context(nc.sbuf_tensor("sb_" + name, shape, dt))

        def sem(name):
            if name not in held:
                held[name] = ctx.enter_context(nc.semaphore(name))
            return held[name]

        psum = ctx.enter_context(nc.psum_tensor("psum", [P, 8, S], F32))
        x = sb("x", [P, NB, S])
        h = sb("h", [P, NB, S])
        eye, center, mean, ones = (sb(n, [P, P]) for n in ("eye", "center", "mean", "ones"))
        sumrow, before, iota = sb("sumrow", [P, 4]), sb("before", [P, P], BF16), sb("iota", [P, 16])
        ones_b = sb("ones_b", [P, P], BF16)
        eye_b = sb("eye_b", [P, P], BF16)
        leafpath = sb("leafpath", [P, P], BF16)
        offpath = sb("offpath", [P, 3, HCH, P], BF16)
        pick = sb("pick", [KSTACK, 32, P], BF16)
        eps = sb("eps", [P, 1])
        one = sb("one", [P, 1])

        WV0, WO0, WQ1, WK1, WV1, WO1, WX2, WZ2, WOUT2, WSSM, WROUT3, WNODE = range(12)
        wT = sb("wT", [P, 12, D])
        nodeT = wT[:, WNODE, :]

        WIDE = sb("wide", [P, 6 * LEAVES * LEAF_W])
        w1 = [WIDE[:, f * 1024:(f + 1) * 1024] for f in range(3)]
        w2 = [WIDE[:, (3 + f) * 1024:(4 + f) * 1024].rearrange("p (c o) -> p c o", c=HCH) for f in range(3)]
        w1_2 = WIDE[:, 0:2048].rearrange("p (e n) -> p e n", e=E2)
        w2_2 = WIDE[:, 2048:4096].rearrange("p (e n) -> p e n", e=E2)
        w3_2 = WIDE[:, 4096:6144].rearrange("p (e k n) -> p e k n", e=E2, k=2)
        b1 = sb("b1", [P, 3, HCH])
        b2 = sb("b2", [P, 3, D])
        node_b = sb("node_b", [P, 1])

        woT = sb("woT", [P, GROUPS, D])
        bout1 = sb("bout1", [P, 1])
        router1, router1_row = sb("router1", [P, E1]), sb("router1_row", [P, E1])
        shared_gate_up = sb("shared_gate_up", [P, 2 * F1])
        shared_down = sb("shared_down", [P, 2, D])
        gate_up, down_ = sb("gate_up", [P, 2, 2, 2 * F1]), sb("down", [P, 2, 2, 2, D])
        v32 = sb("v32", [P, TT, HEADS, 32])
        qstack = sb("qstack", [P, HEADS, S], BF16)
        kstack = sb("kstack", [P, HEADS, S], BF16)

        xpad = sb("xpad", [P, NB, DCONV - 1 + S])
        conv_diag = sb("conv_diag", [P, DCONV, P])
        dtx_now = sb("dtx_now", [P, S])
        ygate = sb("ygate", [P, S])
        conv_w, conv_b = sb("conv_w", [P, DCONV]), sb("conv_b", [P, 1])
        dt_w, dt_b = sb("dt_w", [P, 1]), sb("dt_b", [P, 1])
        a_neg = sb("a_neg", [P, NSTATE])
        dt_rep = sb("dt_rep", [P, P])
        wg2 = sb("wg2", [P, E2])

        W_IN, W_GX, W_GA, W_OUT = range(4)
        w_3 = sb("w_3", [P, 4, D])
        b_3 = sb("b_3", [P, 4])
        a_par = sb("a_par", [P, 4])
        w_e3 = sb("w_e3", [P, E3, D])
        bias3 = sb("bias3", [P, D])
        router3_row = sb("router3_row", [P, E3])

        small = sb("small", [P, 8, TT])
        ln_std_t, ln_rstd_t = sb("ln_std_t", [P, NB, TT]), sb("ln_rstd_t", [P, NB, TT])
        wparts = sb("wparts", [KSTACK, NB, S], BF16)

        SCR = 15360
        scr = sb("scr", [P, SCR])

        def view(at, n, dt=F32):
            return scr[:, at:at + n] if dt is F32 else scr[:, at:at + n].bitcast(dt)

        squares = view(0, 2 * S).rearrange("p (r s) -> p r s", r=2)
        centered = view(2 * S, NB * S).rearrange("p (b s) -> p b s", b=NB)
        diag = view(6 * S, 2 * S).rearrange("p (r s) -> p r s", r=2)
        squares_one, centered_one, diag_one = (view(12800 + S * n, S) for n in range(3))
        wraw = view(4096, 12 * D).rearrange("p (n d) -> p n d", n=12)

        rows = view(8192, NB * TT * D).rearrange("p (t d) -> p t d", d=D)
        part_r, part_b = view(14336, S)[0:2 * NSTATE], view(14848, S // 2, BF16)[0:2 * NSTATE]
        hidden = view(0, HCH * S).rearrange("p (c s) -> p c s", c=HCH)
        qT0, kT0, v0 = view(4096, S), view(4608, S), view(5120, S)
        probs0 = view(5632, 2 * S).rearrange("p (r s) -> p r s", r=2)
        probsT0 = view(6656, TT * S).rearrange("p (k s) -> p k s", k=TT)
        gates = view(8704, S // 2, BF16)
        leaf = view(8960, S)
        token_sum, value_sum, attn0 = (sb(n, [P, NB]) for n in ("token_sum", "value_sum", "attn0"))

        expT = view(0, 4096).rearrange("p (r j s) -> p r j s", r=2, j=4)
        qparts = view(9856, 768, BF16).rearrange("p (i s) -> p i s", i=PARTS)
        kparts = view(10624, 768, BF16).rearrange("p (i s) -> p i s", i=PARTS)
        qrem, krem = view(11392, S), view(11904, S)
        vT1, vtok = view(6656, S), view(7168, S).rearrange("p (t h d) -> p t h d", t=TT, h=HEADS)
        headmax = view(7680, 2 * TT * 4).rearrange("p (r t j) -> p r t j", r=2, t=TT)
        maxrem = view(7712, 2 * TT * 4).rearrange("p (r t j) -> p r t j", r=2, t=TT)
        maxparts = view(7744, TT * PARTS * 4, BF16).rearrange("p (r t i j) -> p r t i j", r=2, t=TT, i=PARTS)
        sum_inv = view(7792, TT * 4).rearrange("p (t j) -> p t j", t=TT)
        max_rows = view(7808, S, BF16).rearrange("p (r s) -> p r s", r=2)
        head_raw, head_out = view(8320, S), view(8832, S)
        inv_rows = view(9344, S).rearrange("p (t j c) -> p t j c", t=TT, j=4)

        gact0 = view(0, 2 * S).rearrange("p (r s) -> p r s", r=2)
        prod0 = view(2048, 2 * S).rearrange("p (r s) -> p r s", r=2)
        hid0 = view(4096, 2 * S).rearrange("p (r s) -> p r s", r=2)

        def by_expert(at):
            return view(at, NT * E1).rearrange("p (t e) -> p t e", t=NT)

        def by_choice(n, dt=F32):
            return view(5632 + n * K1 * NT, K1 * NT, dt).rearrange("p (k t) -> p k t", k=K1)

        prob1, first1, second1, place_first, place_second = (by_expert(4096 + 256 * n) for n in range(5))
        top1 = view(5376, NT * 8).rearrange("p (t k) -> p t k", t=NT)
        top1_at = view(5504, NT * 8, U32).rearrange("p (t k) -> p t k", t=NT)
        expert_at, place, beyond, base, scatter_f, gather_f, pair_weight = (by_choice(n) for n in range(7))
        scatter_at, gather_at = by_choice(7, U32), by_choice(8, U32)
        peak1, sum1, sum1_inv = (view(5920 + NT * n, NT) for n in range(3))
        chosen1 = view(6016, NT * E1 // 2, BF16).rearrange("p (t e) -> p t e", t=NT)
        h_rows = view(6208, NT * D).rearrange("p (t d) -> p t d", t=NT)
        gathered = view(6208, 2 * NT * D).rearrange("p (t k d) -> p t k d", t=NT, k=K1)
        shared_act0, shared_act1, shared_hid0, shared_hid1 = (view(8256 + S * n, S) for n in range(4))
        x_in = view(10304, 2 * PT * D).rearrange("p (r t d) -> p r t d", r=2, t=PT)
        xT_in = view(11584, 2 * P).rearrange("p (r t) -> p r t", r=2)
        gate_act = view(11840, 2 * F1).rearrange("p (r f) -> p r f", r=2)
        hid_rows = view(12192, 4 * P).rearrange("p (r f) -> p r f", r=2)
        hidT = view(0, 4 * P).rearrange("p (r f t) -> p r f t", r=2, f=2)
        y_rows = view(512, 2 * PT * D).rearrange("p (r t d) -> p r t d", r=2, t=PT)
        zeros = view(10240, 2560)

        def batches(at):
            return view(at, NB * S).rearrange("p (b s) -> p b s", b=NB)

        def ring(at, n):
            return view(at, n * S).rearrange("p (r s) -> p r s", r=n)

        dt, dtx, zgate = (batches(NB * S * n) for n in range(3))
        xconv, dtl, dtv = batches(6144), batches(10240), batches(12288)
        RB, RC = 4, 4
        decay, drive, bcast_b, state = (ring(6144 + RB * S * n, RB) for n in range(4))
        read = ring(6144 + 4 * RB * S, 2)

        xw, gx, ga, dec, drv, st3 = (batches(NB * S * n) for n in range(6))
        weight2, weight_rem = (view(at, NT * E2).rearrange("p (t e) -> p t e", t=NT) for at in (5120, 5248))
        weight_parts = view(6208, NT * KSTACK // 2, BF16).rearrange("p (t n) -> p t n", t=NT)
        sel3 = batches(8192)
        RP = 4
        picked = ring(512, RP)

        q_bounce = nc.dram_tensor("q_bounce", [HEADS, PARTS, DH, S], BF16, kind="Internal").ap()
        k_bounce = nc.dram_tensor("k_bounce", [HEADS, PARTS, DH, S], BF16, kind="Internal").ap()

        expert_in = nc.dram_tensor("expert_in", [E1 * CAP, D], F32, kind="Internal").ap()
        expert_out = nc.dram_tensor("expert_out", [E1 * CAP, D], F32, kind="Internal").ap()

        x_ready, ln_done = sem("x_ready"), sem("ln_done")
        GTILES = 4 * TT
        STACKS, BOUNCES = 16 * PARTS * (1 + PARTS), 16 * 2 * PARTS
        stacked, max_stacked = ([sem(f"{n}{g}") for g in range(GROUPS)] for n in ("stacked", "max_stacked"))
        PAIR_LOADS = 16 * 5
        gathered_sem, x_loaded, y_stored = ([sem(f"{n}{g}") for g in range(m)] for n, m in
                                            (("gathered", NB), ("x_loaded", 2), ("y_stored", 2)))
        ATTN0, FFN0, ATTN1, FFN1, ATTN2, FFN2, ATTN3, FFN3 = range(8)

        def x_before(stage):
            return NB * (stage + 1)

        def outs_before(stage):
            return NB * (FFN0, FFN1, ATTN2, ATTN3).index(stage)

        setup = sem("setup")
        SETUP = ("eye_b", "hid1", "logits1", "chosen1", "places1", "dt_rep", "a_neg", "xpad", "parts2", "gap2", "apar", "apar_8",
                 "apar_16", "parts3")

        def run_tiles(engine, steps):
            per = 2 * PT

            def turn_of(u, begin):
                for c in range(per):
                    for k, step in enumerate(steps):
                        if step is None:
                            continue
                        if c >= k:
                            step(u, c - k, per * u + c - k, begin)
                        elif not begin:
                            step(u - 1, per + c - k, per * (u - 1) + per + c - k, False)

            turn_of(0, True)
            with engine.Fori(1, E1 // 4) as u:
                turn_of(u, False)
            last = E1 // 4 - 1
            for c in range(len(steps) - 1):
                for k, step in enumerate(steps):
                    if step is not None and k > c:
                        step(last, per + c - k, per * last + per + c - k, False)

        block = ctx.enter_context(nc.Block())

        @block.sync
        def _(sp):
            sp.dma_start(eye[:], a["c_eye"]).then_inc(sem("input_loaded"), 16)
            xr = a["L0_attn_x"].rearrange("b (t p) d -> p (b t) d", p=P)
            sp.dma_start(rows, xr).then_inc(sem("input_loaded"), 16)
            for t, n in ((center, "c_center"), (mean, "c_mean"), (ones, "c_ones")):
                sp.dma_start(t[:], a[n]).then_inc(sem("ln_consts"), 16)
            sp.wait_ge(sem("cleared"), 3)
            square = {WV0: a["L0_attn_w_qkv"][2 * D:3 * D, :], WO0: a["L0_attn_w_o"], WQ1: a["L1_attn_Wq"], WK1: a["L1_attn_Wk"],
                      WV1: a["L1_attn_Wv"], WO1: a["L1_attn_Wout"], WX2: a["L2_attn_in_proj_w"][0:D, :],
                      WZ2: a["L2_attn_in_proj_w"][D:2 * D, :], WOUT2: a["L2_attn_out_proj_w"], WSSM: a["L2_attn_x_proj_w"],
                      WROUT3: a["L3_ffn_router_weight"]}
            for n, src in square.items():
                sp.dma_start(wraw[0:src.shape[0], n, :], src).then_inc(sem("wraw_loaded"), 16)
            for f, name in enumerate(TREES):
                sp.dma_start(wraw[32 * f:32 * f + NODES, WNODE, :], a[f"L0_ffn_{name}_node_w"]).then_inc(sem("wraw_loaded"), 16)

            def column(name):
                return a[name].rearrange("(n o) -> n o", o=1)

            def load(group, dst, src):
                sp.dma_start(dst, src).then_inc(sem(group), 16)

            load("trees_loaded", leafpath[:], a["c_leafpath"])
            load("trees_loaded", offpath[:], a["c_offpath"])
            for f, name in enumerate(TREES):
                load("trees_loaded", node_b[32 * f:32 * f + NODES, :], column(f"L0_ffn_{name}_node_b"))
                load("trees_loaded", b2[32 * f:32 * f + LEAVES, f, :], a[f"L0_ffn_{name}_b2"])
                load("trees_loaded", b1[:, f, :], a[f"L0_ffn_{name}_b1"].rearrange("(c t) h -> (t h) c", t=2))
                load("trees_loaded", w1[f].rearrange("p (l h) -> p l h", h=LEAF_W), a[f"L0_ffn_{name}_w1"].rearrange("l d h -> d l h"))
                load("trees_loaded", w2[f], a[f"L0_ffn_{name}_w2"].rearrange("(c t) h o -> (t h) c o", t=2))
            load("attn1_loaded", sumrow[:], a["c_sumrow"])
            sp.wait_ge(sem("cleared"), N_CLEARED)
            load("attn1_loaded", bout1[:], column("L1_attn_bout"))
            load("ffn1_loaded", before[:], a["c_before"])
            load("ffn1_loaded", iota[:], a["c_iota"])
            load("ffn1_loaded", pick[:], a["c_pick"])
            load("ffn1_loaded", router1[:], a["L1_ffn_router_w"])
            load("ffn1_loaded", router1_row[0:1, :], a["L1_ffn_router_b"].rearrange("(o n) -> o n", o=1))
            for at, n in ((0, "gate"), (F1, "up")):
                load("ffn1_loaded", shared_gate_up[:, at:at + F1], a[f"L1_ffn_sw_{n}"])
            for k, (lo, hi) in enumerate(((0, P), (P, F1))):
                load("ffn1_loaded", shared_down[0:hi - lo, k, :], a["L1_ffn_sw_down"][lo:hi])
            table = expert_in.rearrange("(n p r) d -> n p (r d)", n=2, p=P)
            for n in range(2):
                sp.dma_start(table[n], zeros).then_inc(sem("table_cleared"), 16)
            load("attn2_loaded", conv_w[:], a["L2_attn_conv_w"].rearrange("d o k -> d (o k)"))
            load("attn2_loaded", conv_b[:], column("L2_attn_conv_b"))
            load("attn2_loaded", dt_w[:], a["L2_attn_dt_proj_w"])
            load("attn2_loaded", dt_b[:], column("L2_attn_dt_proj_b"))
            load("attn2_loaded", a_neg[:], a["L2_attn_A_log"])
            for n, name in enumerate(("in", "gx", "ga", "out")):
                load("attn3_loaded", w_3[:, n, :], a[f"L3_attn_W_{name}"])
                load("attn3_loaded", b_3[:, n:n + 1], column(f"L3_attn_b_{name}"))
            load("attn3_loaded", a_par[:, 0:1], column("L3_attn_a_param"))
            load("ffn3_loaded", w_e3[:], a["L3_ffn_weight"].rearrange("e d n -> d e n"))
            load("ffn3_loaded", bias3[0:E3, :], a["L3_ffn_bias"])
            load("ffn3_loaded", router3_row[0:1, :], a["L3_ffn_router_bias"].rearrange("(o n) -> o n", o=1))
            sp.wait_ge(sem("wT_ready"), 3)
            for g in range(GROUPS):
                for j in range(4):
                    head = 4 * g + j
                    load("woT_ready", woT[32 * j:32 * j + DH, g, :], wT[head * DH:(head + 1) * DH, WO1, :])

            def bounce(b):
                sp.wait_ge(sem("kparts_ready"), b + 1)
                for i in range(PARTS):
                    sp.dma_start(q_bounce[:, i], qparts[:, i, :]).then_inc(sem("bounced"), 16)
                    sp.dma_start(k_bounce[:, i], kparts[:, i, :]).then_inc(sem("bounced"), 16)
                sp.wait_ge(sem("bounced"), (b + 1) * BOUNCES)

            def stack(b, g):
                hs = slice(4 * g, 4 * g + 4)
                for j in range(PARTS):
                    rows_j = slice(PARTS * DH * j, PARTS * DH * (j + 1))
                    sp.dma_start(qstack[rows_j, hs, :], q_bounce[hs].rearrange("h i d s -> (i d) h s")).then_inc(stacked[g], 16)
                    for i in range(PARTS):
                        r = DH * (PARTS * j + i)
                        sp.dma_start(kstack[r:r + DH, hs, :], k_bounce[hs, j].rearrange("h d s -> d h s")).then_inc(stacked[g], 16)

            def stack_maxima(b, g):
                n = GROUPS * b + g
                sp.wait_ge(sem("max_rows_ready"), n + 1)
                for i in range(PARTS):
                    sp.dma_start(qstack[96 + i:97 + i, 4 * g:4 * g + 4, :],
                                 max_rows[4 * i:4 * i + 4, g % 2, :]).then_inc(max_stacked[g], 16)

            def stack_batch(b, first, last):
                for g in range(GROUPS):
                    n = GROUPS * b + g
                    if g == 0 or not last:
                        if g >= 1 or not first:
                            sp.wait_ge(sem("scoresT1"), n * GTILES)
                        stack(b, 3) if g == 0 else stack(b + 1, g - 1)
                    if g < GROUPS - 1 or not last:
                        stack_maxima(*((b, g + 1) if g < GROUPS - 1 else (b + 1, 0)))
                    if g == 0 and not last:
                        bounce(b + 1)

            bounce(0)
            for g in range(GROUPS - 1):
                stack(0, g)
            stack_maxima(0, 0)
            stack_batch(0, True, False)
            with sp.Fori(1, NB - 1) as b:
                stack_batch(b, False, False)
            stack_batch(NB - 1, False, True)

            sp.wait_ge(x_ready, x_before(ATTN1))
            load("ffn2_loaded", w1_2, a["L2_ffn_W1"].rearrange("e d n -> d e n"))
            load("ffn2_loaded", w2_2, a["L2_ffn_W2"].rearrange("e d n -> d e n"))
            load("ffn2_loaded", w3_2, a["L2_ffn_W3"].rearrange("e (k p) n -> p e k n", p=P))
            load("ffn2_loaded", wg2[:], a["L2_ffn_Wg"])

            pair_in = expert_in.rearrange("(q t p) d -> q p t d", q=NPAIR, t=PT)
            pair_out = expert_out.rearrange("(q t p) d -> q p t d", q=NPAIR, t=PT)

            def load_tokens(q):
                sp.dma_start(x_in[:, q % 2], pair_in[q]).then_inc(x_loaded[q % 2], 16)

            def load_gate_up(q):
                for at, n in ((0, "gate"), (F1, "up")):
                    sp.dma_start(gate_up[:, q % 2, :, at:at + F1],
                                 a[f"L1_ffn_w_{n}"][2 * q:2 * q + 2].rearrange("e d f -> d e f")).then_inc(x_loaded[q % 2], 16)

            def load_down(q):
                for k, (lo, hi) in enumerate(((0, P), (P, F1))):
                    sp.dma_start(down_[0:hi - lo, q % 2, :, k, :],
                                 a["L1_ffn_w_down"][2 * q:2 * q + 2].rearrange("e f d -> f e d")[lo:hi]).then_inc(x_loaded[q % 2], 16)

            for q in range(2):
                load_gate_up(q)
                load_down(q)
            sp.wait_ge(sem("scattered"), 16 * K1 * NT)
            for q in range(2):
                load_tokens(q)
            for q in range(2, NPAIR + 2):
                if q < NPAIR:
                    sp.wait_ge(sem("xT1_ready"), PT * (q - 1))
                    load_tokens(q)
                    sp.wait_ge(sem("hid1_ready"), PT * (q - 1))
                    load_gate_up(q)
                sp.wait_ge(sem("y1_ready"), PT * (q - 1))
                if q < NPAIR:
                    load_down(q)
                sp.dma_start(pair_out[q - 2], y_rows[:, q % 2]).then_inc(y_stored[q % 2], 16)

            orr = out.rearrange("(t p) d -> p t d", p=P)
            for b in range(NB):
                sp.wait_ge(sem("out_rows"), b + 1)
                sp.dma_start(orr[:, b * TT:(b + 1) * TT, :], rows[:, b * TT:(b + 1) * TT, :]).then_inc(sem("stored"), 16)
            sp.wait_ge(sem("stored"), 16 * NB)

        @block.gpsimd
        def _(pool):
            clears = [(wraw, 0.0), (b2[:], 0.0), (node_b[:], 0.0), (eps[:], EPS), (one[:], 1.0), (woT[:], 0.0),
                      (zeros, 0.0), (shared_down[:], 0.0), (down_[:], 0.0), (v32[:], 0.0), (qstack[64:P, :, :], 0.0), (kstack[64:96, :, :], 0.0),
                      (kstack[96:P, :, :], 1.0), (wparts[:], 0.0), (ones_b[:], 1.0), (bias3[:], 0.0), (router1_row[:], 0.0),
                      (router3_row[:], 0.0)]
            assert len(clears) == N_CLEARED - 1
            for n, (t, value) in enumerate(clears):
                if n >= 1:
                    pool.wait_ge(sem("cleared"), n)
                pool.memset(t, value).then_inc(sem("cleared"), 1)
            pool.wait_ge(sem("cleared"), N_CLEARED - 1)
            pool.memset(v32[:, :, :, DH], 1.0).then_inc(sem("cleared"), 1)

            pool.wait_ge(setup, SETUP.index("places1") + 1)
            pool.wait_ge(sem("h_rows_ready"), NB)
            pool.wait_ge(sem("table_cleared"), 32)
            for t in range(NT):
                for k in range(K1):
                    nc.gpsimd.indirect_dma_start(
                        out=expert_in, out_offset=bass.IndirectOffsetOnAxis(ap=scatter_at[:, k, t:t + 1], axis=0),
                        in_=h_rows[:, t, :], in_offset=None, bounds_check=E1 * CAP - 1, oob_is_err=False).then_inc(sem("scattered"), 16)
            for r in range(2):
                pool.wait_ge(y_stored[r], 16 * (NPAIR // 2))
            for t in range(NT):
                for k in range(K1):
                    nc.gpsimd.indirect_dma_start(
                        out=gathered[:, t, k, :], out_offset=None, in_=expert_out,
                        in_offset=bass.IndirectOffsetOnAxis(ap=gather_at[:, k, t:t + 1], axis=0)).then_inc(gathered_sem[t // TT], 16)

            with pool.Fori(0, NB) as b:
                for n in range(NSTATE):
                    if n == 0:
                        pool.wait_ge(sem("dtx_taken"), b + 1)
                    pool.wait_ge(sem("b_spread"), b * NSTATE + n + 1)
                    if n >= RB:
                        pool.wait_ge(sem("scanned"), b * NSTATE + n - RB + 1)
                    nc.gpsimd.tensor_tensor(drive[:, n % RB, :], dtx_now[:], bcast_b[:, n % RB, :], ALU.mult).then_inc(sem("drive_ready"), 1)

        @block.tensor
        def _(pe):
            def bank(n, m=S):
                return psum[:, n, 0:m]

            def mm(out_, w, r, start=True, stop=True, **kw):
                return nc.tensor.matmul(out_, w, r, start=start, stop=stop, **kw)

            def norm_steps(s):
                n = NB * s

                def subtract_mean(b):
                    pe.wait_ge(x_ready, n + b + 1)
                    if b >= 2:
                        pe.wait_ge(sem("ln_squared"), n + b - 1)
                    mm(bank(b % 2), center[:], x[:, b, :]).then_inc(sem("ln_centered"), 1)

                def variance(b):
                    pe.wait_ge(sem("ln_squared"), n + b + 1)
                    if b >= 2:
                        pe.wait_ge(sem("ln_std"), n + b - 1)
                    for t in range(TT):
                        m = mm(psum[:, 2 + b % 2, t:t + 1], squares[:, b % 2, t * P:(t + 1) * P], mean[:, 0:1],
                               skip_group_check=True)
                    m.then_inc(sem("ln_var"), 1)

                def spread_rstd(b):
                    pe.wait_ge(sem("ln_diag"), n + b + 1)
                    if b >= 2:
                        pe.wait_ge(ln_done, n + b - 1)
                    mm(bank(4 + b % 2), ones[:], diag[:, b % 2, :]).then_inc(sem("ln_spread"), 1)

                return subtract_mean, variance, spread_rstd

            def center_one(s, b, at):
                n = NB * s
                pe.wait_ge(x_ready, n + b + 1)
                if b >= 1:
                    pe.wait_ge(ln_done, n + b)
                mm(bank(at), center[:], x[:, b, :]).then_inc(sem("ln_centered"), 1)

            def variance_one(s, b, at):
                pe.wait_ge(sem("ln_squared"), NB * s + b + 1)
                for t in range(TT):
                    m = mm(psum[:, at, t:t + 1], squares_one[:, t * P:(t + 1) * P], mean[:, 0:1], skip_group_check=True)
                m.then_inc(sem("ln_var"), 1)

            def spread_one(s, b, at):
                pe.wait_ge(sem("ln_diag"), NB * s + b + 1)
                mm(bank(at), ones[:], diag_one).then_inc(sem("ln_spread"), 1)

            def layer_norm(s, beside={}):
                subtract_mean, variance, spread_rstd = norm_steps(s)
                if s == 0:
                    pe.wait_ge(sem("ln_consts"), 48)
                    pe.wait_ge(x_ready, NB)
                for b in range(NB + 2):
                    if b < NB:
                        subtract_mean(b)
                    if 1 <= b <= NB:
                        variance(b - 1)
                    if b >= 2:
                        if s == 0 and b == 2:
                            pe.wait_ge(sem("wT_ready"), 3)
                        spread_rstd(b - 2)
                    if b in beside:
                        beside[b]()

            def stage_norm(s, beside={}):
                layer_norm(s, beside)
                pe.wait_ge(ln_done, NB * s + NB)

            pe.wait_ge(sem("input_loaded"), 32)
            for b in range(NB):
                for t in range(TT):
                    m = nc.tensor.transpose(psum[:, b, t * P:(t + 1) * P], rows[:, b * TT + t, :], eye[:])
                m.then_inc(sem("x_turned"), 1)
            pe.wait_ge(sem("wraw_loaded"), 16 * (11 + 3))
            for k in range(3):
                for t in range(4):
                    m = nc.tensor.transpose(psum[:, 4 + k, t * P:(t + 1) * P], wraw[:, 4 * k + t, :], eye[:])
                m.then_inc(sem("w_turned"), 1)

            stage_norm(ATTN0)
            pe.wait_ge(sem("wT_ready"), 3)
            pe.wait_ge(sem("token_sums"), NB)
            mm(psum[:, 0, 0:NB], wT[:, WV0, :], token_sum[:]).then_inc(sem("attn0_mm"), 1)
            pe.wait_ge(sem("attn0_out"), 1)
            mm(psum[:, 1, 0:NB], wT[:, WO0, :], value_sum[:]).then_inc(sem("attn0_mm"), 1)

            def project_q(b):
                pe.wait_ge(ln_done, b + NB * ATTN1 + 1)
                mm(bank(6), wT[:, WQ1, :], h[:, b, :]).then_inc(sem("qkv1_done"), 1)

            def project_k(b):
                pe.wait_ge(sem("qparts_ready"), b + 1)
                mm(bank(6), wT[:, WK1, :], h[:, b, :]).then_inc(sem("qkv1_done"), 1)

            stage_norm(FFN0)
            pe.wait_ge(sem("trees_loaded"), 16 * (2 + 15))
            n_hid = 3 * HCH

            def nodes(b):
                if not (isinstance(b, int) and b == 0):
                    pe.wait_ge(sem("qkv0_ready"), b * 3 - 1)
                mm(bank(3), nodeT, h[:, b, :]).then_inc(sem("nodes0"), 1)

            def leaves(b):
                pe.wait_ge(sem("path_ready"), 2 * b + 1)
                mm(bank(4), leafpath[:], gates).then_inc(sem("nodes0"), 1)

            def out_of(b, i):
                f, c = divmod(i, HCH)
                pe.wait_ge(sem("hid_act" if i % 2 == 0 else "hid_dve"), b * (n_hid // 2) + i // 2 + 1)
                if f < 2:
                    m = mm(bank(3 + f), w2[f][:, c, :], hidden[:, c, :], c == 0, False)
                else:
                    for t in range(TT):
                        m = mm(psum[:, 5, t * D:(t + 1) * D], hidden[:, c, t * P:(t + 1) * P], w2[f][:, c, :],
                               c == 0 and t == 0, False, skip_group_check=True)
                if c < HCH - 1:
                    return
                if i == HCH - 1:
                    pe.wait_ge(sem("path_ready"), 2 * b + 2)
                if f < 2:
                    m = mm(bank(3 + f), b2[:, f, :], leaf, False, True)
                else:
                    for t in range(TT):
                        m = mm(psum[:, 5, t * D:(t + 1) * D], leaf[:, t * P:(t + 1) * P], b2[:, f, :],
                               False, t == TT - 1, skip_group_check=True)
                m.then_inc(sem("tree_out"), 1)

            def hidden_chunk(b, i):
                f, c = divmod(i, HCH)
                if i >= 3:
                    pe.wait_ge(sem("hid_act" if (i - 3) % 2 == 0 else "hid_dve"), b * (n_hid // 2) + (i - 3) // 2 + 1)
                mm(bank(i % 3), w1[f][:, c * P:(c + 1) * P], h[:, b, :], True, False)
                mm(bank(i % 3), offpath[:, f, c, :], gates, False, True).then_inc(sem("hidden0"), 1)

            def attend(b, t):
                pe.wait_ge(sem("probs0"), b * TT + t + 1)
                if t >= 2:
                    pe.wait_ge(sem("probsT0"), b * TT + t - 1)
                for k in range(TT):
                    m = nc.tensor.transpose(psum[:, (2, 6)[t % 2], k * P:(k + 1) * P], probs0[:, t % 2, k * P:(k + 1) * P], eye[:])
                m.then_inc(sem("probs_turned0"), 1)

            def trees(b, last):
                beside = {2: lambda: center_one(ATTN1, 0, 6), 4: lambda: variance_one(ATTN1, 0, 6),
                          7: lambda: spread_one(ATTN1, 0, 6), 9: lambda: project_q(0), 11: lambda: project_k(0),
                          14: lambda: center_one(ATTN1, 1, 6), 17: lambda: variance_one(ATTN1, 1, 6),
                          20: lambda: spread_one(ATTN1, 1, 6), 22: lambda: center_one(ATTN1, 2, 6)} if last else {}
                for i in range(2, n_hid):
                    hidden_chunk(b, i)
                    out_of(b, i - 2)
                    if i in beside:
                        if i == 14:
                            pe.wait_ge(sem("kparts_ready"), 1)
                        beside[i]()
                out_of(b, n_hid - 2)
                if last:
                    variance_one(ATTN1, 2, 6)
                out_of(b, n_hid - 1)
                if last:
                    spread_one(ATTN1, 2, 6)
                    pe.wait_ge(ln_done, NB * ATTN1 + 3)
                pe.wait_ge(sem("qkv0_ready"), b * 3 + 2)
                for t in range(TT):
                    if t >= 2:
                        pe.wait_ge(sem("exp0"), b * TT + t - 1)
                    mm(bank(t % 2), qT0[:, t * P:(t + 1) * P], kT0).then_inc(sem("scores0"), 1)
                    if t == 1 and not last:
                        nodes(b + 1)
                    if t >= 1:
                        attend(b, t - 1)
                if not last:
                    leaves(b + 1)
                attend(b, TT - 1)
                if not last:
                    hidden_chunk(b + 1, 0)
                    hidden_chunk(b + 1, 1)
                pe.wait_ge(sem("probsT0"), b * TT + TT)
                pe.wait_ge(sem("qkv0_ready"), b * 3 + 3)
                pe.wait_ge(x_ready, b + x_before(FFN0))
                for k in range(TT):
                    m = mm(bank(7), v0[:, k * D:(k + 1) * D], probsT0[:, k, :], k == 0, k == TT - 1)
                m.then_inc(sem("batch_out"), 1)

            nodes(0)
            leaves(0)
            hidden_chunk(0, 0)
            hidden_chunk(0, 1)
            with pe.Fori(0, NB - 1) as b:
                trees(b, False)
            trees(NB - 1, True)

            def project_v(b):
                pe.wait_ge(sem("kparts_ready"), b + 1)
                mm(bank(6), wT[:, WV1, :], h[:, b, :]).then_inc(sem("qkv1_done"), 1)

            def turn_v(b):
                pe.wait_ge(sem("vT_ready"), b + 1)
                for t in range(TT):
                    m = nc.tensor.transpose(psum[:, 6, t * P:(t + 1) * P], vT1[:, t * P:(t + 1) * P], eye[:])
                m.then_inc(sem("v_turned"), 1)

            def score_for_max(b, g, i, first, ring=2):
                j, t = divmod(i, TT)
                n = GROUPS * b + g
                if i == 0:
                    pe.wait_ge(stacked[g], (b + 1) * STACKS)
                if i >= ring or not first:
                    pe.wait_ge(sem("maxed"), n * GTILES + i - ring + 1)
                mm(bank(i % ring), qstack[0:96, 4 * g + j, t * P:(t + 1) * P], kstack[0:96, 4 * g + j, :]).then_inc(sem("scores1"), 1)

            def turn_maxima(b, g):
                n = GROUPS * b + g
                pe.wait_ge(sem("maxparts_ready"), n + 1)
                for t in range(TT):
                    m = mm(psum[0:4 * PARTS, 6, t * P:(t + 1) * P], maxparts[:, g % 2, t].rearrange("p i j -> p (i j)"), eye_b[:],
                           skip_group_check=True)
                m.then_inc(sem("max_turned"), 1)

            def score(b, g, i, first):
                kt, j = divmod(i, 4)
                n = GROUPS * b + g
                if i == 0:
                    pe.wait_ge(max_stacked[g], (b + 1) * 16 * PARTS)
                if i >= 2 or not first:
                    pe.wait_ge(sem("exp1"), n * GTILES + i - 1)
                else:
                    pe.wait_ge(sem("maxed"), 2 * GTILES)
                mm(bank(2 + i % 2), kstack[:, 4 * g + j, kt * P:(kt + 1) * P], qstack[:, 4 * g + j, :]).then_inc(sem("scoresT1"), 1)

            def values(b, g, kt, first):
                n = GROUPS * b + g
                pe.wait_ge(sem("exp1"), n * GTILES + 4 * kt + 4)
                if kt == 0:
                    pe.wait_ge(sem("v_ready"), n + 1)
                    if not first:
                        pe.wait_ge(sem("head_raw_ready"), n)
                for j in range(4):
                    m = mm(psum[32 * j:32 * j + 32, 4, :], v32[:, kt, 4 * g + j, :], expT[:, kt % 2, j, :],
                           kt == 0, kt == TT - 1, tile_position=(0, 32 * j))
                m.then_inc(sem("keys_added"), 1)

            def sum_by_token(b, g):
                n = GROUPS * b + g
                pe.wait_ge(sem("head_raw_ready"), n + 1)
                if not (isinstance(b, int) and n == 0):
                    pe.wait_ge(sem("head_out_ready"), n)
                for t in range(TT):
                    m = mm(psum[:, 5, 4 * t:4 * t + 4], head_raw[:, t * P:(t + 1) * P], sumrow[:], skip_group_check=True)
                m.then_inc(sem("sums_by_token"), 1)

            def spread_inverse(b, g):
                n = GROUPS * b + g
                pe.wait_ge(sem("inv_rows_ready"), n + 1)
                for t in range(TT):
                    m = mm(psum[:, 5, t * P:(t + 1) * P], inv_rows[:, t].rearrange("p j c -> p (j c)"), eye[:], skip_group_check=True)
                m.then_inc(sem("inverse_spread"), 1)

            def project(b, g):
                n = GROUPS * b + g
                pe.wait_ge(sem("head_out_ready"), n + 1)
                if g == 0:
                    pe.wait_ge(x_ready, b + x_before(ATTN1))
                mm(bank(7), woT[:, g, :], head_out, g == 0, g == GROUPS - 1).then_inc(sem("attn_out1"), 1)

            def attend_batch(b, first, last):
                for g in range(GROUPS):
                    begin = first and g == 0
                    prev = (b, g - 1) if g >= 1 else (b - 1, GROUPS - 1)
                    ahead = (b, g + 2) if g < 2 else (b + 1, g - 2)
                    for kt in range(TT):
                        for j in range(4):
                            i = 4 * kt + j
                            score(b, g, i, begin)
                            if g < 2 or not last:
                                score_for_max(*ahead, i, False)
                            if j == 1 and kt >= 1:
                                values(b, g, kt - 1, begin)
                            elif j == 1 and not begin:
                                values(*prev, TT - 1, False)
                        if kt == 0 and (g < GROUPS - 1 or not last):
                            if g == 2 and not last:
                                pe.wait_ge(sem("vtok_ready"), b + 2)
                            if g == 1 and not last:
                                pe.wait_ge(sem("kparts_ready"), b + 2)
                            turn_maxima(*((b, g + 1) if g < GROUPS - 1 else (b + 1, 0)))
                        if kt == 1 and not begin:
                            sum_by_token(*prev)
                        if kt == 2 and not begin:
                            spread_inverse(*prev)
                        if kt == 3 and not begin:
                            project(*prev)
                        if not last:
                            if g == 0 and kt == 1:
                                pe.wait_ge(sem("max_rows_ready"), GROUPS * b + 2)
                                project_q(b + 1)
                            if g == 0 and kt == 2:
                                project_k(b + 1)
                            if g == 1 and kt == 1:
                                pe.wait_ge(sem("max_rows_ready"), GROUPS * b + 3)
                                project_v(b + 1)
                            if g == 1 and kt == 3:
                                turn_v(b + 1)

            pe.wait_ge(sem("attn1_loaded"), 32)
            pe.wait_ge(sem("woT_ready"), 256)
            pe.wait_ge(setup, SETUP.index("eye_b") + 1)
            project_v(0)
            beside = {1: lambda: center_one(ATTN1, NB - 1, 5), 3: lambda: turn_v(0), 7: lambda: variance_one(ATTN1, NB - 1, 5),
                      12: lambda: spread_one(ATTN1, NB - 1, 5)}
            for g in range(2):
                for i in range(GTILES):
                    score_for_max(0, g, i, g == 0, 4)
                    if g == 0 and i in beside:
                        beside[i]()
                    if g == 1 and i == 3:
                        pe.wait_ge(sem("vtok_ready"), 1)
                        turn_maxima(0, 0)
            pe.wait_ge(ln_done, NB * ATTN1 + NB)
            attend_batch(0, True, False)
            with pe.Fori(1, NB - 1) as b:
                attend_batch(b, False, False)
            attend_batch(NB - 1, False, True)
            end = (NB - 1, GROUPS - 1)
            values(*end, TT - 1, False)
            sum_by_token(*end)
            spread_inverse(*end)
            project(*end)

            def score_tokens(w, n, at, row=None):
                if row is not None:
                    mm(psum[:, at, 0:NT * n].rearrange("p (t e) -> p t e", t=NT), ones[:],
                       row[:].unsqueeze(1).broadcast_to([P, NT, n]), True, False, skip_group_check=True)
                for t in range(NT):
                    m = mm(psum[:, at, t * n:(t + 1) * n], h[:, t // TT, t % TT * P:(t % TT + 1) * P], w,
                           t == 0 and row is None, t == NT - 1, skip_group_check=True)
                m.then_inc(sem("route_scored"), 1)

            def turn_weights(k, at):
                pe.wait_ge(sem("route_weights"), k)
                for b in range(NB):
                    for t in range(TT):
                        m = mm(psum[0:KSTACK, at + b, t * P:(t + 1) * P], weight_parts[:, b * TT + t, :], eye_b[:], skip_group_check=True)
                    m.then_inc(sem("route_weights_turned"), 1)
                pe.wait_ge(sem("route_parts"), NB * k)

            stage_norm(FFN1)
            pe.wait_ge(sem("ffn1_loaded"), 16 * N_FFN1)
            score_tokens(router1[:], E1, 0, router1_row)
            for b in range(NB):
                if b >= 2:
                    pe.wait_ge(sem("h_rows_ready"), b - 1)
                for t in range(TT):
                    m = nc.tensor.transpose(psum[:, 1 + b % 2, t * P:(t + 1) * P], h[:, b, t * P:(t + 1) * P], eye[:])
                m.then_inc(sem("h_turned"), 1)

            def shared_up(b):
                if b >= 1:
                    pe.wait_ge(sem("shared_hid"), b)
                for n, (lo, hi) in enumerate(((0, P), (P, F1), (F1, F1 + P), (F1 + P, 2 * F1))):
                    m = mm(psum[0:hi - lo, 3 + n, :], shared_gate_up[:, lo:hi], h[:, b, :])
                    if n % 2 == 1:
                        m.then_inc(sem("shared_up"), 1)

            def shared_out(b):
                if b >= 1:
                    pe.wait_ge(sem("shared_added"), b)
                mm(bank(7), eye[:], h[:, b, :], True, False)
                pe.wait_ge(sem("shared_hid"), b + 1)
                mm(bank(7), shared_down[:, 0, :], shared_hid0, False, False)
                mm(bank(7), shared_down[:, 1, :], shared_hid1, False, True).then_inc(sem("shared_out"), 1)

            shared_up(0)
            pe.wait_ge(setup, SETUP.index("chosen1") + 1)
            mm(psum[:, 0, 0:NT * E1], before[:], chosen1.rearrange("p t e -> p (t e)"), True, False, skip_group_check=True)
            for t in range(NT - 1):
                later = NT - 1 - t
                m = mm(psum[:, 0, (t + 1) * E1:NT * E1].rearrange("p (t e) -> p t e", t=later), ones_b[:],
                       chosen1[:, t, :].unsqueeze(1).broadcast_to([P, later, E1]), False, t == NT - 2, skip_group_check=True)
            m.then_inc(sem("counted1"), 1)
            shared_out(0)
            for b in range(1, NB):
                shared_up(b)
                shared_out(b)

            def tile(c):
                p, j = divmod(c, PT)
                if j == PT // 2:
                    return ((slice(0, P // 2), p, 0), (slice(P // 2, P), p, 1))
                return ((slice(0, P), p, j // (PT // 2 + 1)),)

            def turn_in(u, c, n, begin):
                r = c // PT
                if c % PT == 0:
                    pe.wait_ge(x_loaded[r], PAIR_LOADS * (u + 1))
                if c >= 2 or not begin:
                    pe.wait_ge(sem("xT1_ready"), n - 1)
                nc.tensor.transpose(psum[:, c % 2, 0:P], x_in[:, r, c % PT, :], eye[:]).then_inc(sem("x1_turned"), 1)

            def gate_and_up(u, c, n, begin):
                pe.wait_ge(sem("xT1_ready"), n + 1)
                if c >= 2 or not begin:
                    pe.wait_ge(sem("hid1_ready"), n - 1)
                for rows_, p, e in tile(c):
                    m = mm(psum[rows_, 2 + c % 2, 0:2 * F1], xT_in[:, c % 2, rows_], gate_up[:, p, e, :],
                           tile_position=(0, rows_.start))
                m.then_inc(sem("up1_done"), 1)

            def turn_hidden(u, c, n, begin):
                pe.wait_ge(sem("hid1_ready"), n + 1)
                if c >= 2 or not begin:
                    pe.wait_ge(sem("hidT1_ready"), n - 1)
                for k in range(2):
                    m = nc.tensor.transpose(psum[:, 4 + c % 2, k * P:(k + 1) * P], hid_rows[:, c % 2, k * P:(k + 1) * P], eye[:])
                m.then_inc(sem("hid1_turned"), 1)

            def down(u, c, n, begin):
                pe.wait_ge(sem("hidT1_ready"), n + 1)
                if c >= 2 or not begin:
                    pe.wait_ge(sem("y1_ready"), n - 1)
                for rows_, p, e in tile(c):
                    for k in range(2):
                        m = mm(psum[rows_, 6 + c % 2, 0:D], hidT[:, c % 2, k, rows_], down_[:, p, e, k, :], k == 0, k == 1,
                               tile_position=(0, rows_.start))
                m.then_inc(sem("y1_done"), 1)

            pe.wait_ge(sem("shared_added"), NB)
            run_tiles(pe, (turn_in, gate_and_up, turn_hidden, down))

            pe.wait_ge(sem("ffn1_loaded"), 16 * N_FFN1)
            pe.wait_ge(setup, SETUP.index("xpad") + 1)

            subtract_mean, variance, spread_rstd = norm_steps(ATTN2)

            def turn_back(b):
                pe.wait_ge(sem("combined"), b + 1)
                if b >= 2:
                    pe.wait_ge(x_ready, x_before(FFN1) + b - 1)
                for t in range(TT):
                    m = nc.tensor.transpose(psum[:, 6 + b % 2, t * P:(t + 1) * P], gathered[:, b * TT + t, 0, :], eye[:])
                m.then_inc(sem("batch_out"), 1)

            def project_in(b):
                pe.wait_ge(ln_done, NB * ATTN2 + b + 1)
                mm(bank(b % 2), wT[:, WX2, :], h[:, b, :])
                mm(bank(2 + b % 2), wT[:, WZ2, :], h[:, b, :]).then_inc(sem("proj2_done"), 1)

            def convolve(b):
                pe.wait_ge(sem("xin_ready"), b + 1)
                if b >= 2:
                    pe.wait_ge(sem("xconv_ready"), b - 1)
                for k in range(DCONV):
                    m = mm(bank(4 + b % 2), conv_diag[:, k, :], xpad[:, b, k:k + S], k == 0, k == DCONV - 1)
                m.then_inc(sem("conv_ready"), 1)

            def state_inputs(b):
                pe.wait_ge(sem("xconv_ready"), b + 1)
                mm(bank(2 + b % 2), wT[:, WSSM, :], xconv[:, b, :])
                mm(bank(4 + b % 2), dt_rep[:], xconv[:, b, :]).then_inc(sem("ssm_done"), 1)

            turn_back(0)
            for b in range(NB + 1):
                if b < NB:
                    subtract_mean(b)
                if b >= 1:
                    project_in(b - 1)
                    convolve(b - 1)
                if b + 1 < NB:
                    turn_back(b + 1)
                if b < NB:
                    if b >= 2:
                        pe.wait_ge(sem("bc_parts"), b - 1)
                    variance(b)
                if b >= 1:
                    state_inputs(b - 1)
                if b < NB:
                    spread_rstd(b)
            pe.wait_ge(sem("bc_parts"), NB)

            def add_state(b, n):
                pe.wait_ge(sem("read_ready"), b * NSTATE + n + 1)
                mm(bank(6), eye[:], read[:, n % 2, :], n == 0, n == NSTATE - 1).then_inc(sem("y_added"), 1)

            def project_out(b):
                pe.wait_ge(sem("ygate_ready"), b + 1)
                mm(bank(7), wT[:, WOUT2, :], ygate[:]).then_inc(sem("batch_out"), 1)

            def states(b, begin):
                for n in range(NSTATE):
                    if n >= 2 or not begin:
                        pe.wait_ge(sem("b_spread"), b * NSTATE + n - 1)
                    mm(bank(n % 2), pick[:, n, :], wparts[:, b, :]).then_inc(sem("b_done"), 1)
                    if n >= RC or not begin:
                        pe.wait_ge(sem("read_ready"), b * NSTATE + n - RC + 1)
                    mm(bank(2 + n % RC), pick[:, NSTATE + n, :], wparts[:, b, :]).then_inc(sem("c_done"), 1)
                    if n == RC and not begin:
                        project_out(b - 1)
                    if n >= RC:
                        add_state(b, n - RC)
                    elif not begin:
                        add_state(b - 1, NSTATE + n - RC)

            states(0, True)
            with pe.Fori(1, NB) as b:
                states(b, False)
            for n in range(NSTATE - RC, NSTATE):
                add_state(NB - 1, n)
            project_out(NB - 1)

            stage_norm(FFN2)
            pe.wait_ge(sem("ffn2_loaded"), 64)
            score_tokens(wg2[:], E2, 6)
            NC = 2 * E2

            def up2(b, i):
                e, k = divmod(i, 2)
                s0 = 2 * (i % 2)
                mm(bank(s0), w1_2[:, e, k * P:(k + 1) * P], h[:, b, :])
                mm(bank(s0 + 1), w2_2[:, e, k * P:(k + 1) * P], h[:, b, :]).then_inc(sem("up2_done"), 1)

            for i in range(2):
                up2(0, i)
            turn_weights(1, 4)

            def down2(b, i):
                e, k = divmod(i, 2)
                pe.wait_ge(sem("hid2_ready"), b * NC + i + 1)
                m = mm(bank(7), w3_2[:, e, k, :], hid0[:, i % 2, :], i == 0, i == NC - 1)
                m.then_inc(sem("down2_done"), 1)

            def experts2(b, begin):
                for i in range(NC):
                    e, k = divmod(i, 2)
                    if i >= 2 or not begin:
                        pe.wait_ge(sem("gact2_ready"), b * NC + i - 1)
                        pe.wait_ge(sem("prod2_ready"), b * NC + i - 1)
                        up2(b, i)
                    if k == 0:
                        if e >= 2 or not begin:
                            pe.wait_ge(sem("hid2_ready"), b * NC + 2 * (e - 1))
                        mm(bank(4 + e % 2), pick[:, e, :], wparts[:, b, :]).then_inc(sem("weights_spread"), 1)
                    if i == 1 and not begin:
                        pe.wait_ge(x_ready, x_before(FFN2) + b)
                    if i >= 1:
                        down2(b, i - 1)
                    elif not begin:
                        down2(b - 1, NC - 1)

            experts2(0, True)
            with pe.Fori(1, NB) as b:
                experts2(b, False)
            down2(NB - 1, NC - 1)

            stage_norm(ATTN3)
            pe.wait_ge(sem("attn3_loaded"), 16 * 9)
            for b in range(NB):
                mm(bank(b), w_3[:, W_IN, :], h[:, b, :]).then_inc(sem("proj3_done"), 1)
            for b in range(NB):
                pe.wait_ge(sem("xw_ready"), b + 1)
                if b >= 2:
                    pe.wait_ge(sem("ga_ready"), b - 1)
                mm(bank(4 + b % 2), w_3[:, W_GX, :], xw[:, b, :])
                mm(bank(6 + b % 2), w_3[:, W_GA, :], xw[:, b, :]).then_inc(sem("proj3_done"), 1)
            for b in range(NB):
                pe.wait_ge(sem("state3_ready"), b + 1)
                mm(bank((0, 1, 6, 7)[b]), w_3[:, W_OUT, :], st3[:, b, :]).then_inc(sem("batch_out"), 1)

            stage_norm(FFN3)
            pe.wait_ge(sem("ffn3_loaded"), 48)
            score_tokens(wT[:, WROUT3, 0:E3], E3, 0, router3_row)
            turn_weights(2, 1)

            def add_expert(b, e):
                pe.wait_ge(sem("picked_ready"), b * E3 + e + 1)
                mm(bank(7), w_e3[:, e, :], picked[:, e % RP, :], False, e == E3 - 1).then_inc(sem("y3_added"), 1)

            def experts3(b, begin):
                for e in range(E3):
                    if e >= RP or not begin:
                        pe.wait_ge(sem("picked_ready"), b * E3 + e - RP + 1)
                    mm(bank(3 + e % RP), pick[:, e, :], wparts[:, b, :]).then_inc(sem("weights_spread"), 1)
                    if e == 2:
                        if not begin:
                            pe.wait_ge(x_ready, x_before(FFN3) + b)
                        mm(bank(7), bias3[0:E3, :], sel3[0:E3, b, :], True, False)
                    if e >= 2:
                        add_expert(b, e - 2)
                    elif not begin:
                        add_expert(b - 1, E3 - 2 + e)

            experts3(0, True)
            with pe.Fori(1, NB) as b:
                experts3(b, False)
            for e in range(E3 - 2, E3):
                add_expert(NB - 1, e)

            pe.wait_ge(x_ready, x_before(FFN3 + 1))
            for b in range(NB):
                for t in range(TT):
                    m = nc.tensor.transpose(psum[:, b, t * D:(t + 1) * D], x[:, b, t * P:(t + 1) * P], eye[:])
                m.then_inc(sem("x_turned"), 1)

        @block.scalar
        def _(act):
            def bank(n, m=S):
                return psum[:, n, 0:m]

            def f(out_, in_, func, **kw):
                return nc.scalar.activation(out_, in_, func, **kw)

            def center_and_square(n, b):
                act.wait_ge(sem("ln_centered"), n + b + 1)
                if b >= 2:
                    act.wait_ge(sem("ln_var"), n + b - 1)
                f(centered[:, b, :], bank(b % 2), ACT.Copy)
                f(squares[:, b % 2, :], bank(b % 2), ACT.Square).then_inc(sem("ln_squared"), 1)

            def deviation(n, b):
                act.wait_ge(sem("ln_var"), n + b + 1)
                f(ln_std_t[:, b, :], psum[:, 2 + b % 2, 0:TT], ACT.Sqrt, bias=eps[:]).then_inc(sem("ln_std"), 1)

            def center_and_square_one(s, b, at):
                act.wait_ge(sem("ln_centered"), NB * s + b + 1)
                f(centered_one, bank(at), ACT.Copy)
                f(squares_one, bank(at), ACT.Square).then_inc(sem("ln_squared"), 1)

            def deviation_one(s, b, at):
                act.wait_ge(sem("ln_var"), NB * s + b + 1)
                f(ln_std_t[:, b, :], psum[:, at, 0:TT], ACT.Sqrt, bias=eps[:]).then_inc(sem("ln_std"), 1)

            def layer_norm(s):
                n = NB * s
                for b in range(NB + 1):
                    if b < NB:
                        center_and_square(n, b)
                    if b >= 1:
                        deviation(n, b - 1)

            act.wait_ge(sem("cleared"), 5)
            for k in range(3):
                act.wait_ge(sem("w_turned"), k + 1)
                f(wT[:, 4 * k:4 * k + 4, :], bank(4 + k).rearrange("p (n d) -> p n d", n=4), ACT.Copy).then_inc(sem("wT_ready"), 1)

            layer_norm(ATTN0)
            act.wait_ge(sem("attn0_mm"), 1)
            f(value_sum[:], psum[:, 0, 0:NB], ACT.Copy).then_inc(sem("attn0_out"), 1)
            act.wait_ge(sem("attn0_mm"), 2)
            f(attn0[:], psum[:, 1, 0:NB], ACT.Copy).then_inc(sem("attn0_out"), 1)

            layer_norm(FFN0)
            act.wait_ge(sem("trees_loaded"), 16 * (2 + 15))
            n_hid = 3 * HCH

            def trees(b, last):
                beside = {2: lambda: center_and_square_one(ATTN1, 0, 6), 4: lambda: deviation_one(ATTN1, 0, 6),
                          14: lambda: center_and_square_one(ATTN1, 1, 6), 18: lambda: deviation_one(ATTN1, 1, 6),
                          22: lambda: center_and_square_one(ATTN1, 2, 6)} if last else {}
                for i in range(0, n_hid, 2):
                    t, c = divmod(i, HCH)
                    act.wait_ge(sem("hidden0"), b * n_hid + i + 1)
                    if i >= HCH and c == 0:
                        act.wait_ge(sem("tree_out"), b * 3 + t)
                    f(hidden[:, c, :], bank(i % 3), ACT.Relu, bias=b1[:, t, c:c + 1]).then_inc(sem("hid_act"), 1)
                    if i in beside:
                        beside[i]()
                    if i in (HCH + 2, 2 * HCH + 2):
                        act.wait_ge(sem("tree_out"), b * 3 + t)
                        f((qT0, kT0)[t - 1], bank(2 + t), ACT.Copy).then_inc(sem("qkv0_ready"), 1)
                if last:
                    deviation_one(ATTN1, 2, 6)
                act.wait_ge(sem("tree_out"), b * 3 + 3)
                f(v0, bank(5), ACT.Copy).then_inc(sem("qkv0_ready"), 1)

                def copy_turned(t):
                    act.wait_ge(sem("probs_turned0"), b * TT + t + 1)
                    f(probsT0[:, :, t * P:(t + 1) * P], bank((2, 6)[t % 2]).rearrange("p (k q) -> p k q", k=TT),
                      ACT.Copy).then_inc(sem("probsT0"), 1)

                for t in range(TT):
                    act.wait_ge(sem("shift0"), b * TT + t + 1)
                    if t >= 2:
                        act.wait_ge(sem("probs_turned0"), b * TT + t - 1)
                    f(probs0[:, t % 2, :], bank(t % 2), ACT.Exp, bias=small[:, 1, t:t + 1], scale=SCALE0,
                      accum_out=small[:, 2, t:t + 1]).then_inc(sem("exp0"), 1)
                    if t >= 1:
                        copy_turned(t - 1)
                copy_turned(TT - 1)

            with act.Fori(0, NB - 1) as b:
                trees(b, False)
            trees(NB - 1, True)

            def copy_vT(b):
                act.wait_ge(sem("qkv1_done"), 3 * b + 3)
                f(vT1, bank(6), ACT.Copy).then_inc(sem("vT_ready"), 1)

            def copy_max_rows(b, g):
                n = GROUPS * b + g
                act.wait_ge(sem("max_turned"), n + 1)
                if not (isinstance(b, int) and n < 2):
                    act.wait_ge(max_stacked[(g + 2) % GROUPS], (b + g // 2) * 16 * PARTS)
                f(max_rows[0:4 * PARTS, g % 2, :], psum[0:4 * PARTS, 6, :], ACT.Copy).then_inc(sem("max_rows_ready"), 1)

            def copy_heads(b, g):
                n = GROUPS * b + g
                act.wait_ge(sem("keys_added"), (n + 1) * TT)
                if not (isinstance(b, int) and n == 0):
                    act.wait_ge(sem("head_out_ready"), n)
                f(head_raw, bank(4), ACT.Copy).then_inc(sem("head_raw_ready"), 1)

            def exp_batch(b, first, last):
                for g in range(GROUPS):
                    n = GROUPS * b + g
                    begin = first and g == 0
                    for kt in range(TT):
                        for j in range(4):
                            i = 4 * kt + j
                            act.wait_ge(sem("scoresT1"), n * GTILES + i + 1)
                            if j == 0 and (kt >= 2 or not begin):
                                act.wait_ge(sem("keys_added"), n * TT + kt - 1)
                            f(expT[:, kt % 2, j, :], bank(2 + i % 2), ACT.Exp).then_inc(sem("exp1"), 1)
                        if kt == 0 and not begin:
                            copy_heads(*((b, g - 1) if g >= 1 else (b - 1, GROUPS - 1)))
                        if kt == 0 and (g < GROUPS - 1 or not last):
                            copy_max_rows(*((b, g + 1) if g < GROUPS - 1 else (b + 1, 0)))
                        if kt == 2 and g == 1 and not last:
                            copy_vT(b + 1)

            copy_vT(0)
            center_and_square_one(ATTN1, NB - 1, 5)
            deviation_one(ATTN1, NB - 1, 5)
            copy_max_rows(0, 0)
            exp_batch(0, True, False)
            with act.Fori(1, NB - 1) as b:
                exp_batch(b, False, False)
            exp_batch(NB - 1, False, True)
            copy_heads(NB - 1, GROUPS - 1)

            layer_norm(FFN1)
            act.wait_ge(setup, SETUP.index("logits1") + 1)
            f(prob1, prob1, ACT.Exp).then_inc(sem("act_setup"), 1)
            for b in range(NB):
                act.wait_ge(sem("h_turned"), b + 1)
                f(h_rows[:, b * TT:(b + 1) * TT, :], bank(1 + b % 2).rearrange("p (t d) -> p t d", t=TT),
                  ACT.Copy).then_inc(sem("h_rows_ready"), 1)
            for b in range(NB):
                act.wait_ge(sem("shared_up"), 2 * b + 1)
                if b >= 1:
                    act.wait_ge(sem("shared_hid"), b)
                f(shared_act0, bank(3), ACT.Silu).then_inc(sem("shared_gate"), 1)
                f(shared_act1[0:F1R], psum[0:F1R, 4, :], ACT.Silu).then_inc(sem("shared_gate"), 1)

            def copy_in(u, c, n, begin):
                act.wait_ge(sem("x1_turned"), n + 1)
                if c >= 2 or not begin:
                    act.wait_ge(sem("up1_done"), n - 1)
                f(xT_in[:, c % 2, :], psum[:, c % 2, 0:P], ACT.Copy).then_inc(sem("xT1_ready"), 1)

            def gate(u, c, n, begin):
                act.wait_ge(sem("up1_done"), n + 1)
                if c >= 2 or not begin:
                    act.wait_ge(sem("hid1_ready"), n - 1)
                f(gate_act[:, c % 2, :], psum[:, 2 + c % 2, 0:F1], ACT.Silu).then_inc(sem("gate1_ready"), 1)

            def copy_out(u, c, n, begin):
                r = c // PT
                act.wait_ge(sem("y1_done"), n + 1)
                if c % PT == 0 and not begin:
                    act.wait_ge(y_stored[r], 16 * u)
                f(y_rows[:, r, c % PT, :], psum[:, 6 + c % 2, 0:D], ACT.Copy).then_inc(sem("y1_ready"), 1)

            run_tiles(act, (copy_in, gate, None, copy_out))

            act.wait_ge(sem("attn2_loaded"), 80)
            f(a_neg[:], a_neg[:], ACT.Exp).then_inc(sem("act_setup"), 1)
            act.wait_ge(setup, SETUP.index("a_neg") + 1)

            def conv_silu(b):
                act.wait_ge(sem("conv_ready"), b + 1)
                f(xconv[:, b, :], bank(4 + b % 2), ACT.Silu, bias=conv_b[:]).then_inc(sem("xconv_ready"), 1)

            def softplus(b):
                n = 3 * b
                for i in range(2):
                    act.wait_ge(sem("dtv_ready"), b + i + 1)
                    f(dtl[:, b + i, :], dtv[:, b + i, :], ACT.Abs).then_inc(sem("dtl_step"), 1)
                for i in range(2):
                    act.wait_ge(sem("dtl_step"), n + i + 1)
                    f(dtl[:, b + i, :], dtl[:, b + i, :], ACT.Exp, scale=-1.0).then_inc(sem("dtl_step"), 1)
                for i in range(2):
                    act.wait_ge(sem("dtl_step"), n + 2 + i + 1)
                    f(dtl[:, b + i, :], dtl[:, b + i, :], ACT.Ln, bias=one[:]).then_inc(sem("dtl_step"), 1)

            for b in range(NB + 1):
                if b < NB:
                    center_and_square(NB * ATTN2, b)
                if b >= 1:
                    act.wait_ge(sem("proj2_done"), b)
                    f(xpad[:, b - 1, DCONV - 1:], bank((b - 1) % 2), ACT.Copy).then_inc(sem("xin_ready"), 1)
                    f(zgate[:, b - 1, :], bank(2 + (b - 1) % 2), ACT.Silu).then_inc(sem("zgate_ready"), 1)
                    conv_silu(b - 1)
                if b < NB:
                    deviation(NB * ATTN2, b)
                if b == NB - 1:
                    softplus(0)
            softplus(NB - 2)
            act.wait_ge(sem("dtx_ready"), NB)

            def states(b, begin):
                if not begin:
                    act.wait_ge(sem("drive_ready"), b * NSTATE)
                f(dtx_now[:], dtx[:, b, :], ACT.Copy).then_inc(sem("dtx_taken"), 1)
                for n in range(NSTATE):
                    r = n % RB
                    act.wait_ge(sem("b_done"), b * NSTATE + n + 1)
                    if n >= RB or not begin:
                        act.wait_ge(sem("drive_ready"), b * NSTATE + n - RB + 1)
                        act.wait_ge(sem("scanned"), b * NSTATE + n - RB + 1)
                    f(bcast_b[:, r, :], bank(n % 2), ACT.Copy).then_inc(sem("b_spread"), 1)
                    f(decay[:, r, :], dt[:, b, :], ACT.Exp, scale=a_neg[:, n:n + 1]).then_inc(sem("decay_ready"), 1)

            states(0, True)
            with act.Fori(1, NB) as b:
                states(b, False)

            def copy_parts(k, at):
                for b in range(NB):
                    act.wait_ge(sem("route_weights_turned"), NB * (k - 1) + b + 1)
                    if k == 2:
                        f(sel3[0:E3, b, :], psum[0:E3, at + b, :], ACT.Copy)
                    f(wparts[:, b, :], psum[0:KSTACK, at + b, :], ACT.Copy).then_inc(sem("route_parts"), 1)

            layer_norm(FFN2)
            act.wait_ge(setup, SETUP.index("gap2") + 1)
            f(sum1, peak1, ACT.Exp).then_inc(sem("act_setup"), 1)
            copy_parts(1, 4)
            NC = 2 * E2
            with act.Fori(0, NB) as b:
                for i in range(NC):
                    act.wait_ge(sem("up2_done"), b * NC + i + 1)
                    if i >= 2:
                        act.wait_ge(sem("prod2_ready"), b * NC + i - 1)
                    f(gact0[:, i % 2, :], bank(2 * (i % 2)), ACT.Silu).then_inc(sem("gact2_ready"), 1)

            layer_norm(ATTN3)
            act.wait_ge(sem("attn3_loaded"), 16 * 9)
            f(a_par[:, 1:2], a_par[:, 0:1], ACT.Abs).then_inc(sem("act_setup"), 1)
            act.wait_ge(sem("act_setup"), 4)
            f(a_par[:, 1:2], a_par[:, 1:2], ACT.Exp, scale=-1.0).then_inc(sem("act_setup"), 1)
            act.wait_ge(sem("act_setup"), 5)
            f(a_par[:, 1:2], a_par[:, 1:2], ACT.Ln, bias=one[:]).then_inc(sem("act_setup"), 1)
            act.wait_ge(setup, SETUP.index("apar_16") + 1)
            for b in range(NB):
                act.wait_ge(sem("proj3_done"), b + 1)
                f(xw[:, b, :], bank(b), ACT.Identity, bias=b_3[:, W_IN:W_IN + 1]).then_inc(sem("xw_ready"), 1)
            for b in range(NB):
                act.wait_ge(sem("proj3_done"), NB + b + 1)
                f(gx[:, b, :], bank(4 + b % 2), ACT.Sigmoid, bias=b_3[:, W_GX:W_GX + 1]).then_inc(sem("gx_ready"), 1)
                f(ga[:, b, :], bank(6 + b % 2), ACT.Sigmoid, bias=b_3[:, W_GA:W_GA + 1]).then_inc(sem("ga_ready"), 1)
            for b in range(NB):
                act.wait_ge(sem("ga_ready"), b + 1)
                f(dec[:, b, :], ga[:, b, :], ACT.Exp, scale=a_par[:, 2:3])
                f(drv[:, b, :], ga[:, b, :], ACT.Exp, scale=a_par[:, 3:4]).then_inc(sem("drv_step"), 1)
            for b in range(NB):
                act.wait_ge(sem("drv_step"), b + 1)
                f(drv[:, b, :], drv[:, b, :], ACT.Sqrt, scale=-1.0, bias=one[:]).then_inc(sem("drv_ready"), 1)

            layer_norm(FFN3)
            copy_parts(2, 1)

            for b in range(NB):
                act.wait_ge(sem("x_turned"), NB + b + 1)
                f(rows[:, b * TT:(b + 1) * TT, :], bank(b).rearrange("p (t d) -> p t d", t=TT), ACT.Copy).then_inc(sem("out_rows"), 1)

        @block.vector
        def _(dve):
            v = nc.vector

            def bank(n, m=S):
                return psum[:, n, 0:m]

            class Steps:

                def __init__(self, name, b, per, before=0):
                    self.sem, self.b, self.per, self.n, self.before = sem(name), b, per, 0, before

                def did(self, instruction):
                    instruction.then_inc(self.sem, 1)
                    self.n += 1

                def wait(self):
                    dve.wait_ge(self.sem, self.b * self.per + (self.before + self.n))

                def then(self, instruction_of):
                    self.wait()
                    self.did(instruction_of())

                def end(self):
                    assert self.n == self.per, self.n

            Q_STEPS, R1_STEPS, R2_STEPS, R3_STEPS = NB * PARTS, 55, 44, 35

            def spread_factors(n, b):
                dve.wait_ge(sem("ln_std"), n + b + 1)
                v.reciprocal(ln_rstd_t[:, b, :], ln_std_t[:, b, :]).then_inc(sem("ln_rstd"), 1)
                dve.wait_ge(sem("ln_rstd"), n + b + 1)
                if b >= 2:
                    dve.wait_ge(sem("ln_spread"), n + b - 1)
                for t in range(TT):
                    m = v.tensor_scalar(diag[:, b % 2, t * P:(t + 1) * P], eye[:], ln_rstd_t[:, b, t:t + 1], None, ALU.mult)
                m.then_inc(sem("ln_diag"), 1)

            def normalize(n, b):
                dve.wait_ge(sem("ln_spread"), n + b + 1)
                v.tensor_tensor(h[:, b, :], centered[:, b, :], bank(4 + b % 2), ALU.mult).then_inc(ln_done, 1)

            def layer_norm(s, beside={}):
                n = NB * s
                for b in range(NB + 1):
                    if b < NB:
                        spread_factors(n, b)
                    if b >= 1:
                        normalize(n, b - 1)
                    if b in beside:
                        beside[b]()

            def spread_factors_one(s, b):
                n = NB * s
                dve.wait_ge(sem("ln_std"), n + b + 1)
                v.reciprocal(ln_rstd_t[:, b, :], ln_std_t[:, b, :]).then_inc(sem("ln_rstd"), 1)
                dve.wait_ge(sem("ln_rstd"), n + b + 1)
                for t in range(TT):
                    m = v.tensor_scalar(diag_one[:, t * P:(t + 1) * P], eye[:], ln_rstd_t[:, b, t:t + 1], None, ALU.mult)
                m.then_inc(sem("ln_diag"), 1)

            def normalize_one(s, b, at):
                dve.wait_ge(sem("ln_spread"), NB * s + b + 1)
                v.tensor_tensor(h[:, b, :], centered_one, bank(at), ALU.mult).then_inc(ln_done, 1)

            MAX_STEPS = NB * GROUPS * PARTS + NB

            def add_to_x(b, n):
                v.tensor_tensor(x[:, b, :], bank(n), x[:, b, :], ALU.add).then_inc(x_ready, 1)

            for b in range(NB):
                dve.wait_ge(sem("x_turned"), b + 1)
                v.tensor_copy(x[:, b, :], bank(b)).then_inc(x_ready, 1)

            def sum_tokens(b):
                dve.wait_ge(ln_done, b + 1)
                v.reduce_sum(token_sum[:, b:b + 1], h[:, b, :], AX.X).then_inc(sem("token_sums"), 1)

            layer_norm(ATTN0, {2: lambda: sum_tokens(0), 3: lambda: sum_tokens(1)})
            for b in range(2, NB):
                sum_tokens(b)
            dve.wait_ge(sem("attn0_out"), 2)
            for b in range(NB):
                v.tensor_scalar(x[:, b, :], x[:, b, :], attn0[:, b:b + 1], None, ALU.add).then_inc(x_ready, 1)

            def cut(b, tag, src, scale, parts, rem):
                st = Steps(tag + "_step", b, PARTS)
                st.did(v.tensor_scalar(parts(0), src, scale, None, ALU.mult))
                st.then(lambda: v.scalar_tensor_tensor(rem, src, scale, parts(0), ALU.mult, ALU.subtract))
                st.then(lambda: v.tensor_copy(parts(1), rem))
                st.wait()
                st.end()
                v.tensor_tensor(parts(2), rem, parts(1), ALU.subtract).then_inc(sem(tag + "parts_ready"), 1)

            def cut_q(b):
                dve.wait_ge(sem("qkv1_done"), 3 * b + 1)
                if not (isinstance(b, int) and b == 0):
                    dve.wait_ge(sem("bounced"), b * BOUNCES)
                cut(b, "q", bank(6), SCALE1, lambda i: qparts[:, i, :], qrem)

            def cut_k(b):
                dve.wait_ge(sem("qkv1_done"), 3 * b + 2)
                if not (isinstance(b, int) and b == 0):
                    dve.wait_ge(sem("bounced"), b * BOUNCES)
                    dve.wait_ge(stacked[GROUPS - 1], b * STACKS)
                cut(b, "k", bank(6), SCALE1, lambda i: kparts[:, i, :], krem)

            v.tensor_copy(eye_b[:], eye[:]).then_inc(setup, 1)
            layer_norm(FFN0)
            dve.wait_ge(sem("trees_loaded"), 16 * (2 + 15))
            n_hid = 3 * HCH

            def go_right(b):
                dve.wait_ge(sem("nodes0"), 2 * b + 1)
                v.tensor_scalar(gates, bank(3), node_b[:], 0.0, ALU.add, ALU.is_ge).then_inc(sem("path_ready"), 1)

            def reach_leaves(b):
                dve.wait_ge(sem("nodes0"), 2 * b + 2)
                v.tensor_scalar(leaf, bank(4), 0.0, None, ALU.is_equal).then_inc(sem("path_ready"), 1)

            def relu(b, i):
                t, c = divmod(i, HCH)
                dve.wait_ge(sem("hidden0"), b * n_hid + i + 1)
                if t >= 1 and c == 1:
                    dve.wait_ge(sem("tree_out"), b * 3 + t)
                v.tensor_scalar(hidden[:, c, :], bank(i % 3), b1[:, t, c:c + 1], 0.0, ALU.add, ALU.max).then_inc(sem("hid_dve"), 1)

            def trees(b, last):
                beside = {5: lambda: spread_factors_one(ATTN1, 0), 7: lambda: normalize_one(ATTN1, 0, 6), 9: lambda: cut_q(0),
                          11: lambda: cut_k(0), 19: lambda: spread_factors_one(ATTN1, 1),
                          21: lambda: normalize_one(ATTN1, 1, 6), 23: lambda: spread_factors_one(ATTN1, 2)} if last else {}
                if last:
                    dve.wait_ge(sem("table_cleared"), 32)
                for i in range(3, n_hid, 2):
                    relu(b, i)
                    if i in beside:
                        beside[i]()
                if last:
                    normalize_one(ATTN1, 2, 6)
                for t in range(TT):
                    dve.wait_ge(sem("scores0"), b * TT + t + 1)
                    v.reduce_max(small[:, 0, t:t + 1], bank(t % 2), AX.X).then_inc(sem("softmax0_step"), 1)
                    dve.wait_ge(sem("softmax0_step"), 2 * (b * TT + t) + 1)
                    v.tensor_scalar(small[:, 1, t:t + 1], small[:, 0, t:t + 1], -SCALE0, None, ALU.mult).then_inc(sem("shift0"), 1)
                    if t == 1 and not last:
                        go_right(b + 1)
                    dve.wait_ge(sem("exp0"), b * TT + t + 1)
                    v.reciprocal(small[:, 3, t:t + 1], small[:, 2, t:t + 1]).then_inc(sem("softmax0_step"), 1)
                    dve.wait_ge(sem("softmax0_step"), 2 * (b * TT + t) + 2)
                    v.tensor_scalar(probs0[:, t % 2, :], probs0[:, t % 2, :], small[:, 3, t:t + 1], None, ALU.mult).then_inc(sem("probs0"), 1)
                if not last:
                    reach_leaves(b + 1)
                    relu(b + 1, 1)
                dve.wait_ge(sem("batch_out"), b + outs_before(FFN0) + 1)
                add_to_x(b, 7)

            go_right(0)
            reach_leaves(0)
            relu(0, 1)
            with dve.Fori(0, NB - 1) as b:
                trees(b, False)
            trees(NB - 1, True)

            def values_by_token(b):
                dve.wait_ge(sem("v_turned"), b + 1)
                v.tensor_copy(vtok, bank(6).rearrange("p (t h d) -> p t h d", t=TT, h=HEADS)).then_inc(sem("vtok_ready"), 1)

            def place_values(b, g):
                hs = slice(4 * g, 4 * g + 4)
                dve.wait_ge(sem("vtok_ready"), b + 1)
                if not (isinstance(b, int) and b == 0):
                    dve.wait_ge(sem("keys_added"), (GROUPS * (b - 1) + g + 1) * TT)
                v.tensor_copy(v32[:, :, hs, 0:DH], vtok[:, :, hs, :]).then_inc(sem("v_ready"), 1)

            def maximum(b, g, i, ring=2):
                j, t = divmod(i, TT)
                dve.wait_ge(sem("scores1"), (GROUPS * b + g) * GTILES + i + 1)
                v.reduce_max(headmax[:, g % 2, t, j:j + 1], bank(i % ring), AX.X).then_inc(sem("maxed"), 1)

            def cut_maxima(b, g):
                n = GROUPS * b + g
                dve.wait_ge(sem("maxed"), (n + 1) * GTILES)
                if not (isinstance(b, int) and n < 2):
                    dve.wait_ge(sem("max_turned"), n - 1)
                cut(n, "max", headmax[:, g % 2], -1.0, lambda i: maxparts[:, g % 2, :, i, :], maxrem[:, g % 2])

            def invert_sums(b, g):
                n = GROUPS * b + g
                dve.wait_ge(sem("sums_by_token"), n + 1)
                v.reciprocal(sum_inv, psum[:, 5, 0:4 * TT].rearrange("p (t j) -> p t j", t=TT)).then_inc(sem("sum_inv_ready"), 1)
                dve.wait_ge(sem("sum_inv_ready"), n + 1)
                v.tensor_copy(inv_rows, sum_inv.unsqueeze(3).broadcast_to([P, TT, 4, 32])).then_inc(sem("inv_rows_ready"), 1)

            def divide_heads(b, g):
                n = GROUPS * b + g
                dve.wait_ge(sem("inverse_spread"), n + 1)
                if not (isinstance(b, int) and n == 0):
                    dve.wait_ge(sem("attn_out1"), n)
                v.tensor_tensor(head_out, head_raw, bank(5), ALU.mult).then_inc(sem("head_out_ready"), 1)

            def add_attention(b):
                dve.wait_ge(sem("attn_out1"), GROUPS * b + GROUPS)
                v.scalar_tensor_tensor(x[:, b, :], bank(7), bout1[:], x[:, b, :], ALU.add, ALU.add).then_inc(x_ready, 1)

            def maxima_batch(b, first, last):
                for g in range(GROUPS):
                    begin = first and g == 0
                    prev = (b, g - 1) if g >= 1 else (b - 1, GROUPS - 1)
                    ahead = (b, g + 2) if g < 2 else (b + 1, g - 2)
                    for kt in range(TT):
                        if g < 2 or not last:
                            for j in range(4):
                                maximum(*ahead, 4 * kt + j)
                        if kt == 0:
                            if g == 0:
                                place_values(b, GROUPS - 1)
                            if not last:
                                if g == 2:
                                    values_by_token(b + 1)
                                    place_values(b + 1, 0)
                                    place_values(b + 1, 1)
                                if g == 3:
                                    place_values(b + 1, 2)
                        if kt == 1:
                            if not begin:
                                invert_sums(*prev)
                            if g == 0 and not last:
                                cut_q(b + 1)
                        if kt == 2 and not begin:
                            divide_heads(*prev)
                        if kt == 3:
                            if g < 2 or not last:
                                cut_maxima(*ahead)
                            if g == 0 and not begin:
                                add_attention(b - 1)
                            if g == 0 and not last:
                                cut_k(b + 1)

            dve.wait_ge(sem("cleared"), N_CLEARED)
            for g in range(2):
                for i in range(GTILES):
                    maximum(0, g, i, 4)
                    if g == 0 and i == 4:
                        values_by_token(0)
                        for n in range(GROUPS - 1):
                            place_values(0, n)
                    if g == 0 and i == 8:
                        spread_factors_one(ATTN1, NB - 1)
                    if g == 0 and i == 13:
                        normalize_one(ATTN1, NB - 1, 5)
                cut_maxima(0, g)
            maxima_batch(0, True, False)
            with dve.Fori(1, NB - 1) as b:
                maxima_batch(b, False, False)
            maxima_batch(NB - 1, False, True)
            invert_sums(NB - 1, GROUPS - 1)
            divide_heads(NB - 1, GROUPS - 1)
            add_attention(NB - 1)

            def each(per_tile, n):
                return per_tile.unsqueeze(2).broadcast_to([P, NT, n])

            def two_best(st, scores, n):
                for t in range(NT):
                    st.did(v.max(top1[:, t, :], scores[:, t, :]))
                st.wait()
                for t in range(NT):
                    st.did(v.max_index(top1_at[:, t, :], top1[:, t, :], scores[:, t, :]))
                st.then(lambda: v.tensor_copy(expert_at, top1_at[:, :, 0:K1].rearrange("p t k -> p k t")))
                st.wait()
                experts = iota[:, 0:n].unsqueeze(1).broadcast_to([P, NT, n])
                for k, dst in enumerate((first1, second1)):
                    st.did(v.tensor_tensor(dst[:, :, 0:n], experts, each(expert_at[:, k, :], n), ALU.is_equal))
                st.wait()

            layer_norm(FFN1)
            dve.wait_ge(sem("ffn1_loaded"), 16 * N_FFN1)
            dve.wait_ge(ln_done, NB * FFN1 + NB)
            v.memset(shared_hid1, 0.0)
            v.memset(hid_rows, 0.0).then_inc(setup, 1)
            dve.wait_ge(sem("route_scored"), 1)
            scores1 = psum[:, 0, 0:NT * E1].rearrange("p (t e) -> p t e", t=NT)

            st = Steps("q_step", 0, R1_STEPS, Q_STEPS)
            st.did(v.reduce_max(peak1, scores1, AX.X))
            st.wait()
            v.tensor_tensor(prob1, scores1, each(peak1, E1), ALU.subtract).then_inc(setup, 1)
            dve.wait_ge(sem("act_setup"), 1)
            st.did(v.reduce_sum(sum1, prob1, AX.X))
            st.then(lambda: v.reciprocal(sum1_inv, sum1))
            st.then(lambda: v.tensor_tensor(prob1, prob1, each(sum1_inv, E1), ALU.mult))
            st.wait()
            two_best(st, prob1, E1)
            v.tensor_tensor(chosen1, first1, second1, ALU.add).then_inc(setup, 1)
            st.did(v.tensor_tensor(sum1, top1[:, :, 0], top1[:, :, 1], ALU.add))
            st.then(lambda: v.tensor_scalar(sum1, sum1, 1e-9, None, ALU.add))
            st.then(lambda: v.reciprocal(sum1_inv, sum1))
            st.wait()
            for k in range(K1):
                st.did(v.tensor_tensor(pair_weight[:, k, :], top1[:, :, k], sum1_inv, ALU.mult))
            st.did(v.tensor_scalar(base, expert_at, float(CAP), None, ALU.mult))

            def shared_products(b):
                for n, (src, gates_, dst, rr) in enumerate(((5, shared_act0, shared_hid0, slice(0, P)),
                                                            (6, shared_act1, shared_hid1, slice(0, F1R)))):
                    dve.wait_ge(sem("shared_gate"), 2 * b + n + 1)
                    dve.wait_ge(sem("shared_up"), 2 * b + 2)
                    if b >= 1:
                        dve.wait_ge(sem("shared_out"), b)
                    m = v.tensor_tensor(dst[rr], psum[rr, src, :], gates_[rr], ALU.mult)
                m.then_inc(sem("shared_hid"), 1)

            def add_shared(b):
                dve.wait_ge(sem("shared_out"), b + 1)
                v.tensor_tensor(x[:, b, :], bank(7), x[:, b, :], ALU.add).then_inc(sem("shared_added"), 1)

            shared_products(0)
            dve.wait_ge(sem("counted1"), 1)
            for oh, dst in ((first1, place_first), (second1, place_second)):
                st.did(v.tensor_tensor(dst, scores1, oh, ALU.mult))
            st.wait()
            for k, src in enumerate((place_first, place_second)):
                st.did(v.reduce_sum(place[:, k, :], src, AX.X))
            st.then(lambda: v.tensor_scalar(beyond, place, float(CAP), None, ALU.is_ge))
            st.did(v.scalar_tensor_tensor(gather_f, place, float(CAP - 1), base, ALU.min, ALU.add))
            st.did(v.scalar_tensor_tensor(pair_weight, place, float(CAP), pair_weight, ALU.is_lt, ALU.mult))
            st.did(v.tensor_tensor(scatter_f, place, base, ALU.add))
            st.then(lambda: v.scalar_tensor_tensor(scatter_f, beyond, SKIP, scatter_f, ALU.mult, ALU.add))
            st.then(lambda: v.tensor_copy(gather_at, gather_f))
            st.end()
            v.tensor_copy(scatter_at, scatter_f).then_inc(setup, 1)
            for b in range(1, NB):
                add_shared(b - 1)
                shared_products(b)
            add_shared(NB - 1)

            def hidden_rows(u, c, n, begin):
                dve.wait_ge(sem("gate1_ready"), n + 1)
                if c >= 2 or not begin:
                    dve.wait_ge(sem("hid1_turned"), n - 1)
                v.tensor_tensor(hid_rows[:, c % 2, 0:F1], psum[:, 2 + c % 2, F1:2 * F1], gate_act[:, c % 2, :],
                                ALU.mult).then_inc(sem("hid1_ready"), 1)

            def copy_hidden(u, c, n, begin):
                dve.wait_ge(sem("hid1_turned"), n + 1)
                if c >= 2 or not begin:
                    dve.wait_ge(sem("y1_done"), n - 1)
                v.tensor_copy(hidT[:, c % 2], psum[:, 4 + c % 2, 0:2 * P].rearrange("p (f t) -> p f t", f=2)).then_inc(sem("hidT1_ready"), 1)

            run_tiles(dve, (None, hidden_rows, copy_hidden, None))

            def combine(b):
                dve.wait_ge(gathered_sem[b], 16 * K1 * TT)
                for t in range(b * TT, (b + 1) * TT):
                    m = v.tensor_scalar(gathered[:, t, 0, :], gathered[:, t, 0, :], pair_weight[:, 0, t:t + 1], None, ALU.mult)
                m.then_inc(sem("max_step"), 1)
                dve.wait_ge(sem("max_step"), NB * GROUPS * PARTS + b + 1)
                for t in range(b * TT, (b + 1) * TT):
                    m = v.scalar_tensor_tensor(gathered[:, t, 0, :], gathered[:, t, 1, :], pair_weight[:, 1, t:t + 1],
                                               gathered[:, t, 0, :], ALU.mult, ALU.add)
                m.then_inc(sem("combined"), 1)

            def add_routed(b):
                dve.wait_ge(sem("batch_out"), b + outs_before(FFN1) + 1)
                add_to_x(b, 6 + b % 2)

            dve.wait_ge(sem("wT_ready"), 3)
            v.tensor_scalar(dt_rep[:], ones[:], wT[:, WSSM, 2 * NSTATE:2 * NSTATE + 1], None, ALU.mult).then_inc(setup, 1)
            dve.wait_ge(sem("act_setup"), 2)
            v.tensor_scalar(a_neg[:], a_neg[:], -1.0, None, ALU.mult).then_inc(setup, 1)
            for k in range(DCONV):
                v.tensor_scalar(conv_diag[:, k, :], eye[:], conv_w[:, k:k + 1], None, ALU.mult)
            v.memset(xpad[:, :, 0:DCONV - 1], 0.0).then_inc(setup, 1)

            def state_inputs(b):
                dve.wait_ge(sem("ssm_done"), b + 1)
                v.tensor_scalar(dtv[:, b, :], bank(4 + b % 2), dt_w[:], dt_b[:], ALU.mult, ALU.add).then_inc(sem("dtv_ready"), 1)
                bcp = psum[0:2 * NSTATE, 2 + b % 2, :]
                st = Steps("k_step", b, 4, NB * PARTS)
                st.did(v.tensor_copy(wparts[0:32, b, :], bcp))
                st.then(lambda: v.tensor_tensor(part_r, bcp, wparts[0:32, b, :], ALU.subtract))
                st.then(lambda: v.tensor_copy(part_b, part_r))
                st.then(lambda: v.tensor_copy(wparts[32:64, b, :], part_b))
                st.end()
                v.tensor_tensor(wparts[64:96, b, :], part_r, part_b, ALU.subtract).then_inc(sem("bc_parts"), 1)

            combine(0)
            add_routed(0)
            def steps_taken(b):
                for i in range(2):
                    dve.wait_ge(sem("dtl_step"), 3 * b + 4 + i + 1)
                    dve.wait_ge(sem("dtv_ready"), b + i + 1)
                    v.scalar_tensor_tensor(dt[:, b + i, :], dtv[:, b + i, :], 0.0, dtl[:, b + i, :], ALU.max,
                                           ALU.add).then_inc(sem("dt_ready"), 1)
                for i in range(2):
                    dve.wait_ge(sem("dt_ready"), b + i + 1)
                    v.tensor_tensor(dtx[:, b + i, :], dt[:, b + i, :], xconv[:, b + i, :], ALU.mult).then_inc(sem("dtx_ready"), 1)

            for b in range(NB + 2):
                if b >= 2:
                    state_inputs(b - 2)
                if b + 1 < NB:
                    combine(b + 1)
                if b < NB:
                    spread_factors(NB * ATTN2, b)
                if b + 1 < NB:
                    add_routed(b + 1)
                if b < NB:
                    normalize(NB * ATTN2, b)
                if b == NB:
                    steps_taken(0)
            steps_taken(NB - 2)

            def scan(b, n, begin):
                i = b * NSTATE + n
                dve.wait_ge(sem("decay_ready"), i + 1)
                dve.wait_ge(sem("drive_ready"), i + 1)
                if n >= RB or not begin:
                    dve.wait_ge(sem("read_ready"), i - RB + 1)
                v.tensor_tensor_scan(state[:, n % RB, :], decay[:, n % RB, :], drive[:, n % RB, :], 0.0,
                                     ALU.mult, ALU.add).then_inc(sem("scanned"), 1)

            def read_state(b, n, begin):
                i = b * NSTATE + n
                dve.wait_ge(sem("c_done"), i + 1)
                if n >= 2 or not begin:
                    dve.wait_ge(sem("y_added"), i - 1)
                dve.wait_ge(sem("scanned"), i + 1)
                v.tensor_tensor(read[:, n % 2, :], bank(2 + n % RC), state[:, n % RB, :], ALU.mult).then_inc(sem("read_ready"), 1)

            def gate_batch(b, begin):
                dve.wait_ge(sem("y_added"), b * NSTATE + NSTATE)
                dve.wait_ge(sem("zgate_ready"), NB)
                v.tensor_tensor(ygate[:], bank(6), zgate[:, b, :], ALU.mult).then_inc(sem("ygate_ready"), 1)

            def add_batch(b):
                dve.wait_ge(sem("batch_out"), b + outs_before(ATTN2) + 1)
                add_to_x(b, 7)

            def states(b, begin):
                for n in range(NSTATE + 1):
                    if n == 2 and not begin:
                        gate_batch(b - 1, False)
                    if n < NSTATE:
                        scan(b, n, begin)
                    if n >= 1:
                        read_state(b, n - 1, begin)
                    if n == 2 * RC and not begin:
                        add_batch(b - 1)

            states(0, True)
            with dve.Fori(1, NB) as b:
                states(b, False)
            gate_batch(NB - 1, False)
            add_batch(NB - 1)

            layer_norm(FFN2)
            NC = 2 * E2
            dve.wait_ge(ln_done, NB * FFN2 + NB)
            v.memset(weight_parts, 0.0).then_inc(setup, 1)
            dve.wait_ge(sem("route_scored"), 2)
            st = Steps("q_step", 0, R2_STEPS, Q_STEPS + R1_STEPS)
            two_best(st, psum[:, 6, 0:NT * E2].rearrange("p (t e) -> p t e", t=NT), E2)
            v.tensor_tensor(peak1, top1[:, :, 1], top1[:, :, 0], ALU.subtract).then_inc(setup, 1)
            dve.wait_ge(sem("act_setup"), 3)
            st.did(v.tensor_scalar(sum1_inv, sum1, 1.0, None, ALU.add))
            st.then(lambda: v.reciprocal(pair_weight[:, 0, :], sum1_inv))
            st.then(lambda: v.tensor_tensor(pair_weight[:, 1, :], sum1, pair_weight[:, 0, :], ALU.mult))
            st.wait()
            for k, one_hot in enumerate((first1, second1)):
                st.did(v.tensor_tensor(one_hot[:, :, 0:E2], one_hot[:, :, 0:E2], each(pair_weight[:, k, :], E2), ALU.mult))
            st.then(lambda: v.tensor_tensor(weight2, first1[:, :, 0:E2], second1[:, :, 0:E2], ALU.add))
            dve.wait_ge(setup, SETUP.index("parts2") + 1)
            st.then(lambda: v.tensor_copy(weight_parts[:, :, 0:E2], weight2))
            st.then(lambda: v.tensor_tensor(weight_rem, weight2, weight_parts[:, :, 0:E2], ALU.subtract))
            st.then(lambda: v.tensor_copy(weight_parts[:, :, 32:32 + E2], weight_rem))
            st.wait()
            st.end()
            v.tensor_tensor(weight_parts[:, :, 64:64 + E2], weight_rem, weight_parts[:, :, 32:32 + E2],
                            ALU.subtract).then_inc(sem("route_weights"), 1)
            with dve.Fori(0, NB) as b:
                for i in range(NC):
                    e, k = divmod(i, 2)
                    s0, r = 2 * (i % 2), i % 2
                    dve.wait_ge(sem("gact2_ready"), b * NC + i + 1)
                    v.tensor_tensor(prod0[:, r, :], bank(s0 + 1), gact0[:, r, :], ALU.mult).then_inc(sem("prod2_ready"), 1)
                    dve.wait_ge(sem("weights_spread"), b * E2 + e + 1)
                    if i >= 2:
                        dve.wait_ge(sem("down2_done"), b * NC + i - 1)
                    dve.wait_ge(sem("prod2_ready"), b * NC + i + 1)
                    v.tensor_tensor(hid0[:, r, :], bank(4 + e % 2), prod0[:, r, :], ALU.mult).then_inc(sem("hid2_ready"), 1)
                dve.wait_ge(sem("down2_done"), b * NC + NC)
                add_to_x(b, 7)

            layer_norm(ATTN3)
            dve.wait_ge(sem("act_setup"), 6)
            v.scalar_tensor_tensor(a_par[:, 1:2], a_par[:, 0:1], 0.0, a_par[:, 1:2], ALU.max, ALU.add).then_inc(setup, 1)
            dve.wait_ge(setup, SETUP.index("apar") + 1)
            v.tensor_scalar(a_par[:, 2:3], a_par[:, 1:2], -8.0, None, ALU.mult).then_inc(setup, 1)
            v.tensor_scalar(a_par[:, 3:4], a_par[:, 1:2], -16.0, None, ALU.mult).then_inc(setup, 1)
            for b in range(NB):
                dve.wait_ge(sem("gx_ready"), b + 1)
                v.tensor_tensor(gx[:, b, :], gx[:, b, :], xw[:, b, :], ALU.mult).then_inc(sem("max_step"), 1)
            for b in range(NB):
                dve.wait_ge(sem("max_step"), MAX_STEPS + NB)
                dve.wait_ge(sem("drv_ready"), b + 1)
                v.tensor_tensor(gx[:, b, :], gx[:, b, :], drv[:, b, :], ALU.mult).then_inc(sem("max_step"), 1)
                dve.wait_ge(sem("max_step"), MAX_STEPS + NB + b + 1)
                v.tensor_tensor_scan(st3[:, b, :], dec[:, b, :], gx[:, b, :], 0.0, ALU.mult, ALU.add).then_inc(sem("state3_ready"), 1)
            for b in range(NB):
                dve.wait_ge(sem("batch_out"), b + outs_before(ATTN3) + 1)
                v.scalar_tensor_tensor(x[:, b, :], bank((0, 1, 6, 7)[b]), b_3[:, W_OUT:W_OUT + 1], x[:, b, :], ALU.add, ALU.add).then_inc(x_ready, 1)

            layer_norm(FFN3)
            dve.wait_ge(ln_done, NB * FFN3 + NB)
            v.memset(weight_parts, 0.0).then_inc(setup, 1)
            dve.wait_ge(sem("route_scored"), 3)
            st = Steps("q_step", 0, R3_STEPS, Q_STEPS + R1_STEPS + R2_STEPS)
            two_best(st, psum[:, 0, 0:NT * E3].rearrange("p (t e) -> p t e", t=NT), E3)
            st.end()
            dve.wait_ge(setup, SETUP.index("parts3") + 1)
            v.tensor_tensor(weight_parts[:, :, 0:E3], first1[:, :, 0:E3], second1[:, :, 0:E3], ALU.add).then_inc(sem("route_weights"), 1)

            def add_batch3(b):
                dve.wait_ge(sem("y3_added"), b * E3 + E3)
                add_to_x(b, 7)

            def pick_experts(b, begin):
                for e in range(E3):
                    dve.wait_ge(sem("weights_spread"), NB * E2 + b * E3 + e + 1)
                    if e >= RP or not begin:
                        dve.wait_ge(sem("y3_added"), b * E3 + e - RP + 1)
                    v.tensor_tensor(picked[:, e % RP, :], h[:, b, :], bank(3 + e % RP), ALU.mult).then_inc(sem("picked_ready"), 1)
                    if e == 1 and not begin:
                        add_batch3(b - 1)

            pick_experts(0, True)
            with dve.Fori(1, NB) as b:
                pick_experts(b, False)
            add_batch3(NB - 1)


N_CLEARED = 19
N_FFN1 = 3 + 2 + 2 + 2


def kernel(**inputs):
    import concourse.bacc as bacc
    from concourse.bass_utils import run_bass_kernel_spmd

    nc = bacc.Bacc("TRN2", target_bir_lowering=False, num_devices=1)
    arrays = {name: np.ascontiguousarray(value) for name, value in {**inputs, **shape_constants()}.items()}
    args = {name: nc.dram_tensor(name, value.shape, mybir.dt.from_np(value.dtype), kind="ExternalInput").ap()
            for name, value in arrays.items()}
    out = nc.dram_tensor("out", (NTOK, D), F32, kind="ExternalOutput").ap()
    build(nc, args, out)
    result = run_bass_kernel_spmd(nc, [arrays], core_ids=[0])
    return result.results[0]["out"].reshape(NB, S, D)
```
